# Optimizing a Trainium2 kernel written in Bass

```python
import numpy as np
import jax
import jax.numpy as jnp

def _softmax(x, axis=-1):
    return jax.nn.softmax(x, axis=axis)

def _gelu(x):
    return jax.nn.gelu(x, approximate=True)

def _silu(x):
    return jax.nn.silu(x)

def _sigmoid(x):
    return jax.nn.sigmoid(x)

def _layernorm(x, axis=-1, eps=1e-05):
    m = jnp.mean(x, axis=axis, keepdims=True)
    v = jnp.var(x, axis=axis, keepdims=True)
    return (x - m) / jnp.sqrt(v + eps)

def _scatter_add(tgt, idx, src, axis=0):
    return tgt.at[idx].add(src)

def _segment_sum(src, seg, n):
    return jax.ops.segment_sum(src, seg, n)
kernel_name = 'mk_cond_resid_d2_seqx_r4_aac9f7'

def setup_inputs(seed: int=0):
    np.random.seed(seed)
    _w = jnp.asarray

    def _rec_inputs():
        import jax
        import jax.numpy as jnp
        _rk = jax.random.key(seed)
        x = -0.0002928 + 1 * jax.random.normal(jax.random.fold_in(_rk, 1), (8, 512, 256), jnp.float32)
        _lenS = 512 - jax.random.randint(jax.random.fold_in(_rk, 7), (8,), 0, max(1, 512 // 4) + 1, jnp.int32)
        _lenS2 = 512 - jax.random.randint(jax.random.fold_in(_rk, 8), (8,), 0, max(1, 512 // 4) + 1, jnp.int32)
        cond_256 = -0.0209273 + 1.04763 * jax.random.normal(jax.random.fold_in(_rk, 11), (8, 64), jnp.float32)
        return (x, cond_256)
    x, cond_256 = _rec_inputs()

    def _L0_cond_setup():
        import jax, jax.numpy as jnp
        import numpy as np
        B, S, E, H, CD = (4, 256, 256, 16, 64)
        HD = E // H
        FIELD_COHERENCE = 0.7
        COH_THRESHOLD = 0.5
        FIELD_COUPLING = 0.3

        def _layernorm(x, g, b, eps=1e-05):
            mu = x.mean(-1, keepdims=True)
            var = ((x - mu) ** 2).mean(-1, keepdims=True)
            return (x - mu) * jax.lax.rsqrt(var + eps) * g + b
        key = jax.random.key(seed)
        ks = jax.random.split(key, 10)
        s = 0.02
        f32 = jnp.float32
        return {'x': jax.random.normal(ks[0], (B, S, E), f32), 'consciousness_state': jax.random.normal(ks[1], (B, CD), f32), 'Wqkv': jax.random.normal(ks[2], (3 * E, E), f32) * s, 'bqkv': jnp.zeros((3 * E,), f32), 'Wout': jax.random.normal(ks[3], (E, E), f32) * s, 'bout': jnp.zeros((E,), f32), 'Wc1': jax.random.normal(ks[4], (E, E + CD), f32) * s, 'bc1': jnp.zeros((E,), f32), 'Wc2': jax.random.normal(ks[5], (H, E), f32) * s, 'bc2': jnp.zeros((H,), f32), 'We1': jax.random.normal(ks[6], (E, CD), f32) * s, 'be1': jnp.zeros((E,), f32), 'We2': jax.random.normal(ks[7], (E, E), f32) * s, 'be2': jnp.zeros((E,), f32), 'ln_g': jnp.ones((E,), f32), 'ln_b': jnp.zeros((E,), f32)}
    _L0_cond_all = _L0_cond_setup()
    _L0_cond_in = {k: v for k, v in _L0_cond_all.items() if k in ('Wqkv', 'bqkv', 'Wout', 'bout', 'Wc1', 'bc1', 'Wc2', 'bc2', 'We1', 'be1', 'We2', 'be2', 'ln_g', 'ln_b')}
    del _L0_cond_all

    def _L1_cond_setup():
        import jax, jax.numpy as jnp
        import numpy as np
        TOP_K = 2
        EPS = 1e-06
        B, S, H, G, E, M = (2, 512, 256, 64, 8, 512)
        key = jax.random.key(seed)
        ks = jax.random.split(key, 16)
        s_h = 1.0 / np.sqrt(H)
        s_g = 1.0 / np.sqrt(G)
        s_m = 1.0 / np.sqrt(M)
        return {'x': jax.random.normal(ks[0], (B, S, H), jnp.float32), 'genre_embed': jax.random.normal(ks[1], (B, 1, G), jnp.float32), 'rms_w': jnp.ones((H,), jnp.float32), 'wg_W': jax.random.normal(ks[2], (H, E), jnp.float32) * s_h, 'wg_b': jnp.zeros((E,), jnp.float32), 'gg_W': jax.random.normal(ks[3], (G, E), jnp.float32) * s_g, 'gg_b': jnp.zeros((E,), jnp.float32), 'W1': jax.random.normal(ks[4], (E, H, M), jnp.float32) * s_h, 'b1': jnp.zeros((E, M), jnp.float32), 'W2': jax.random.normal(ks[5], (E, M, M), jnp.float32) * s_m, 'b2': jnp.zeros((E, M), jnp.float32), 'W3': jax.random.normal(ks[6], (E, M, H), jnp.float32) * s_m, 'b3': jnp.zeros((E, H), jnp.float32)}
    _L1_cond_all = _L1_cond_setup()
    _L1_cond_in = {k: v for k, v in _L1_cond_all.items() if k in ('rms_w', 'wg_W', 'wg_b', 'gg_W', 'gg_b', 'W1', 'b1', 'W2', 'b2', 'W3', 'b3')}
    del _L1_cond_all
    return {'x': x, 'cond_256': cond_256, 'L0_cond_Wqkv': _L0_cond_in['Wqkv'], 'L0_cond_bqkv': _L0_cond_in['bqkv'], 'L0_cond_Wout': _L0_cond_in['Wout'], 'L0_cond_bout': _L0_cond_in['bout'], 'L0_cond_Wc1': _L0_cond_in['Wc1'], 'L0_cond_bc1': _L0_cond_in['bc1'], 'L0_cond_Wc2': _L0_cond_in['Wc2'], 'L0_cond_bc2': _L0_cond_in['bc2'], 'L0_cond_We1': _L0_cond_in['We1'], 'L0_cond_be1': _L0_cond_in['be1'], 'L0_cond_We2': _L0_cond_in['We2'], 'L0_cond_be2': _L0_cond_in['be2'], 'L0_cond_ln_g': _L0_cond_in['ln_g'], 'L0_cond_ln_b': _L0_cond_in['ln_b'], 'L1_cond_rms_w': _L1_cond_in['rms_w'], 'L1_cond_wg_W': _L1_cond_in['wg_W'], 'L1_cond_wg_b': _L1_cond_in['wg_b'], 'L1_cond_gg_W': _L1_cond_in['gg_W'], 'L1_cond_gg_b': _L1_cond_in['gg_b'], 'L1_cond_W1': _L1_cond_in['W1'], 'L1_cond_b1': _L1_cond_in['b1'], 'L1_cond_W2': _L1_cond_in['W2'], 'L1_cond_b2': _L1_cond_in['b2'], 'L1_cond_W3': _L1_cond_in['W3'], 'L1_cond_b3': _L1_cond_in['b3']}

def reference(x, cond_256, L0_cond_Wqkv, L0_cond_bqkv, L0_cond_Wout, L0_cond_bout, L0_cond_Wc1, L0_cond_bc1, L0_cond_Wc2, L0_cond_bc2, L0_cond_We1, L0_cond_be1, L0_cond_We2, L0_cond_be2, L0_cond_ln_g, L0_cond_ln_b, L1_cond_rms_w, L1_cond_wg_W, L1_cond_wg_b, L1_cond_gg_W, L1_cond_gg_b, L1_cond_W1, L1_cond_b1, L1_cond_W2, L1_cond_b2, L1_cond_W3, L1_cond_b3):
    import jax
    import jax.numpy as jnp

    def _L0_cond_ref(x, consciousness_state, Wqkv, bqkv, Wout, bout, Wc1, bc1, Wc2, bc2, We1, be1, We2, be2, ln_g, ln_b):
        import jax, jax.numpy as jnp
        import numpy as np
        B, S, E, H, CD = (4, 256, 256, 16, 64)
        HD = E // H
        FIELD_COHERENCE = 0.7
        COH_THRESHOLD = 0.5
        FIELD_COUPLING = 0.3

        def _layernorm(x, g, b, eps=1e-05):
            mu = x.mean(-1, keepdims=True)
            var = ((x - mu) ** 2).mean(-1, keepdims=True)
            return (x - mu) * jax.lax.rsqrt(var + eps) * g + b
        Bb, Ss, Ee = x.shape
        qkv = (x @ Wqkv.T + bqkv).reshape(Bb, Ss, 3, H, HD).transpose(2, 0, 3, 1, 4)
        q, k, v = (qkv[0], qkv[1], qkv[2])
        attn = jax.nn.softmax(jnp.einsum('bhid,bhjd->bhij', q, k) / jnp.sqrt(jnp.float32(HD)), axis=-1)
        cs_exp = jnp.broadcast_to(consciousness_state[:, None, :], (Bb, Ss, CD))
        comb = jnp.concatenate([x, cs_exp], axis=-1)
        coh = jax.nn.sigmoid(jnp.tanh(comb @ Wc1.T + bc1) @ Wc2.T + bc2).transpose(0, 2, 1)
        mod = attn * coh[..., None]
        mod = mod / (mod.sum(-1, keepdims=True) + 1e-08)
        fp = _layernorm(jax.nn.relu(consciousness_state @ We1.T + be1) @ We2.T + be2, ln_g, ln_b)
        pos = jnp.arange(Ss, dtype=jnp.float32)
        inv = 10000.0 ** jnp.repeat(jnp.arange(0, Ee, 2, dtype=jnp.float32) / Ee, 2)
        pe = jnp.sin(pos[:, None] / inv[None, :])
        fa = jax.nn.softmax(jnp.einsum('be,se->bs', fp, pe), axis=-1)
        fi = FIELD_COUPLING * FIELD_COHERENCE
        mod = (1.0 - fi) * mod + fi * fa[:, None, :, None]
        out = jnp.einsum('bhij,bhjd->bhid', mod, v).transpose(0, 2, 1, 3).reshape(Bb, Ss, Ee)
        return out @ Wout.T + bout

    def _L1_cond_ref(x, genre_embed, rms_w, wg_W, wg_b, gg_W, gg_b, W1, b1, W2, b2, W3, b3):
        import jax, jax.numpy as jnp
        import numpy as np
        TOP_K = 2
        EPS = 1e-06
        E = W1.shape[0]
        var = jnp.mean(x * x, axis=-1, keepdims=True)
        xn = rms_w * (x * jax.lax.rsqrt(var + EPS))
        gate = xn @ wg_W + wg_b + (genre_embed @ gg_W + gg_b)
        gate_w = jax.nn.softmax(gate, axis=-1)
        topk_w, topk_i = jax.lax.top_k(gate_w, TOP_K)
        cw = jnp.sum(jax.nn.one_hot(topk_i, E, dtype=x.dtype) * topk_w[..., None], axis=-2)
        h1 = jax.nn.relu(jnp.einsum('bsh,ehm->bsem', x, W1) + b1)
        h2 = jax.nn.relu(jnp.einsum('bsem,emn->bsen', h1, W2) + b2)
        out_e = jnp.einsum('bsen,enh->bseh', h2, W3) + b3
        return jnp.einsum('bseh,bse->bsh', out_e, cw)
    x = x + _L0_cond_ref(x, cond_256, L0_cond_Wqkv, L0_cond_bqkv, L0_cond_Wout, L0_cond_bout, L0_cond_Wc1, L0_cond_bc1, L0_cond_Wc2, L0_cond_bc2, L0_cond_We1, L0_cond_be1, L0_cond_We2, L0_cond_be2, L0_cond_ln_g, L0_cond_ln_b)
    x = x + _L1_cond_ref(x, cond_256[:, None, :], L1_cond_rms_w, L1_cond_wg_W, L1_cond_wg_b, L1_cond_gg_W, L1_cond_gg_b, L1_cond_W1, L1_cond_b1, L1_cond_W2, L1_cond_b2, L1_cond_W3, L1_cond_b3)
    return x

_drawn_inputs = setup_inputs


def setup_inputs(seed=0):
    import zlib

    import numpy as np

    out = dict(_drawn_inputs(seed))
    spreads = {'L0_cond_bqkv': (0.0, 0.1),
     'L0_cond_bout': (0.0, 0.1),
     'L0_cond_bc1': (0.0, 2.0),
     'L0_cond_bc2': (0.0, 2.0),
     'L0_cond_be1': (0.0, 0.1),
     'L0_cond_be2': (0.0, 0.1),
     'L0_cond_ln_g': (1.0, 0.2),
     'L0_cond_ln_b': (0.0, 0.1),
     'L1_cond_rms_w': (1.0, 0.2),
     'L1_cond_wg_b': (0.0, 0.1),
     'L1_cond_gg_b': (0.0, 0.1),
     'L1_cond_b1': (0.0, 0.329),
     'L1_cond_b2': (0.0, 0.1),
     'L1_cond_b3': (0.0, 0.1)}
    factors = {'L0_cond_Wqkv': 3.882, 'L0_cond_Wc1': 64.0, 'L0_cond_Wc2': 64.0}
    for name, (base, spread) in spreads.items():
        noise = np.random.default_rng([zlib.crc32(name.encode()), seed]).standard_normal(out[name].shape)
        drawn = base * np.exp(spread * noise) if base else spread * noise
        out[name] = jnp.asarray(drawn.astype(out[name].dtype))
    for name, factor in factors.items():
        out[name] = (out[name] * factor).astype(out[name].dtype)
    return out
```

```python
from contextlib import ExitStack

import numpy as np

import concourse.bass as bass
from concourse import mybir

P = 128
B, S, E = 8, 512, 256
H, HD = 16, 16
CD = 64
NX, M = 8, 512
T = B * S
ET = E // P
TT = S // P
G = 4
NG = H // G
HW = 32
SHIFT = HD
COUPLING = 0.3 * 0.7
KEEP = 1.0 - COUPLING
SCALE = 1.0 / float(HD) ** 0.5
RING = 3

TS = 256
TILES_MAX = 2 * T // TS + NX
WSCALE = 16.0

F32 = mybir.dt.float32
F16 = mybir.dt.float16
I32 = mybir.dt.int32
F32R = mybir.dt.float32r
ALU = mybir.AluOpType
ACT = mybir.ActivationFunctionType
X = mybir.AxisListType.X

INPUTS = {
    "xT": [P, ET, T], "x": [P, T // P, E],
    "wq": [P, ET, NG * P], "wk": [P, ET, NG * P], "bq": [P, NG], "bk": [P, NG],
    "wv": [P, ET, E], "bv": [P, E], "wo": [P, ET, E], "bo": [P, E],
    "wc1x": [P, ET, E], "wc1c": [CD, E], "bc1": [P, ET], "wc2": [P, ET, H], "bc2": [P, H],
    "cT": [CD, B], "we1": [CD, E], "be1": [P, ET], "we2": [P, ET, E], "be2": [B, E],
    "ln_g": [B, E], "ln_b": [B, E], "pe": [P, ET, S], "ident": [P, P],
    "rms_w": [P, ET], "wg": [P, ET, NX], "gate_b": [P, 2, NX], "gg": [CD, NX],
    "w1": [P, NX, ET, M], "b1": [P, NX, M // P], "w2": [P, NX, M // P, M], "b2": [P, NX, M // P],
    "w3": [P, NX, M // P, E], "b3": [P, NX, E], "tri": [P, P], "count": [P, TILES_MAX + 2],
}


KEPT_ON_CHIP = ("rms_w", "gate_b", "b1", "b2", "b3", "ident", "tri", "count")


def program(nc, dram, out, dbg=None):
    with ExitStack() as ctx:
        def sb(name, shape, dt=F32):
            return ctx.enter_context(nc.sbuf_tensor(name, shape, dt))

        banks = [ctx.enter_context(nc.psum_tensor(f"bank{i}", [P, 512], F32)) for i in range(8)]
        w = {n: sb("w_" + n, INPUTS[n]) for n in KEPT_ON_CHIP}
        x1 = sb("x1", [P, T // P, E])
        gbias = sb("gbias", [P, B, NX])
        wgr = sb("wgr", [P, ET, NX])
        xs = nc.dram_tensor("xs", [(TILES_MAX + 2) * TS, E], F32).ap()
        ys = nc.dram_tensor("ys", [TILES_MAX * TS, E], F32).ap()

        with ExitStack() as own:
            for n, shape in INPUTS.items():
                if n not in KEPT_ON_CHIP + ("xT", "x", "w1", "w2", "w3"):
                    w[n] = own.enter_context(nc.sbuf_tensor("w_" + n, shape, F32))
            fa = own.enter_context(nc.sbuf_tensor("fa", [P, TT, B], F32))
            cbias = own.enter_context(nc.sbuf_tensor("cbias", [P, ET, B], F32))
            setup(nc, dram, banks, w, x1, fa, cbias, gbias, wgr)
            attention(nc, banks, dram, w, x1, fa, cbias, xs)
        split = {n: (sb(n + "_hi", INPUTS[n], F16), sb(n + "_lo", INPUTS[n], F16)) for n in ("w1", "w2", "w3")}
        top = sb("top", [P, 2, T // P])
        slots = sb("slots", [P, 2, T // P], I32)
        expert = sb("expert", [P, TILES_MAX + 2], I32)
        route(nc, banks, dram, w, x1, gbias, wgr, split, top, slots, expert, xs)
        experts(nc, banks, w, split, expert, xs, ys)
        combine(nc, x1, top, slots, ys, out)


def setup(nc, dram, banks, w, x1, fa, cbias, gbias, wgr):
    with ExitStack() as own:
        def sb(name, shape, dt=F32):
            return own.enter_context(nc.sbuf_tensor(name, shape, dt))

        loaded = own.enter_context(nc.semaphore("loaded"))
        x_loaded = own.enter_context(nc.semaphore("x_loaded"))
        pe_done = own.enter_context(nc.semaphore("setup_pe"))
        dve_done = own.enter_context(nc.semaphore("setup_dve"))
        act_done = own.enter_context(nc.semaphore("setup_act"))
        crep = sb("crep", [CD, B, P])
        e1 = sb("e1", [P, ET, B])
        fp = sb("fp", [B, E])
        sq = sb("sq", [B, E])
        fpT = sb("fpT", [P, ET, B])
        lg = sb("lg", [B, S])
        st = sb("st", [B, 8])
        block = own.enter_context(nc.Block())

        @block.sync
        def _(sp):
            sp.dma_start(x1[:, :, :], dram["x"]).then_inc(x_loaded, 16)
            for n, t in w.items():
                sp.dma_start(t[tuple(slice(None) for _ in t.shape)], dram[n]).then_inc(loaded, 16)

        @block.gpsimd
        def _(pool):
            pool.wait_ge(loaded, 16 * len(w))
            pool.wait_ge(x_loaded, 16)
            nc.gpsimd.tensor_tensor(x1[:, :, :], x1[:, :, :],
                                    w["bo"][:, None, :].to_broadcast([P, T // P, E]), ALU.add)

        @block.tensor
        def _(pe):
            pe.wait_ge(loaded, 16 * len(w))
            for m in range(ET):
                nc.tensor.matmul(banks[0][:, m * B:(m + 1) * B], w["we1"][:, m * P:(m + 1) * P], w["cT"][:, :],
                                 start=(m == 0), stop=True, skip_group_check=True)
                nc.tensor.matmul(banks[2][:, m * B:(m + 1) * B], w["wc1c"][:, m * P:(m + 1) * P], w["cT"][:, :],
                                 start=(m == 0), stop=True, skip_group_check=True).then_inc(pe_done, 1)
            pe.wait_ge(dve_done, 1)
            for b in range(B):
                last = nc.tensor.matmul(banks[3][:, b * NX:(b + 1) * NX], crep[:, b, :], w["gg"][:, :],
                                        start=(b == 0), stop=True, skip_group_check=True)
            last.then_inc(pe_done, 1)
            pe.wait_ge(act_done, 2)
            for k in range(ET):
                last = nc.tensor.matmul(banks[4][0:B, 0:E], e1[:, k, :], w["we2"][:, k, :], start=(k == 0), stop=(k == ET - 1))
            last.then_inc(pe_done, 1)
            pe.wait_ge(dve_done, 18)
            for k in range(ET):
                last = nc.tensor.transpose(banks[5][:, k * B:(k + 1) * B], fp[:, k * P:(k + 1) * P], w["ident"][0:B, 0:B])
            last.then_inc(pe_done, 1)
            pe.wait_ge(dve_done, 19)
            for k in range(ET):
                last = nc.tensor.matmul(banks[6][0:B, :], fpT[:, k, :], w["pe"][:, k, :], start=(k == 0), stop=(k == ET - 1))
            last.then_inc(pe_done, 1)
            pe.wait_ge(dve_done, 22)
            for t in range(TT):
                last = nc.tensor.transpose(banks[7][:, t * B:(t + 1) * B], lg[:, t * P:(t + 1) * P], w["ident"][0:B, 0:B])
            last.then_inc(pe_done, 1)

        @block.scalar
        def _(act):
            act.wait_ge(loaded, 16 * len(w))
            act.wait_ge(pe_done, 2)
            for m in range(ET):
                nc.scalar.activation(e1[:, m, :], banks[0][:, m * B:(m + 1) * B], ACT.Relu,
                                     bias=w["be1"][:, m:m + 1]).then_inc(act_done, 1)
            for m in range(ET):
                nc.scalar.activation(cbias[:, m, :], banks[2][:, m * B:(m + 1) * B], ACT.Identity,
                                     bias=w["bc1"][:, m:m + 1])
            act.wait_ge(dve_done, 11)
            nc.scalar.activation(st[:, 7:8], st[:, 3:4], ACT.Sqrt).then_inc(act_done, 1)
            act.wait_ge(dve_done, 20)
            nc.scalar.activation(lg[:, :], banks[6][0:B, :], ACT.Exp, bias=st[:, 5:6],
                                 accum_out=st[:, 6:7]).then_inc(act_done, 1)

        @block.vector
        def _(dve):
            n = [0]

            def chain(ins):
                n[0] += 1
                ins.then_inc(dve_done, 1)
                dve.wait_ge(dve_done, n[0])

            dve.wait_ge(loaded, 16 * len(w))
            chain(nc.vector.tensor_copy(crep[:, :, :], w["cT"][:, :, None].to_broadcast([CD, B, P])))
            for k in range(ET):
                last = nc.vector.tensor_scalar(wgr[:, k, :], w["wg"][:, k, :], w["rms_w"][:, k:k + 1], None, ALU.mult)
            chain(last)
            dve.wait_ge(pe_done, 3)
            gb = gbias[:, :, :]
            chain(nc.vector.tensor_tensor(gb, banks[3][:, 0:B * NX].rearrange("p (b e) -> p b e", b=B),
                                          w["gate_b"][:, 0:1, :].to_broadcast([P, B, NX]), ALU.add))
            chain(nc.vector.tensor_tensor(gb, gb, w["gate_b"][:, 1:2, :].to_broadcast([P, B, NX]), ALU.add))
            dve.wait_ge(pe_done, 4)
            chain(nc.vector.tensor_tensor(fp[:, :], banks[4][0:B, 0:E], w["be2"][:, :], ALU.add))
            chain(nc.vector.reduce_sum(st[:, 0:1], fp[:, :], axis=X))
            chain(nc.vector.tensor_scalar(st[:, 1:2], st[:, 0:1], 1.0 / E, None, ALU.mult))
            chain(nc.vector.tensor_scalar(fp[:, :], fp[:, :], st[:, 1:2], None, ALU.subtract))
            chain(nc.vector.tensor_tensor(sq[:, :], fp[:, :], fp[:, :], ALU.mult))
            chain(nc.vector.reduce_sum(st[:, 2:3], sq[:, :], axis=X))
            chain(nc.vector.tensor_scalar(st[:, 3:4], st[:, 2:3], 1.0 / E, 1e-5, ALU.mult, ALU.add))
            dve.wait_ge(act_done, 3)
            chain(nc.vector.reciprocal(st[:, 4:5], st[:, 7:8]))
            chain(nc.vector.tensor_tensor(st[:, 6:7], st[:, 4:5], st[:, 4:5], ALU.mult))
            chain(nc.vector.tensor_tensor(st[:, 6:7], st[:, 6:7], st[:, 3:4], ALU.mult))
            chain(nc.vector.tensor_scalar(st[:, 6:7], st[:, 6:7], -0.5, 1.5, ALU.mult, ALU.add))
            chain(nc.vector.tensor_tensor(st[:, 4:5], st[:, 4:5], st[:, 6:7], ALU.mult))
            chain(nc.vector.scalar_tensor_tensor(fp[:, :], fp[:, :], st[:, 4:5], w["ln_g"][:, :],
                                                 ALU.mult, ALU.mult))
            chain(nc.vector.tensor_tensor(fp[:, :], fp[:, :], w["ln_b"][:, :], ALU.add))
            dve.wait_ge(pe_done, 5)
            chain(nc.vector.tensor_copy(fpT[:, :, :], banks[5][:, 0:ET * B].rearrange("p (k b) -> p k b", k=ET)))
            dve.wait_ge(pe_done, 6)
            chain(nc.vector.tensor_reduce(st[:, 5:6], banks[6][0:B, :], X, ALU.max, negate=True))
            dve.wait_ge(act_done, 4)
            chain(nc.vector.reciprocal(st[:, 7:8], st[:, 6:7]))
            chain(nc.vector.tensor_scalar(lg[:, :], lg[:, :], st[:, 7:8], COUPLING, ALU.mult, ALU.mult))
            dve.wait_ge(pe_done, 7)
            chain(nc.vector.tensor_copy(fa[:, :, :], banks[7][:, 0:TT * B].rearrange("p (t b) -> p t b", t=TT)))


PLAN = {
    (0, 0): [("q", 3), ("k", 3)],
    (0, 1): [("v", 3), ("c1", 0)],
    (0, 2): [("ot", 3), ("c1", 1)],
    (0, 3): [("mt", 1), ("coh", 0)],
    (1, 0): [("at", 0), ("vs", 0)],
    (1, 1): [("q", 0), ("k", 0)],
    (1, 2): [("ot", 0), ("v", 0)],
    (1, 3): [("mt", 2), ("at", 1)],
    (2, 0): [("q", 1), ("k", 1)],
    (2, 1): [("v", 1), ("op", 0)],
    (2, 2): [("ot", 1), ("op", 1)],
    (2, 3): [("mt", 3)],
    (3, 0): [("q", 2), ("k", 2)],
    (3, 1): [("v", 2)],
    (3, 2): [("ot", 2)],
    (3, 3): [("mt", 0)],
}
LAST_WORK = [("ot", 3), ("at", 0), ("at", 1), ("op", 0), ("op", 1)]
NEXT_WORK = [(c, g) for g in range(NG - 1) for c in "qkv"] + [("mt", 0)]
FIRST, TAIL = NEXT_WORK, LAST_WORK
ON_ACT = ("q", "k", "c1")
ORDER = [task for step in range(NG) for slot in range(TT) for task in PLAN[step, slot]]
LEAD = 6
TILES = NG * TT * G
SLOTS = NG * TT
LINKS = 2 * NG + 3


def kept(kind):
    left_out = {"first": LAST_WORK, "mid": [], "last": NEXT_WORK}[kind]
    return [task for task in ORDER if task not in left_out]


def misc_base(kind, b):
    return len(FIRST) if kind == "first" else len(FIRST) + len(kept("first")) + (b - 1) * len(ORDER)


def misc_use(kind, b, task):
    return misc_base(kind, b) + kept(kind).index(task)


TAIL_BASE = misc_base("last", B - 1) + len(kept("last"))


def lead_block(kind, b, g, jt):
    at = g * TT + jt + LEAD
    if at < SLOTS:
        return b, at
    return None if kind == "last" else (b + 1, at - SLOTS)


def after(engine, semaphore, count):
    if not (isinstance(count, int) and count == 0):
        engine.wait_ge(semaphore, count)


def batches(engine, body):
    body("first", 0)
    with engine.Fori(1, B - 1) as b:
        body("mid", b)
    body("last", B - 1)


def attention(nc, banks, dram, w, x1, fa, cbias, xs):
    with ExitStack() as own:
        def sb(name, shape, dt=F32):
            return own.enter_context(nc.sbuf_tensor(name, shape, dt))

        def sem(name):
            return own.enter_context(nc.semaphore(name))

        xT = sb("xT", [P, ET, S])
        q = sb("q", [P, NG, S])
        qs = sb("qs", [P, 2, S])
        k = sb("k", [P, NG, S])
        v = sb("v", [P, TT, NG, G, HW])
        mx = sb("mx", [P, 2, TT, G, HW])
        pr = sb("pr", [P, TT, G, S])
        oT = sb("oT", [P, S])
        hT = sb("hT", [P, ET, S])
        z = sb("z", [P, TT, H])
        ez = sb("ez", [P, TT, H])
        coh = sb("coh", [P, TT, H])
        div = sb("div", [P, TT, G])
        rdiv = sb("rdiv", [P, TT, G])
        att = sb("att", [P, TT, E])
        attT = sb("attT", [P, ET, S])
        vsum = sb("vsum", [P, E])
        facur = sb("facur", [P, TT])
        ones = sb("ones", [P, P])
        zeros = sb("zeros", [P, 4 * E])

        cleared = sem("cleared")
        xs_cleared = sem("xs_cleared")
        x_in = sem("x_in")
        a_ready, a_read = sem("a_ready"), sem("a_read")
        b_ready, b_read = sem("b_ready"), sem("b_read")
        slots_free = sem("slots_free")
        out_copied = sem("out_copied")
        misc_ready, misc_read = sem("misc_ready"), sem("misc_read")
        z_ready, ez_ready = sem("z_ready"), sem("ez_ready")
        link = sem("link")
        a_bank, b_bank, pv_bank, misc = banks[0:RING], banks[RING:2 * RING], banks[6], banks[7]
        block = own.enter_context(nc.Block())

        @block.sync
        def _(sp):
            sp.dma_start(xT[:, :, :], dram["xT"][:, :, 0:S]).then_inc(x_in, 16)

            def load_next(kind, b):
                sp.wait_ge(misc_ready, misc_use(kind, b, ("c1", 1)) + 1)
                sp.dma_start(xT[:, :, :], dram["xT"][:, :, bass.ds((b + 1) * S, S)]).then_inc(x_in, 16)

            sp.wait_ge(cleared, 5)
            for t in range((TILES_MAX + 2) * TS // (4 * P)):
                sp.dma_start(xs[t * 4 * P:(t + 1) * 4 * P, :].rearrange("(p r) e -> p (r e)", r=4),
                             zeros[:, :]).then_inc(xs_cleared, 16)
            load_next("first", 0)
            with sp.Fori(1, B - 1) as b:
                load_next("mid", b)
            sp.wait_ge(xs_cleared, 16 * ((TILES_MAX + 2) * TS // (4 * P)))

        @block.gpsimd
        def _(pool):
            nc.gpsimd.memset(ones[:, :], 1.0).then_inc(cleared, 1)
            nc.gpsimd.memset(mx[:, :, :, :, :], 0.0).then_inc(cleared, 1)
            nc.gpsimd.memset(v[:, :, :, :, SHIFT + 1:HW], 0.0).then_inc(cleared, 1)
            nc.gpsimd.memset(v[:, :, :, :, SHIFT:SHIFT + 1], 1.0).then_inc(cleared, 1)
            nc.gpsimd.memset(z[:, :, :], 0.0).then_inc(slots_free, TT)
            nc.gpsimd.memset(zeros[:, :], 0.0).then_inc(cleared, 1)

        @block.tensor
        def _(pe):
            def bank_free(read, b, n):
                if n >= RING:
                    pe.wait_ge(read, b * TILES + n - RING + 1)
                elif not (isinstance(b, int) and b == 0):
                    pe.wait_ge(read, b * TILES)

            def a_block(b, at):
                g, it = at // TT, at % TT
                for h in range(G):
                    n = at * G + h
                    bank_free(a_read, b, n)
                    r = slice(HW * h, HW * h + HW)
                    nc.tensor.matmul(a_bank[n % RING][:, :], q[r, g, it * P:(it + 1) * P], k[r, g, :],
                                     start=True, stop=True, tile_position=(HW * h, 0)).then_inc(a_ready, 1)

            def b_block(b, g, jt):
                for h in range(G):
                    n = (g * TT + jt) * G + h
                    bank_free(b_read, b, n)
                    r = slice(HW * h, HW * h + HW)
                    nc.tensor.matmul(b_bank[n % RING][:, :], k[r, g, jt * P:(jt + 1) * P], qs[r, g % 2, :],
                                     start=True, stop=True, tile_position=(HW * h, 0)).then_inc(b_ready, 1)

            def pv(b, g, jt):
                pe.wait_ge(b_read, b * TILES + (g * TT + jt + 1) * G)
                if jt == 0 and not (isinstance(b, int) and b == 0 and g == 0):
                    pe.wait_ge(out_copied, b * NG + g)
                for h in range(G):
                    last = nc.tensor.matmul(pv_bank[HW * h:HW * h + HW, :], v[:, jt, g, h, :], pr[:, jt, h, :],
                                            start=(jt == 0), stop=(jt == TT - 1), tile_position=(0, HW * h))
                last.then_inc(slots_free, 1)

            def product(task, no):
                what, i = task
                if not (isinstance(no, int) and no == 0):
                    pe.wait_ge(misc_read, no)
                if what in ("q", "k", "c1"):
                    wt = w[{"q": "wq", "k": "wk", "c1": "wc1x"}[what]]
                    for e in range(ET):
                        last = nc.tensor.matmul(misc[:, :], wt[:, e, i * P:(i + 1) * P], xT[:, e, :],
                                                start=(e == 0), stop=(e == ET - 1))
                elif what == "v":
                    n = G * HD
                    for t in range(TT):
                        for e in range(ET):
                            last = nc.tensor.matmul(misc[:, t * n:(t + 1) * n], xT[:, e, t * P:(t + 1) * P],
                                                    w["wv"][:, e, i * n:(i + 1) * n], start=(t == 0 and e == 0),
                                                    stop=(e == ET - 1), skip_group_check=True)
                elif what == "coh":
                    for t in range(TT):
                        for e in range(ET):
                            last = nc.tensor.matmul(misc[:, t * H:(t + 1) * H], hT[:, e, t * P:(t + 1) * P],
                                                    w["wc2"][:, e, :], start=(t == 0 and e == 0),
                                                    stop=(e == ET - 1), skip_group_check=True)
                elif what == "vs":
                    for t in range(TT):
                        last = nc.tensor.matmul(misc[:, 0:E].rearrange("p (g h d) -> p g h d", g=NG, h=G), ones[:, :],
                                                v[:, t, :, :, 0:HD], start=(t == 0), stop=(t == TT - 1))
                elif what == "ot":
                    for t in range(TT):
                        last = nc.tensor.transpose(misc[:, t * P:(t + 1) * P], oT[:, t * P:(t + 1) * P],
                                                   w["ident"][:, :])
                elif what == "mt":
                    for t in range(TT):
                        last = nc.tensor.transpose(misc[:, t * P:(t + 1) * P],
                                                   mx[:, i % 2, t, :, :].rearrange("p h r -> p (h r)"),
                                                   w["ident"][:, :])
                elif what == "at":
                    for t in range(TT):
                        last = nc.tensor.transpose(misc[:, t * P:(t + 1) * P], att[:, t, i * P:(i + 1) * P],
                                                   w["ident"][:, :])
                elif what == "op":
                    for t in range(2):
                        for e in range(ET):
                            r = slice((2 * i + t) * P, (2 * i + t + 1) * P)
                            last = nc.tensor.matmul(misc[:, t * E:(t + 1) * E], attT[:, e, r], w["wo"][:, e, :],
                                                    start=(t == 0 and e == 0), stop=(e == ET - 1),
                                                    skip_group_check=True)
                last.then_inc(misc_ready, 1)

            def inputs_ready(task, b):
                what, i = task
                if task == ("q", 0):
                    pe.wait_ge(x_in, 16 * (b + 2))
                if what == "mt":
                    step = i * TT * G if i > 0 else TILES
                    pe.wait_ge(a_read, b * TILES + step + TT * G)
                if what == "ot":
                    pe.wait_ge(out_copied, b * NG + (i + 1 if i < NG - 1 else 0))

            pe.wait_ge(cleared, 4)
            pe.wait_ge(x_in, 16)
            for no, task in enumerate(FIRST):
                if task == ("mt", 0):
                    pe.wait_ge(misc_read, no)
                    for at in range(TT):
                        a_block(0, at)
                    pe.wait_ge(a_read, TT * G)
                product(task, no)
            for at in range(TT, LEAD):
                a_block(0, at)

            def body(kind, b):
                for g in range(NG):
                    for jt in range(TT):
                        if jt == 0:
                            pe.wait_ge(misc_read, misc_use(kind, b, ("mt", g)) + 1 if g else misc_base(kind, b))
                        b_block(b, g, jt)
                        lead = lead_block(kind, b, g, jt)
                        if lead is not None:
                            a_block(*lead)
                        tasks = [t if t in kept(kind) else None for t in PLAN[g, jt]] + [None] * 2
                        for i, task in enumerate(tasks[:2]):
                            if task is not None:
                                inputs_ready(task, b)
                                product(task, misc_use(kind, b, task))
                            if i == 0 and (g, jt) == (0, 0):
                                if kind != "first":
                                    pv(b - 1, NG - 1, TT - 1)
                            elif i == 0:
                                pv(b, g if jt else g - 1, (jt - 1) % TT)

            batches(pe, body)
            pv(B - 1, NG - 1, TT - 1)
            for n, task in enumerate(TAIL):
                inputs_ready(task, B)
                product(task, TAIL_BASE + n)

        @block.scalar
        def _(act):
            def read_misc(task, no, b):
                what, i = task
                act.wait_ge(misc_ready, no + 1)
                if what == "c1":
                    nc.scalar.activation(hT[:, i, :], misc[:, :], ACT.Tanh,
                                         bias=cbias[:, i, bass.ds(b, 1)]).then_inc(misc_read, 1)
                else:
                    nc.scalar.activation((q if what == "q" else k)[:, i, :], misc[:, :], ACT.Identity,
                                         bias=w["b" + what][:, i:i + 1]).then_inc(misc_read, 1)

            for no, task in enumerate(FIRST):
                if task[0] in ON_ACT:
                    read_misc(task, no, 0)

            def body(kind, b):
                for g in range(NG):
                    for jt in range(TT):
                        if (g, jt) == (1, 0):
                            act.wait_ge(z_ready, b + 1)
                            nc.scalar.activation(ez[:, :, :], z[:, :, :], ACT.Exp, scale=-1.0).then_inc(ez_ready, 1)
                        act.wait_ge(slots_free, b * SLOTS + g * TT + jt + 1)
                        for h in range(G):
                            n = (g * TT + jt) * G + h
                            act.wait_ge(b_ready, b * TILES + n + 1)
                            nc.scalar.activation(pr[:, jt, h, :], b_bank[n % RING][:, :], ACT.Exp,
                                                 scale=SCALE).then_inc(b_read, 1)
                        for task in PLAN[g, jt]:
                            if task in kept(kind) and task[0] in ON_ACT:
                                read_misc(task, misc_use(kind, b, task), b)

            batches(act, body)

        @block.vector
        def _(dve):
            def reduce_block(b, at):
                g, it = at // TT, at % TT
                for h in range(G):
                    n = at * G + h
                    dve.wait_ge(a_ready, b * TILES + n + 1)
                    nc.vector.tensor_reduce(mx[:, g % 2, it, h, SHIFT:SHIFT + 1], a_bank[n % RING][:, :], X,
                                            ALU.max).then_inc(a_read, 1)

            def copy_out(step):
                dve.wait_ge(slots_free, (step + 2) * TT)
                nc.vector.tensor_copy(oT[:, :], pv_bank[:, :]).then_inc(out_copied, 1)

            def read_misc(task, no, b, n):
                what, i = task
                dve.wait_ge(misc_ready, no + 1)
                if what == "v":
                    nc.vector.tensor_tensor(
                        v[:, :, i, :, 0:HD], misc[:, 0:TT * G * HD].rearrange("p (t h d) -> p t h d", t=TT, h=G),
                        w["bv"][:, i * G * HD:(i + 1) * G * HD].rearrange("p (h d) -> p h d", h=G)[:, None, :, :]
                        .to_broadcast([P, TT, G, HD]), ALU.add).then_inc(misc_read, 1)
                elif what == "mt":
                    nc.vector.tensor_tensor(qs[:, i % 2, :], q[:, i, :], misc[:, :],
                                            ALU.subtract).then_inc(misc_read, 1)
                elif what == "coh":
                    nc.vector.tensor_tensor(z[:, :, :], misc[:, 0:TT * H].rearrange("p (t h) -> p t h", t=TT),
                                            w["bc2"][:, None, :].to_broadcast([P, TT, H]), ALU.add).then_inc(link, 1)
                    dve.wait_ge(link, n + 1)
                    nc.vector.tensor_scalar(z[:, :, :], z[:, :, :], -88.0, None, ALU.max).then_inc(z_ready, 1)
                    nc.vector.tensor_copy(facur[:, :], fa[:, :, bass.ds(b, 1)].rearrange("p t b -> p (t b)"))\
                        .then_inc(misc_read, 1)
                    return n + 1
                elif what == "vs":
                    nc.vector.tensor_copy(vsum[:, :], misc[:, 0:E]).then_inc(misc_read, 1)
                elif what == "at":
                    nc.vector.tensor_copy(attT[:, i, :], misc[:, :]).then_inc(misc_read, 1)
                elif what == "op":
                    rows = x1[:, bass.ds((b - 1) * TT + 2 * i, 2), :].rearrange("p t e -> p (t e)")
                    nc.vector.tensor_tensor(rows, misc[:, :], rows, ALU.add).then_inc(misc_read, 1)
                elif what == "ot":
                    dve.wait_ge(misc_read, no)
                    dve.wait_ge(link, n)
                    o = misc[:, :].rearrange("p (t h r) -> p t h r", t=TT, h=G)
                    nc.vector.tensor_tensor(div[:, :, :], o[:, :, :, SHIFT], coh[:, :, i * G:(i + 1) * G],
                                            ALU.mult).then_inc(link, 1)
                    dve.wait_ge(link, n + 1)
                    nc.vector.reciprocal(rdiv[:, :, :], div[:, :, :]).then_inc(link, 1)
                    dve.wait_ge(link, n + 2)
                    dst = att[:, :, i * G * HD:(i + 1) * G * HD].rearrange("p t (h d) -> p t h d", h=G)
                    scaled = nc.vector.tensor_tensor(dst, o[:, :, :, 0:HD],
                                                     rdiv[:, :, :, None].to_broadcast([P, TT, G, HD]), ALU.mult)
                    if i < NG - 1:
                        scaled.then_inc(misc_read, 1)
                        return n + 2
                    scaled.then_inc(link, 1)
                    dve.wait_ge(link, n + 3)
                    for t in range(TT):
                        last = nc.vector.scalar_tensor_tensor(att[:, t, :], vsum[:, :], facur[:, t:t + 1],
                                                              att[:, t, :], ALU.mult, ALU.add)
                    last.then_inc(misc_read, 1)
                    return n + 3
                return n

            dve.wait_ge(cleared, 4)
            for no, task in enumerate(FIRST):
                if task == ("mt", 0):
                    for at in range(TT):
                        reduce_block(0, at)
                if task[0] not in ON_ACT:
                    read_misc(task, no, 0, 0)
            for at in range(TT, LEAD):
                reduce_block(0, at)

            def links_before(kind, b):
                return 0 if kind == "first" else LINKS - 3 + (b - 1) * LINKS

            def body(kind, b):
                n = links_before(kind, b)
                for g in range(NG):
                    for jt in range(TT):
                        lead = lead_block(kind, b, g, jt)
                        if lead is not None:
                            reduce_block(*lead)
                        if (g, jt) == (1, 0):
                            dve.wait_ge(ez_ready, b + 1)
                            nc.vector.tensor_scalar(coh[:, :, :], ez[:, :, :], 1e-8 / KEEP, (1.0 + 1e-8) / KEEP,
                                                    ALU.mult, ALU.add).then_inc(link, 1)
                            n = n + 1
                        tasks = [t if t in kept(kind) else None for t in PLAN[g, jt]] + [None] * 2
                        for i, task in enumerate(tasks[:2]):
                            if task is not None and task[0] not in ON_ACT:
                                n = read_misc(task, misc_use(kind, b, task), b, n)
                            if i == 0 and jt == 0 and not (kind == "first" and g == 0):
                                copy_out(b * NG + g - 1)

            batches(dve, body)
            copy_out(B * NG - 1)
            n = links_before("last", B)
            for i, task in enumerate(TAIL):
                n = read_misc(task, TAIL_BASE + i, B, n)


def route(nc, banks, dram, w, x1, gbias, wgr, split, top, slots, expert, xs):
    NT = T // P
    CHUNK = 2048
    chunks = []
    for e in range(0, NX, 2):
        chunks += [("w1", e * ET * M)] + [("w2", (e + i) * M // P * M) for i in range(2)] + [("w3", e * M // P * E)]
    with ExitStack() as own:
        def sb(name, shape, dt=F32):
            return own.enter_context(nc.sbuf_tensor(name, shape, dt))

        def sem(name):
            return own.enter_context(nc.semaphore(name))

        raw = sb("raw", [P, 2, CHUNK])
        x1T = sb("x1T", [P, 2, ET, P])
        junk = sb("junk", [P, E])
        ssq = sb("ssq", [P, NT])
        root = sb("root", [P, NT])
        rstd = sb("rstd", [P, NT])
        tmp = sb("tmp", [P, NT])
        gate = sb("gate", [P, NT, NX])
        g2 = sb("g2", [P, NT, NX])
        hot = [sb(f"hot{i}", [P, NT, NX]) for i in range(2)]
        both = sb("both", [P, NT, NX])
        key = sb("key", [P, NT, NX])
        scan = [sb(f"scan{i}", [P, NT, NX]) for i in range(2)]
        tiles = sb("tiles", [P, NX])
        ends = sb("ends", [P, NX])
        itiles = sb("itiles", [P, NX], I32)
        owner = sb("owner", [P, TILES_MAX + 2, NX])
        ones = sb("ones2", [P, P])
        raw_in = [sem(f"raw_in{i}") for i in range(2)]
        hi_done, lo_done = sem("hi_done"), sem("lo_done")
        turned, copied, gated = sem("turned"), sem("copied"), sem("gated")
        squares = sem("squares")
        act_done, pe_done, link = sem("route_act"), sem("route_pe"), sem("route_link")
        ones_set, sorted_, placed, scattered = sem("ones_set"), sem("sorted"), sem("placed"), sem("scattered")
        logits, below, sums = banks[2], banks[3], banks[4]
        block = own.enter_context(nc.Block())

        def column(t, at):
            return t[:, :, :, :].rearrange("p e k n -> p (e k n)")[:, at:at + CHUNK]

        @block.sync
        def _(sp):
            for n, (name, at) in enumerate(chunks):
                if n >= 2:
                    sp.wait_ge(lo_done, n - 1)
                sp.dma_start(raw[:, n % 2, :], column(dram[name], at)).then_inc(raw_in[n % 2], 16)

        @block.tensor
        def _(pe):
            def gates(t):
                pe.wait_ge(copied, t + 1)
                for e in range(ET):
                    last = nc.tensor.matmul(logits[:, t * NX:(t + 1) * NX], x1T[:, t % 2, e, :], wgr[:, e, :],
                                            start=(e == 0), stop=(e == ET - 1), skip_group_check=True)
                last.then_inc(gated, 1)

            for t in range(NT):
                if t >= 2:
                    pe.wait_ge(copied, t - 1)
                for e in range(ET):
                    last = nc.tensor.transpose(banks[t % 2][:, e * P:(e + 1) * P], x1[:, t, e * P:(e + 1) * P],
                                               w["ident"][:, :])
                last.then_inc(turned, 1)
                if t >= 1:
                    gates(t - 1)
            gates(NT - 1)
            pe.wait_ge(ones_set, 1)
            pe.wait_ge(sorted_, 1)
            marks = both[:, :, :].rearrange("p t e -> p (t e)")
            nc.tensor.matmul(below[:, 0:NT * NX], w["tri"][:, :], marks, start=True, stop=True)
            nc.tensor.matmul(sums[:, 0:NT * NX], ones[:, :], marks, start=True, stop=True).then_inc(pe_done, 1)

        @block.scalar
        def _(act):
            def square(t):
                after(act, squares, t)
                nc.scalar.activation(junk[:, :], x1[:, bass.ds(t, 1), :].rearrange("p a f -> p (a f)"),
                                     ACT.Square, accum_out=ssq[:, bass.ds(t, 1)]).then_inc(squares, 1)

            square(0)
            with act.Fori(1, NT) as t:
                square(t)
            act.wait_ge(link, 1)
            nc.scalar.activation(root[:, :], tmp[:, :], ACT.Sqrt).then_inc(act_done, 1)
            act.wait_ge(link, 10)
            nc.scalar.activation(gate[:, :, :], g2[:, :, :], ACT.Exp).then_inc(act_done, 1)
            for n, (name, at) in enumerate(chunks):
                act.wait_ge(raw_in[n % 2], 16 * (n // 2 + 1))
                nc.scalar.activation(column(split[name][0], at), raw[:, n % 2, :], ACT.Copy, scale=WSCALE).then_inc(hi_done, 1)

        @block.vector
        def _(dve):
            n = [0]

            def chain(ins):
                n[0] += 1
                ins.then_inc(link, 1)
                dve.wait_ge(link, n[0])

            def over_experts(a):
                return a[:, :, None].to_broadcast([P, NT, NX])

            def each_expert(a):
                return a[:, None, 0:NX].to_broadcast([P, NT, NX])

            V = nc.vector
            for t in range(NT):
                dve.wait_ge(turned, t + 1)
                if t >= 2:
                    dve.wait_ge(gated, t - 1)
                V.tensor_copy(x1T[:, t % 2, :, :].rearrange("p e n -> p (e n)"), banks[t % 2][:, 0:E]).then_inc(copied, 1)
            dve.wait_ge(squares, NT)
            chain(V.tensor_scalar(tmp[:, :], ssq[:, :], 1.0 / E, 1e-6, ALU.mult, ALU.add))
            dve.wait_ge(act_done, 1)
            chain(V.reciprocal(rstd[:, :], root[:, :]))
            chain(V.tensor_tensor(root[:, :], rstd[:, :], rstd[:, :], ALU.mult))
            chain(V.tensor_tensor(root[:, :], root[:, :], tmp[:, :], ALU.mult))
            chain(V.tensor_scalar(root[:, :], root[:, :], -0.5, 1.5, ALU.mult, ALU.add))
            chain(V.tensor_tensor(rstd[:, :], rstd[:, :], root[:, :], ALU.mult))
            dve.wait_ge(gated, NT)
            chain(V.tensor_tensor(gate[:, :, :], logits[:, 0:NT * NX].rearrange("p (t e) -> p t e", t=NT),
                                  over_experts(rstd), ALU.mult))
            g4 = gate[:, :, :].rearrange("p (b t) e -> p b t e", b=B)
            chain(V.tensor_tensor(g4, g4, gbias[:, :, None, :].to_broadcast([P, B, TT, NX]), ALU.add))
            chain(V.tensor_reduce(tmp[:, :], gate[:, :, :], X, ALU.max))
            chain(V.tensor_tensor(g2[:, :, :], gate[:, :, :], over_experts(tmp), ALU.subtract))
            dve.wait_ge(act_done, 2)
            chain(V.reduce_sum(tmp[:, :], gate[:, :, :], axis=X))
            chain(V.reciprocal(root[:, :], tmp[:, :]))
            chain(V.tensor_tensor(gate[:, :, :], gate[:, :, :], over_experts(root), ALU.mult))
            src = gate
            for i in range(2):
                chain(V.tensor_reduce(top[:, i, :], src[:, :, :], X, ALU.max))
                chain(V.tensor_tensor(key[:, :, :], src[:, :, :], over_experts(top[:, i, :]), ALU.is_lt))
                chain(V.scalar_tensor_tensor(key[:, :, :], key[:, :, :], float(NX), each_expert(w["count"]),
                                             ALU.mult, ALU.add))
                chain(V.tensor_reduce(tmp[:, :], key[:, :, :], X, ALU.min))
                chain(V.tensor_tensor(hot[i][:, :, :], each_expert(w["count"]), over_experts(tmp), ALU.is_equal))
                if i == 0:
                    chain(V.scalar_tensor_tensor(g2[:, :, :], hot[0][:, :, :], -2.0, gate[:, :, :], ALU.mult, ALU.add))
                    src = g2
            V.tensor_tensor(both[:, :, :], hot[0][:, :, :], hot[1][:, :, :], ALU.add).then_inc(sorted_, 1)
            dve.wait_ge(pe_done, 1)
            per_tile = sums[:, 0:NT * NX].rearrange("p (t e) -> p t e", t=NT)
            chain(V.tensor_copy(scan[0][:, :, :], per_tile))
            cur, step = 0, 1
            while step < NT:
                a, b = scan[cur], scan[1 - cur]
                V.tensor_copy(b[:, 0:step, :], a[:, 0:step, :])
                chain(V.tensor_tensor(b[:, step:, :], a[:, step:, :], a[:, 0:NT - step, :], ALU.add))
                cur, step = 1 - cur, 2 * step
            upto = scan[cur]
            chain(V.tensor_scalar(itiles[:, :], upto[:, NT - 1, :], float(TS - 1), None, ALU.add))
            chain(V.tensor_scalar(itiles[:, :], itiles[:, :], TS.bit_length() - 1, None, ALU.arith_shift_right))
            chain(V.tensor_copy(tiles[:, :], itiles[:, :]))
            chain(V.tensor_scalar(tiles[:, :], tiles[:, :], 1.0, None, ALU.max))
            chain(V.tensor_copy(ends[:, :], tiles[:, :]))
            for e in range(1, NX):
                chain(V.tensor_tensor(ends[:, e:e + 1], ends[:, e:e + 1], ends[:, e - 1:e], ALU.add))
            NO = TILES_MAX + 2
            chain(V.tensor_tensor(owner[:, :, :], ends[:, None, :].to_broadcast([P, NO, NX]),
                                  w["count"][:, :, None].to_broadcast([P, NO, NX]), ALU.is_le))
            chain(V.reduce_sum(w["count"][:, :], owner[:, :, :], axis=X))
            chain(V.tensor_scalar(expert[:, :], w["count"][:, :], float(NX - 1), None, ALU.min))
            chain(V.tensor_tensor(tiles[:, :], ends[:, :], tiles[:, :], ALU.subtract))
            chain(V.tensor_scalar(tiles[:, :], tiles[:, :], float(TS), None, ALU.mult))
            row = scan[1 - cur]
            chain(V.tensor_tensor(row[:, :, :], upto[:, :, :], per_tile, ALU.subtract))
            chain(V.tensor_tensor(row[:, :, :], row[:, :, :], below[:, 0:NT * NX].rearrange("p (t e) -> p t e", t=NT),
                                  ALU.add))
            chain(V.tensor_tensor(row[:, :, :], row[:, :, :], each_expert(tiles), ALU.add))
            for i in range(2):
                chain(V.tensor_tensor(key[:, :, :], hot[i][:, :, :], row[:, :, :], ALU.mult))
                chain(V.reduce_sum(tmp[:, :], key[:, :, :], axis=X))
                V.tensor_copy(slots[:, i, :], tmp[:, :]).then_inc(placed, 1)
                dve.wait_ge(placed, i + 1)
            for m, (name, at) in enumerate(chunks):
                dve.wait_ge(hi_done, m + 1)
                V.scalar_tensor_tensor(column(split[name][1], at), raw[:, m % 2, :], WSCALE, column(split[name][0], at),
                                       ALU.mult, ALU.subtract).then_inc(lo_done, 1)

        @block.gpsimd
        def _(pool):
            nc.gpsimd.memset(ones[:, :], 1.0).then_inc(ones_set, 1)
            pool.wait_ge(placed, 2)
            for i in range(2):
                for t in range(NT):
                    pool.indirect_dma_start(out=xs, out_offset=bass.IndirectOffsetOnAxis(ap=slots[:, i, t:t + 1], axis=0),
                                            in_=x1[:, t, :], in_offset=None).then_inc(scattered, 16)
            pool.wait_ge(scattered, 16 * 2 * NT)


def experts(nc, banks, w, split, expert, xs, ys):
    MT = M // P
    SUB = TS // P
    with ExitStack() as own:
        def sb(name, shape, dt=F32):
            return own.enter_context(nc.sbuf_tensor(name, shape, dt))

        def sem(name):
            return own.enter_context(nc.semaphore(name))

        x = sb("x_tile", [P, SUB, E])
        xh, xl = sb("xh", [P, ET, TS], F16), sb("xl", [P, ET, TS], F16)
        hf = [sb(f"hf{i}", [P, MT, TS]) for i in range(2)]
        hh = [sb(f"hh{i}", [P, MT, TS], F16) for i in range(2)]
        hl = [sb(f"hl{i}", [P, MT, TS], F16) for i in range(2)]
        y = sb("y", [P, SUB, E])
        x_in, turned, x_hi, x_lo = sem("xt_in"), sem("xt_turned"), sem("x_hi"), sem("x_lo")
        made = [sem(f"layer{i}") for i in range(3)]
        full = [sem(f"full{i}") for i in range(2)]
        hi = [sem(f"hi{i}") for i in range(2)]
        lo = [sem(f"lo{i}") for i in range(2)]
        y_done, y_out = sem("y_done"), sem("y_out")
        layer = [banks[0:2], banks[2:4]]
        y_bank, t_bank = banks[4], banks[5]
        bias = [w["b1"], w["b2"]]
        block = own.enter_context(nc.Block())

        def turns(engine, body):
            body(0)
            with engine.Fori(1, TILES_MAX) as i:
                body(i)

        @block.sync
        def _(sp):
            def load(i):
                sp.dma_start(x[:, :, :], xs[bass.ds(i * TS, TS), :].rearrange("(s p) e -> p s e", p=P)).then_inc(x_in, 16)

            load(0)
            sp.wait_ge(turned, 1)
            load(1)

            def body(i):
                sp.wait_ge(turned, i + 2)
                load(i + 2)
                sp.wait_ge(y_done, i + 1)
                sp.dma_start(ys[bass.ds(i * TS, TS), :].rearrange("(s p) e -> p s e", p=P), y[:, :, :]).then_inc(y_out, 16)

            turns(sp, body)
            sp.wait_ge(y_out, 16 * TILES_MAX)

        @block.tensor
        def _(pe):
            def turn(i):
                pe.wait_ge(x_in, (i + 1) * 16)
                after(pe, x_lo, i)
                for e in range(ET):
                    for s in range(SUB):
                        last = nc.tensor.transpose(t_bank[:, (e * SUB + s) * P:(e * SUB + s + 1) * P],
                                                   x[:, s, e * P:(e + 1) * P], w["ident"][:, :])
                last.then_inc(turned, 1)

            def weights(name, part, e, k, cols):
                return split[name][part][:, bass.ds(e, 1), k, cols].rearrange("p a n -> p (a n)")

            def hidden(which, i, e):
                name, K = ("w1", ET) if which == 0 else ("w2", MT)
                ah, al = (xh, xl) if which == 0 else (hh[0], hl[0])
                if which == 0:
                    pe.wait_ge(x_lo, i + 1)
                for m in range(MT):
                    after(pe, full[which], i * MT + m // 2 * 2)
                    out = layer[which][m // 2][:, m % 2 * TS:(m % 2 + 1) * TS]
                    c = slice(m * P, (m + 1) * P)
                    for k in range(K):
                        if which == 1 and m == 0:
                            pe.wait_ge(lo[0], i * MT + k + 1)
                        for a, part in ((ah, 0), (ah, 1), (al, 0)):
                            last = nc.tensor.matmul(out, weights(name, part, e, k, c), a[:, k, :],
                                                    start=(k == 0 and a is ah and part == 0),
                                                    stop=(k == K - 1 and a is al), skip_group_check=True)
                    last.then_inc(made[which], 1)

            def final(i, e):
                after(pe, y_done, i)
                for s in range(SUB):
                    r = slice(s * P, (s + 1) * P)
                    for k in range(MT):
                        if s == 0:
                            pe.wait_ge(lo[1], i * MT + k + 1)
                        for a, part in ((hh[1], 0), (hh[1], 1), (hl[1], 0)):
                            last = nc.tensor.matmul(y_bank[:, s * E:(s + 1) * E], a[:, k, r],
                                                    weights("w3", part, e, k, slice(0, E)),
                                                    start=(k == 0 and a is hh[1] and part == 0),
                                                    stop=(k == MT - 1 and a is hl[1]), skip_group_check=True)
                last.then_inc(made[2], 1)

            def expert_of(i):
                return pe.value_load(expert[0:1, bass.ds(i, 1)], min_val=0, max_val=NX - 1)

            turn(0)
            hidden(0, 0, expert_of(0))
            turn(1)

            def body(i):
                e = expert_of(i)
                e_next = expert_of(i + 1)
                hidden(1, i, e)
                hidden(0, i + 1, e_next)
                turn(i + 2)
                final(i, e)

            turns(pe, body)

        @block.scalar
        def _(act):
            def take_turned(i):
                act.wait_ge(turned, i + 1)
                after(act, made[0], i * MT)
                nc.scalar.activation(xh[:, :, :].rearrange("p e n -> p (e n)"), t_bank[:, :], ACT.Copy).then_inc(x_hi, 1)

            def take_hidden(which, i):
                e = act.value_load(expert[0:1, bass.ds(i, 1)], min_val=0, max_val=NX - 1)
                for m in range(MT):
                    act.wait_ge(made[which], i * MT + m // 2 * 2 + 2)
                    after(act, lo[which], i * MT)
                    nc.scalar.activation(hf[which][:, m, :], layer[which][m // 2][:, m % 2 * TS:(m % 2 + 1) * TS],
                                         ACT.Relu, bias=bias[which][:, bass.ds(e, 1), m], scale=1.0 / WSCALE)\
                        .then_inc(full[which], 1)

            take_turned(0)
            take_hidden(0, 0)
            take_turned(1)

            def body(i):
                take_hidden(1, i)
                take_hidden(0, i + 1)
                take_turned(i + 2)

            turns(act, body)

        @block.vector
        def _(dve):
            def take_turned(i):
                dve.wait_ge(x_hi, i + 1)
                nc.vector.tensor_tensor(xl[:, :, :].rearrange("p e n -> p (e n)"), t_bank[:, :],
                                        xh[:, :, :].rearrange("p e n -> p (e n)"), ALU.subtract).then_inc(x_lo, 1)

            def take_hidden(which, i):
                for m in range(MT):
                    dve.wait_ge(full[which], i * MT + m + 1)
                    if m == 0:
                        after(dve, made[which + 1], i * (MT if which == 0 else 1))
                    nc.vector.tensor_copy(hh[which][:, m, :], hf[which][:, m, :]).then_inc(hi[which], 1)

            def take_final(i):
                e = dve.value_load(expert[0:1, bass.ds(i, 1)], min_val=0, max_val=NX - 1)
                dve.wait_ge(made[2], i + 1)
                after(dve, y_out, i * 16)
                for s in range(SUB):
                    last = nc.vector.scalar_tensor_tensor(y[:, s, :], y_bank[:, s * E:(s + 1) * E], 1.0 / WSCALE,
                                                          w["b3"][:, bass.ds(e, 1), :].rearrange("p a n -> p (a n)"),
                                                          ALU.mult, ALU.add)
                last.then_inc(y_done, 1)

            take_turned(0)
            take_hidden(0, 0)
            take_turned(1)

            def body(i):
                take_hidden(1, i)
                take_hidden(0, i + 1)
                take_turned(i + 2)
                take_final(i)

            turns(dve, body)

        @block.gpsimd
        def _(pool):
            def take_hidden(which, i):
                for m in range(MT):
                    pool.wait_ge(hi[which], i * MT + m + 1)
                    nc.gpsimd.tensor_tensor(hl[which][:, m, :], hf[which][:, m, :], hh[which][:, m, :],
                                            ALU.subtract).then_inc(lo[which], 1)

            take_hidden(0, 0)

            def body(i):
                take_hidden(1, i)
                take_hidden(0, i + 1)

            turns(pool, body)


def combine(nc, x1, top, slots, ys, out):
    NT, RINGS = T // P, 4
    with ExitStack() as own:
        def sem(name):
            return own.enter_context(nc.semaphore(name))

        g = own.enter_context(nc.sbuf_tensor("g", [P, 2, RINGS, E], F32))
        part = own.enter_context(nc.sbuf_tensor("part", [P, RINGS, E], F32))
        gathered = [sem(f"gathered{i}") for i in range(RINGS)]
        half, added, stored = sem("half"), sem("added"), sem("stored")
        block = own.enter_context(nc.Block())

        @block.gpsimd
        def _(pool):
            for t in range(NT):
                if t >= RINGS:
                    pool.wait_ge(added, t - RINGS + 1)
                for i in range(2):
                    pool.indirect_dma_start(out=g[:, i, t % RINGS, :], out_offset=None, in_=ys,
                                            in_offset=bass.IndirectOffsetOnAxis(ap=slots[:, i, t:t + 1], axis=0))\
                        .then_inc(gathered[t % RINGS], 16)

        @block.vector
        def _(dve):
            for t in range(NT):
                dve.wait_ge(gathered[t % RINGS], 32 * (t // RINGS + 1))
                nc.vector.scalar_tensor_tensor(part[:, t % RINGS, :], g[:, 0, t % RINGS, :], top[:, 0, t:t + 1],
                                               x1[:, t, :], ALU.mult, ALU.add).then_inc(half, 1)
                dve.wait_ge(half, t + 1)
                nc.vector.scalar_tensor_tensor(x1[:, t, :], g[:, 1, t % RINGS, :], top[:, 1, t:t + 1],
                                               part[:, t % RINGS, :], ALU.mult, ALU.add).then_inc(added, 1)

        @block.sync
        def _(sp):
            for c in range(NT // TT):
                sp.wait_ge(added, (c + 1) * TT)
                sp.dma_start(out[:, c * TT:(c + 1) * TT, :], x1[:, c * TT:(c + 1) * TT, :]).then_inc(stored, 16)
            sp.wait_ge(stored, 16 * (NT // TT))


def kernel(**inputs):
    import concourse.bacc as bacc
    from concourse.bass_utils import run_bass_kernel_spmd

    arrays = {n: np.ascontiguousarray(a) for n, a in layout(inputs).items()}
    nc = bacc.Bacc("TRN2", target_bir_lowering=False, num_devices=1)
    dram = {}
    for n, shape in INPUTS.items():
        assert list(arrays[n].shape) == shape, n
        dram[n] = nc.dram_tensor("in_" + n, shape, F32, kind="ExternalInput").ap()
    out = nc.dram_tensor("out", OUT, F32, kind="ExternalOutput").ap()
    program(nc, dram, out)
    result = run_bass_kernel_spmd(nc, [{"in_" + n: arrays[n] for n in INPUTS}], core_ids=[0])
    return finish(result.results[0]["out"])


def layout(i):
    def cols(a):
        return np.asarray(a).reshape(-1, P).T

    def rows(a):
        a = np.asarray(a)
        return a.reshape(-1, P, a.shape[-1]).transpose(1, 0, 2)

    def rep(a, n=P):
        return np.broadcast_to(np.asarray(a), (n, np.asarray(a).shape[-1]))

    def strips(a):
        a = np.asarray(a)
        wide = np.zeros((a.shape[0], H, HW), a.dtype)
        wide[:, :, 0:HD] = a.reshape(a.shape[0], H, HD)
        return wide.reshape(a.shape[0], H * HW)

    x = np.asarray(i["x"]).reshape(T, E)
    wqkv, bqkv = np.asarray(i["L0_cond_Wqkv"]), np.asarray(i["L0_cond_bqkv"])
    wc1 = np.asarray(i["L0_cond_Wc1"])
    bk = strips(bqkv[None, E:2 * E]).reshape(H, HW).copy()
    bk[:, SHIFT] = 1.0
    rate = np.float32(10000.0) ** np.repeat(np.arange(0, E, 2, dtype=np.float32) / np.float32(E), 2)
    pe = np.sin(np.arange(S, dtype=np.float32)[:, None] / rate[None, :]).astype(np.float32)
    return {
        "xT": rows(x.T), "x": x.reshape(T // P, P, E).transpose(1, 0, 2),
        "wq": rows(strips(wqkv[0:E].T)), "wk": rows(strips(wqkv[E:2 * E].T)),
        "bq": cols(strips(bqkv[None, 0:E]).reshape(-1)), "bk": cols(bk.reshape(-1)),
        "wv": rows(wqkv[2 * E:].T), "bv": rep(bqkv[2 * E:]),
        "wo": rows(np.asarray(i["L0_cond_Wout"]).T), "bo": rep(i["L0_cond_bout"]),
        "wc1x": rows(wc1[:, 0:E].T), "wc1c": wc1[:, E:].T, "bc1": cols(i["L0_cond_bc1"]),
        "wc2": rows(np.asarray(i["L0_cond_Wc2"]).T), "bc2": rep(i["L0_cond_bc2"]),
        "cT": np.asarray(i["cond_256"]).T, "we1": np.asarray(i["L0_cond_We1"]).T, "be1": cols(i["L0_cond_be1"]),
        "we2": rows(np.asarray(i["L0_cond_We2"]).T), "be2": rep(i["L0_cond_be2"], B),
        "ln_g": rep(i["L0_cond_ln_g"], B), "ln_b": rep(i["L0_cond_ln_b"], B),
        "pe": rows(pe.T), "ident": np.eye(P, dtype=np.float32),
        "rms_w": cols(i["L1_cond_rms_w"]), "wg": rows(i["L1_cond_wg_W"]),
        "gate_b": np.stack([rep(i["L1_cond_wg_b"]), rep(i["L1_cond_gg_b"])], 1), "gg": np.asarray(i["L1_cond_gg_W"]),
        "w1": np.asarray(i["L1_cond_W1"]).reshape(NX, ET, P, M).transpose(2, 0, 1, 3),
        "b1": np.asarray(i["L1_cond_b1"]).reshape(NX, M // P, P).transpose(2, 0, 1),
        "w2": np.asarray(i["L1_cond_W2"]).reshape(NX, M // P, P, M).transpose(2, 0, 1, 3),
        "b2": np.asarray(i["L1_cond_b2"]).reshape(NX, M // P, P).transpose(2, 0, 1),
        "w3": np.asarray(i["L1_cond_W3"]).reshape(NX, M // P, P, E).transpose(2, 0, 1, 3),
        "b3": np.broadcast_to(np.asarray(i["L1_cond_b3"])[None], (P, NX, E)),
        "tri": np.triu(np.ones((P, P), np.float32), 1),
        "count": np.broadcast_to(np.arange(TILES_MAX + 2, dtype=np.float32), (P, TILES_MAX + 2)),
    }


OUT = [P, T // P, E]


def finish(out):
    return np.asarray(out).transpose(1, 0, 2).reshape(B, S, E)
```

```python
from contextlib import ExitStack

import numpy as np

import concourse.bass as bass
from concourse import mybir

P = 128
B, S, E = 8, 512, 256
H, HD = 16, 16
CD = 64
NX, M = 8, 512
T = B * S
ET = E // P
TT = S // P
G = 4
NG = H // G
HW = 32
SUM = HD
Q_PARTS = (0, 1, 2, 0, 1, 0)
K_PARTS = (0, 0, 0, 1, 1, 2)
STACK = HD * len(Q_PARTS)
SHIFTS = 2
COUPLING = 0.3 * 0.7
KEEP = 1.0 - COUPLING
SCALE = 1.0 / float(HD) ** 0.5
RING = 3

TS = 256
TILES_MAX = 2 * T // TS + NX - 1
WSCALE = 16.0

F32 = mybir.dt.float32
F16 = mybir.dt.float16
BF16 = mybir.dt.bfloat16
I32 = mybir.dt.int32
F32R = mybir.dt.float32r
ALU = mybir.AluOpType
ACT = mybir.ActivationFunctionType
X = mybir.AxisListType.X

INPUTS = {
    "xT": [P, ET, T], "x": [P, T // P, E],
    "wq": [P, ET, E], "wk": [P, ET, E], "bq": [P, ET], "bk": [P, ET],
    "wv": [P, ET, E], "bv": [P, E], "wo": [P, ET, E], "bo": [P, E],
    "wc1x": [P, ET, E], "wc1c": [CD, E], "bc1": [P, ET], "wc2": [P, ET, H], "bc2": [P, H],
    "cT": [CD, B], "we1": [CD, E], "be1": [P, ET], "we2": [P, ET, E], "be2": [B, E],
    "ln_g": [B, E], "ln_b": [B, E], "pe": [P, ET, S], "ident": [P, P],
    "rms_w": [P, ET], "wg": [P, ET, NX], "gate_b": [P, 2, NX], "gg": [CD, NX],
    "w1": [P, NX, ET, M], "b1": [P, NX, M // P], "w2": [P, NX, M // P, M], "b2": [P, NX, M // P],
    "w3": [P, NX, M // P, E], "b3": [P, NX, E], "tri": [P, P], "count": [P, TILES_MAX + 2],
}


FOR_SETUP = ("wc1c", "bc1", "cT", "we1", "be1", "we2", "be2", "ln_g", "ln_b", "pe", "rms_w", "wg", "gate_b", "gg")
FOR_ATTENTION = ("wq", "wk", "bq", "bk", "wv", "bv", "wo", "bo", "wc1x", "wc2", "bc2")
FOR_EXPERTS = ("b1", "b2", "b3", "tri", "count")


def program(nc, dram, out, dbg=None):
    with ExitStack() as ctx:
        def sb(name, shape, dt=F32):
            return ctx.enter_context(nc.sbuf_tensor(name, shape, dt))

        banks = [ctx.enter_context(nc.psum_tensor(f"bank{i}", [P, 512], F32)) for i in range(8)]
        w = {"ident": sb("w_ident", [P, P])}
        x1 = sb("x1", [P, T // P, E])
        gbias = sb("gbias", [P, B, NX])
        wgr = sb("wgr", [P, ET, NX])
        xs = nc.dram_tensor("xs", [(TILES_MAX + 2) * TS, E], F32).ap()
        parts_dram = nc.dram_tensor("parts_dram", [3, 2 * E, S], BF16).ap()
        ys = nc.dram_tensor("ys", [TILES_MAX * TS, E], F32).ap()

        with ExitStack() as own:
            for n in FOR_ATTENTION:
                w[n] = own.enter_context(nc.sbuf_tensor("w_" + n, INPUTS[n], F32))
            fa = own.enter_context(nc.sbuf_tensor("fa", [P, TT, B], F32))
            cbias = own.enter_context(nc.sbuf_tensor("cbias", [P, ET, B], F32))
            setup(nc, dram, banks, w, x1, fa, cbias, gbias, wgr)
            attention(nc, banks, dram, w, x1, fa, cbias, xs, parts_dram)
        for n in FOR_EXPERTS:
            w[n] = sb("w_" + n, INPUTS[n])
        split = {n: (sb(n + "_hi", INPUTS[n], F16), sb(n + "_lo", INPUTS[n], F16)) for n in ("w1", "w2", "w3")}
        top = sb("top", [P, 2, T // P])
        slots = sb("slots", [P, 2, T // P], I32)
        expert = sb("expert", [P, TILES_MAX + 2], I32)
        route(nc, banks, dram, w, x1, gbias, wgr, split, top, slots, expert, xs)
        experts(nc, banks, w, split, expert, xs, ys)
        combine(nc, x1, top, slots, ys, out)


def setup(nc, dram, banks, w, x1, fa, cbias, gbias, wgr):
    with ExitStack() as own:
        def sb(name, shape, dt=F32):
            return own.enter_context(nc.sbuf_tensor(name, shape, dt))

        loaded = own.enter_context(nc.semaphore("loaded"))
        x_loaded = own.enter_context(nc.semaphore("x_loaded"))
        pe_done = own.enter_context(nc.semaphore("setup_pe"))
        dve_done = own.enter_context(nc.semaphore("setup_dve"))
        act_done = own.enter_context(nc.semaphore("setup_act"))
        w = dict(w, **{n: sb("w_" + n, INPUTS[n]) for n in FOR_SETUP})
        crep = sb("crep", [CD, B, P])
        e1 = sb("e1", [P, ET, B])
        fp = sb("fp", [B, E])
        sq = sb("sq", [B, E])
        fpT = sb("fpT", [P, ET, B])
        lg = sb("lg", [B, S])
        st = sb("st", [B, 8])
        block = own.enter_context(nc.Block())

        @block.sync
        def _(sp):
            sp.dma_start(x1[:, :, :], dram["x"]).then_inc(x_loaded, 16)
            for n, t in w.items():
                sp.dma_start(t[tuple(slice(None) for _ in t.shape)], dram[n]).then_inc(loaded, 16)

        @block.gpsimd
        def _(pool):
            pool.wait_ge(loaded, 16 * len(w))
            pool.wait_ge(x_loaded, 16)
            nc.gpsimd.tensor_tensor(x1[:, :, :], x1[:, :, :],
                                    w["bo"][:, None, :].to_broadcast([P, T // P, E]), ALU.add)

        @block.tensor
        def _(pe):
            pe.wait_ge(loaded, 16 * len(w))
            for m in range(ET):
                nc.tensor.matmul(banks[0][:, m * B:(m + 1) * B], w["we1"][:, m * P:(m + 1) * P], w["cT"][:, :],
                                 start=(m == 0), stop=True, skip_group_check=True)
                nc.tensor.matmul(banks[2][:, m * B:(m + 1) * B], w["wc1c"][:, m * P:(m + 1) * P], w["cT"][:, :],
                                 start=(m == 0), stop=True, skip_group_check=True).then_inc(pe_done, 1)
            pe.wait_ge(dve_done, 1)
            for b in range(B):
                last = nc.tensor.matmul(banks[3][:, b * NX:(b + 1) * NX], crep[:, b, :], w["gg"][:, :],
                                        start=(b == 0), stop=True, skip_group_check=True)
            last.then_inc(pe_done, 1)
            pe.wait_ge(act_done, 2)
            for k in range(ET):
                last = nc.tensor.matmul(banks[4][0:B, 0:E], e1[:, k, :], w["we2"][:, k, :], start=(k == 0), stop=(k == ET - 1))
            last.then_inc(pe_done, 1)
            pe.wait_ge(dve_done, 18)
            for k in range(ET):
                last = nc.tensor.transpose(banks[5][:, k * B:(k + 1) * B], fp[:, k * P:(k + 1) * P], w["ident"][0:B, 0:B])
            last.then_inc(pe_done, 1)
            pe.wait_ge(dve_done, 19)
            for k in range(ET):
                last = nc.tensor.matmul(banks[6][0:B, :], fpT[:, k, :], w["pe"][:, k, :], start=(k == 0), stop=(k == ET - 1))
            last.then_inc(pe_done, 1)
            pe.wait_ge(dve_done, 22)
            for t in range(TT):
                last = nc.tensor.transpose(banks[7][:, t * B:(t + 1) * B], lg[:, t * P:(t + 1) * P], w["ident"][0:B, 0:B])
            last.then_inc(pe_done, 1)

        @block.scalar
        def _(act):
            act.wait_ge(loaded, 16 * len(w))
            act.wait_ge(pe_done, 2)
            for m in range(ET):
                nc.scalar.activation(e1[:, m, :], banks[0][:, m * B:(m + 1) * B], ACT.Relu,
                                     bias=w["be1"][:, m:m + 1]).then_inc(act_done, 1)
            for m in range(ET):
                nc.scalar.activation(cbias[:, m, :], banks[2][:, m * B:(m + 1) * B], ACT.Identity,
                                     bias=w["bc1"][:, m:m + 1])
            act.wait_ge(dve_done, 11)
            nc.scalar.activation(st[:, 7:8], st[:, 3:4], ACT.Sqrt).then_inc(act_done, 1)
            act.wait_ge(dve_done, 20)
            nc.scalar.activation(lg[:, :], banks[6][0:B, :], ACT.Exp, bias=st[:, 5:6],
                                 accum_out=st[:, 6:7]).then_inc(act_done, 1)

        @block.vector
        def _(dve):
            n = [0]

            def chain(ins):
                n[0] += 1
                ins.then_inc(dve_done, 1)
                dve.wait_ge(dve_done, n[0])

            dve.wait_ge(loaded, 16 * len(w))
            chain(nc.vector.tensor_copy(crep[:, :, :], w["cT"][:, :, None].to_broadcast([CD, B, P])))
            for k in range(ET):
                last = nc.vector.tensor_scalar(wgr[:, k, :], w["wg"][:, k, :], w["rms_w"][:, k:k + 1], None, ALU.mult)
            chain(last)
            dve.wait_ge(pe_done, 3)
            gb = gbias[:, :, :]
            chain(nc.vector.tensor_tensor(gb, banks[3][:, 0:B * NX].rearrange("p (b e) -> p b e", b=B),
                                          w["gate_b"][:, 0:1, :].to_broadcast([P, B, NX]), ALU.add))
            chain(nc.vector.tensor_tensor(gb, gb, w["gate_b"][:, 1:2, :].to_broadcast([P, B, NX]), ALU.add))
            dve.wait_ge(pe_done, 4)
            chain(nc.vector.tensor_tensor(fp[:, :], banks[4][0:B, 0:E], w["be2"][:, :], ALU.add))
            chain(nc.vector.reduce_sum(st[:, 0:1], fp[:, :], axis=X))
            chain(nc.vector.tensor_scalar(st[:, 1:2], st[:, 0:1], 1.0 / E, None, ALU.mult))
            chain(nc.vector.tensor_scalar(fp[:, :], fp[:, :], st[:, 1:2], None, ALU.subtract))
            chain(nc.vector.tensor_tensor(sq[:, :], fp[:, :], fp[:, :], ALU.mult))
            chain(nc.vector.reduce_sum(st[:, 2:3], sq[:, :], axis=X))
            chain(nc.vector.tensor_scalar(st[:, 3:4], st[:, 2:3], 1.0 / E, 1e-5, ALU.mult, ALU.add))
            dve.wait_ge(act_done, 3)
            chain(nc.vector.reciprocal(st[:, 4:5], st[:, 7:8]))
            chain(nc.vector.tensor_tensor(st[:, 6:7], st[:, 4:5], st[:, 4:5], ALU.mult))
            chain(nc.vector.tensor_tensor(st[:, 6:7], st[:, 6:7], st[:, 3:4], ALU.mult))
            chain(nc.vector.tensor_scalar(st[:, 6:7], st[:, 6:7], -0.5, 1.5, ALU.mult, ALU.add))
            chain(nc.vector.tensor_tensor(st[:, 4:5], st[:, 4:5], st[:, 6:7], ALU.mult))
            chain(nc.vector.scalar_tensor_tensor(fp[:, :], fp[:, :], st[:, 4:5], w["ln_g"][:, :],
                                                 ALU.mult, ALU.mult))
            chain(nc.vector.tensor_tensor(fp[:, :], fp[:, :], w["ln_b"][:, :], ALU.add))
            dve.wait_ge(pe_done, 5)
            chain(nc.vector.tensor_copy(fpT[:, :, :], banks[5][:, 0:ET * B].rearrange("p (k b) -> p k b", k=ET)))
            dve.wait_ge(pe_done, 6)
            chain(nc.vector.tensor_reduce(st[:, 5:6], banks[6][0:B, :], X, ALU.max, negate=True))
            dve.wait_ge(act_done, 4)
            chain(nc.vector.reciprocal(st[:, 7:8], st[:, 6:7]))
            chain(nc.vector.tensor_scalar(lg[:, :], lg[:, :], st[:, 7:8], COUPLING, ALU.mult, ALU.mult))
            dve.wait_ge(pe_done, 7)
            chain(nc.vector.tensor_copy(fa[:, :, :], banks[7][:, 0:TT * B].rearrange("p (t b) -> p t b", t=TT)))


PLAN = {
    (0, 0): [("pj", 0), ("pj", 1)],
    (0, 1): [("mt", 1), ("pj", 2)],
    (0, 2): [("ot", 3), ("pj", 3)],
    (0, 3): [("coh", 0)],
    (1, 0): [("at", 0), ("vs", 0)],
    (1, 1): [("mt", 2), ("v", 0)],
    (1, 2): [("ot", 0), ("c1", 0)],
    (1, 3): [("at", 1), ("c1", 1)],
    (2, 0): [("op", 0)],
    (2, 1): [("mt", 3), ("v", 1)],
    (2, 2): [("ot", 1), ("op", 1)],
    (2, 3): [],
    (3, 0): [],
    (3, 1): [("mt", 0)],
    (3, 2): [("ot", 2)],
    (3, 3): [],
}
LAST_WORK = [("ot", 3), ("at", 0), ("at", 1), ("op", 0), ("op", 1)]
NEXT_WORK = [("pj", i) for i in range(4)] + [("c1", 0), ("c1", 1)] + [("v", 0), ("v", 1)] + [("mt", 0)]
FIRST, TAIL = NEXT_WORK, LAST_WORK
ORDER = [task for step in range(NG) for slot in range(TT) for task in PLAN[step, slot]]
LEAD = 2 * TT
TILES = NG * TT * G
SLOTS = NG * TT
LINKS = 2 * NG + 3
READS = 16 * 2 * len(Q_PARTS)


def kept(kind):
    left_out = {"first": LAST_WORK, "mid": [], "last": NEXT_WORK}[kind]
    return [task for task in ORDER if task not in left_out]


def misc_base(kind, b):
    return len(FIRST) if kind == "first" else len(FIRST) + len(kept("first")) + (b - 1) * len(ORDER)


def misc_use(kind, b, task):
    return misc_base(kind, b) + kept(kind).index(task)


TAIL_BASE = misc_base("last", B - 1) + len(kept("last"))


def lead_block(kind, b, g, jt):
    at = g * TT + jt + LEAD
    if at < SLOTS:
        return b, at
    return None if kind == "last" else (b + 1, at - SLOTS)


def after(engine, semaphore, count):
    if not (isinstance(count, int) and count == 0):
        engine.wait_ge(semaphore, count)


def batches(engine, body):
    body("first", 0, 0)
    with engine.Fori(0, (B - 2) // 2) as pair:
        body("mid", 2 * pair + 1, 1)
        body("mid", 2 * pair + 2, 0)
    body("last", B - 1, 1)


def attention(nc, banks, dram, w, x1, fa, cbias, xs, parts_dram):
    with ExitStack() as own:
        def sb(name, shape, dt=F32):
            return own.enter_context(nc.sbuf_tensor(name, shape, dt))

        def sem(name):
            return own.enter_context(nc.semaphore(name))

        xT = sb("xT", [P, 2, ET, S])
        parts = sb("parts", [P, 3, 2 * ET, S], BF16)
        rest = sb("rest", [P, 2 * ET, S])
        q = sb("q", [P, 2, H, S], BF16)
        k = sb("k", [P, 2, H, S], BF16)
        v = sb("v", [P, 2, TT, H, HW])
        mx = sb("mx", [P, 2, TT, G])
        mxp = sb("mxp", [P, 2, TT, SHIFTS, G], BF16)
        shift = sb("shift", [SHIFTS * G, 2, S], BF16)
        ident = sb("ident16", [P, P], BF16)
        pr = sb("pr", [P, TT, G, S])
        oT = sb("oT", [P, S])
        hT = sb("hT", [P, ET, S])
        z = sb("z", [P, TT, H])
        ez = sb("ez", [P, TT, H])
        coh = sb("coh", [P, TT, H])
        div = sb("div", [P, TT, G])
        rdiv = sb("rdiv", [P, TT, G])
        att = sb("att", [P, TT, E])
        attT = sb("attT", [P, ET, S])
        vsum = sb("vsum", [P, E])
        facur = sb("facur", [P, TT])
        ones = sb("ones", [P, P])
        zeros = sb("zeros", [P, 2 * E])

        cleared = sem("cleared")
        xs_cleared = sem("xs_cleared")
        x_in = [sem("x_in0"), sem("x_in1")]
        first_part = sem("first_part")
        second_part, parts_done = sem("second_part"), sem("parts_done")
        parts_out = sem("parts_out")
        stack_in = sem("stack_in")
        a_ready, a_read = sem("a_ready"), sem("a_read")
        b_ready, b_read = sem("b_ready"), sem("b_read")
        max_first, mx_split = sem("max_first"), sem("mx_split")
        shift_in = sem("shift_in")
        slots_free = sem("slots_free")
        out_copied = sem("out_copied")
        misc_ready, misc_read = sem("misc_ready"), sem("misc_read")
        z_ready, ez_ready = sem("z_ready"), sem("ez_ready")
        link = sem("link")
        a_bank, b_bank, pv_bank, misc = banks[0:RING], banks[RING:2 * RING], banks[6], banks[7]
        turned_shift = misc[0:SHIFTS * G, 0:S // 2].bitcast(BF16)
        block = own.enter_context(nc.Block())

        @block.sync
        def _(sp):
            def load_x(b, par):
                sp.dma_start(xT[:, par, :, :], dram["xT"][:, :, bass.ds(b * S, S)]).then_inc(x_in[par], 16)

            def make_stacks(b, par):
                sp.wait_ge(parts_done, 4 * b + 4)
                for c in range(3):
                    sp.dma_start(parts_dram[c].rearrange("(i p) n -> p i n", p=P), parts[:, c, :, :]).then_inc(parts_out, 16)
                sp.wait_ge(parts_out, 48 * b + 48)
                for j in range(len(Q_PARTS)):
                    rows = slice(j * HD, (j + 1) * HD)
                    for stack, c, first in ((q, Q_PARTS[j], 0), (k, K_PARTS[j], E)):
                        sp.dma_start(stack[rows, par, :, :], parts_dram[c][first:first + E, :]
                                     .rearrange("(h d) n -> d h n", d=HD)).then_inc(stack_in, 16)

            load_x(0, 0)
            load_x(1, 1)
            make_stacks(0, 0)
            sp.wait_ge(cleared, 6)
            rows = 2 * P
            for t in range((TILES_MAX + 2) * TS // rows):
                sp.dma_start(xs[t * rows:(t + 1) * rows, :].rearrange("(p r) e -> p (r e)", r=2),
                             zeros[:, :]).then_inc(xs_cleared, 16)

            def body(kind, b, par):
                if kind == "last":
                    return
                sp.wait_ge(stack_in, READS * (b + 1))
                make_stacks(b + 1, 1 - par)

            def load_after(kind, b, par):
                first = (b + 2) * S if isinstance(b, int) else sp.snap((b + 2) * S)
                sp.wait_ge(misc_ready, misc_base(kind, b))
                sp.dma_start(xT[:, par, :, :], dram["xT"][:, :, bass.ds(first, S)]).then_inc(x_in[par], 16)

            def turn(kind, b, par, more=True):
                if more:
                    load_after(kind, b, par)
                body(kind, b, par)

            turn("first", 0, 0)
            with sp.Fori(0, (B - 4) // 2) as pair:
                turn("mid", 2 * pair + 1, 1)
                turn("mid", 2 * pair + 2, 0)
            turn("mid", B - 3, 1)
            turn("mid", B - 2, 0, more=False)
            sp.wait_ge(stack_in, READS * B)
            sp.wait_ge(xs_cleared, 16 * ((TILES_MAX + 2) * TS // rows))

        @block.gpsimd
        def _(pool):
            nc.gpsimd.memset(zeros[:, :], 0.0).then_inc(cleared, 1)
            nc.gpsimd.memset(ones[:, :], 1.0).then_inc(cleared, 1)
            nc.gpsimd.memset(v[:, :, :, :, SUM + 1:HW], 0.0).then_inc(cleared, 1)
            nc.gpsimd.memset(v[:, :, :, :, SUM:SUM + 1], 1.0).then_inc(cleared, 1)
            nc.gpsimd.tensor_copy(ident[:, :], w["ident"][:, :]).then_inc(cleared, 1)
            nc.gpsimd.memset(z[:, :, :], 0.0).then_inc(slots_free, TT)

            def split(b):
                for i in range(4):
                    pool.wait_ge(second_part, 4 * b + i + 1)
                    nc.gpsimd.tensor_tensor(parts[:, 2, i, :], rest[:, i, :], parts[:, 1, i, :],
                                            ALU.subtract).then_inc(parts_done, 1)

            split(0)
            pool.wait_ge(parts_done, 4)
            nc.gpsimd.memset(k[STACK:STACK + SHIFTS, :, :, :], 1.0).then_inc(cleared, 1)
            pool.wait_ge(cleared, 6)

            def body(kind, b, par):
                if kind != "last":
                    split(b + 1)

            batches(pool, body)

        @block.tensor
        def _(pe):
            def bank_free(read, b, n):
                if n >= RING:
                    pe.wait_ge(read, b * TILES + n - RING + 1)
                elif not (isinstance(b, int) and b == 0):
                    pe.wait_ge(read, b * TILES)

            def a_tile(b, at, h, par):
                g, it = at // TT, at % TT
                n = at * G + h
                bank_free(a_read, b, n)
                nc.tensor.matmul(a_bank[n % RING][:, :], q[0:STACK, par, g * G + h, it * P:(it + 1) * P],
                                 k[0:STACK, par, g * G + h, :], start=True, stop=True).then_inc(a_ready, 1)

            def b_tile(b, g, jt, h, par):
                n = (g * TT + jt) * G + h
                bank_free(b_read, b, n)
                r = slice(0, STACK + SHIFTS)
                nc.tensor.matmul(b_bank[n % RING][:, :], k[r, par, g * G + h, jt * P:(jt + 1) * P],
                                 q[r, par, g * G + h, :], start=True, stop=True).then_inc(b_ready, 1)

            def pv(b, g, jt, par):
                pe.wait_ge(b_read, b * TILES + (g * TT + jt + 1) * G)
                if jt == 0 and not (isinstance(b, int) and b == 0 and g == 0):
                    pe.wait_ge(out_copied, b * NG + g)
                for h in range(G):
                    last = nc.tensor.matmul(pv_bank[HW * h:HW * h + HW, :], v[:, par, jt, g * G + h, :], pr[:, jt, h, :],
                                            start=(jt == 0), stop=(jt == TT - 1), tile_position=(0, HW * h))
                last.then_inc(slots_free, 1)

            def turned(src):
                for t in range(TT):
                    last = nc.tensor.transpose(misc[:, t * P:(t + 1) * P], src(t), w["ident"][:, :])
                return last

            def product(task, no, par):
                what, i = task
                after(pe, misc_read, no)
                if what in ("pj", "c1"):
                    wt = w["wc1x"] if what == "c1" else w["wq"] if i < ET else w["wk"]
                    f = i % ET
                    for e in range(ET):
                        last = nc.tensor.matmul(misc[:, :], wt[:, e, f * P:(f + 1) * P], xT[:, par, e, :],
                                                start=(e == 0), stop=(e == ET - 1))
                elif what == "v":
                    for t in range(2):
                        for e in range(ET):
                            last = nc.tensor.matmul(misc[:, t * E:(t + 1) * E],
                                                    xT[:, par, e, (2 * i + t) * P:(2 * i + t + 1) * P], w["wv"][:, e, :],
                                                    start=(t == 0 and e == 0), stop=(e == ET - 1), skip_group_check=True)
                elif what == "coh":
                    for t in range(TT):
                        for e in range(ET):
                            last = nc.tensor.matmul(misc[:, t * H:(t + 1) * H], hT[:, e, t * P:(t + 1) * P],
                                                    w["wc2"][:, e, :], start=(t == 0 and e == 0),
                                                    stop=(e == ET - 1), skip_group_check=True)
                elif what == "vs":
                    for t in range(TT):
                        last = nc.tensor.matmul(misc[:, 0:E].rearrange("p (h d) -> p h d", h=H), ones[:, :],
                                                v[:, par, t, :, 0:HD], start=(t == 0), stop=(t == TT - 1))
                elif what == "ot":
                    last = turned(lambda t: oT[:, t * P:(t + 1) * P])
                elif what == "mt":
                    for t in range(TT):
                        last = nc.tensor.transpose(turned_shift[:, t * P:(t + 1) * P],
                                                   mxp[:, i % 2, t, :, :].rearrange("p c h -> p (c h)"), ident[:, :])
                elif what == "at":
                    last = turned(lambda t: att[:, t, i * P:(i + 1) * P])
                elif what == "op":
                    for t in range(2):
                        for e in range(ET):
                            r = slice((2 * i + t) * P, (2 * i + t + 1) * P)
                            last = nc.tensor.matmul(misc[:, t * E:(t + 1) * E], attT[:, e, r], w["wo"][:, e, :],
                                                    start=(t == 0 and e == 0), stop=(e == ET - 1),
                                                    skip_group_check=True)
                last.then_inc(misc_ready, 1)

            def inputs_ready(task, b, par):
                what, i = task
                if what == "mt":
                    pe.wait_ge(mx_split, b * NG + (i if i > 0 else NG) + 1)
                if what == "ot":
                    pe.wait_ge(out_copied, b * NG + (i + 1 if i < NG - 1 else 0))

            pe.wait_ge(cleared, 5)
            pe.wait_ge(x_in[0], 16)
            for no, task in enumerate(FIRST):
                if task == ("mt", 0):
                    pe.wait_ge(stack_in, READS)
                    for at in range(TT):
                        for h in range(G):
                            a_tile(0, at, h, 0)
                    pe.wait_ge(mx_split, 1)
                product(task, no, 0)
            for at in range(TT, LEAD):
                for h in range(G):
                    a_tile(0, at, h, 0)

            def body(kind, b, par):
                for g in range(NG):
                    for jt in range(TT):
                        if jt == 0:
                            pe.wait_ge(shift_in, 32 * (b * NG + g + 1))
                        if kind == "first" and g == 0 and jt == 0:
                            pe.wait_ge(cleared, 6)
                        lead = lead_block(kind, b, g, jt)
                        if lead is not None and lead[1] == 0:
                            pe.wait_ge(stack_in, READS * (b + 2))
                        for h in range(G):
                            b_tile(b, g, jt, h, par)
                            if lead is not None:
                                a_tile(*lead, h, par if g * TT + jt + LEAD < SLOTS else 1 - par)
                        tasks = [t if t in kept(kind) else None for t in PLAN[g, jt]] + [None] * 2
                        for i, task in enumerate(tasks[:2]):
                            if task is not None:
                                if task == ("pj", 0):
                                    x_loaded(kind, b, par)
                                else:
                                    inputs_ready(task, b, par)
                                product(task, misc_use(kind, b, task), 1 - par if task in NEXT_WORK else par)
                            if i == 0 and (g, jt) == (0, 0):
                                if kind != "first":
                                    pv(b - 1, NG - 1, TT - 1, 1 - par)
                            elif i == 0:
                                pv(b, g if jt else g - 1, (jt - 1) % TT, par)

            def x_loaded(kind, b, par):
                pe.wait_ge(x_in[1 - par], (b + 1 + 2 - (1 - par)) * 8)

            batches(pe, body)
            pv(B - 1, NG - 1, TT - 1, 1)
            for n, task in enumerate(TAIL):
                inputs_ready(task, B, 0)
                product(task, TAIL_BASE + n, 0)

        @block.scalar
        def _(act):
            def hidden_layer(i, no, b):
                act.wait_ge(misc_ready, no + 1)
                nc.scalar.activation(hT[:, i, :], misc[:, :], ACT.Tanh,
                                     bias=cbias[:, i, bass.ds(b, 1)]).then_inc(misc_read, 1)

            def take_first(i, no, b):
                act.wait_ge(misc_ready, no + 1)
                after(act, parts_out, 48 * b)
                nc.scalar.activation(parts[:, 0, i, :], misc[:, :], ACT.Identity,
                                     bias=w["bq" if i < ET else "bk"][:, i % ET:i % ET + 1]).then_inc(first_part, 1)

            def store_shift(no, g, par):
                act.wait_ge(misc_read, no + 1)
                for c in range(SHIFTS):
                    act.dma_start(q[STACK + c:STACK + c + 1, par, g * G:(g + 1) * G, :],
                                  shift[c * G:(c + 1) * G, g % 2, :]).then_inc(shift_in, 16)

            for no, task in enumerate(FIRST):
                if task[0] == "pj":
                    take_first(task[1], no, 0)
                if task[0] == "c1":
                    hidden_layer(task[1], no, 0)
            store_shift(FIRST.index(("mt", 0)), 0, 0)

            def body(kind, b, par):
                for g in range(NG):
                    for jt in range(TT):
                        if (g, jt) == (1, 0):
                            act.wait_ge(z_ready, b + 1)
                            nc.scalar.activation(ez[:, :, :], z[:, :, :], ACT.Exp, scale=-1.0).then_inc(ez_ready, 1)
                        if jt == 2 and not (kind == "last" and g == NG - 1):
                            store_shift(misc_use(kind, b, ("mt", (g + 1) % NG)), (g + 1) % NG,
                                        par if g < NG - 1 else 1 - par)
                        act.wait_ge(slots_free, b * SLOTS + g * TT + jt + 1)
                        for h in range(G):
                            n = (g * TT + jt) * G + h
                            act.wait_ge(b_ready, b * TILES + n + 1)
                            nc.scalar.activation(pr[:, jt, h, :], b_bank[n % RING][:, :], ACT.Exp,
                                                 scale=SCALE).then_inc(b_read, 1)
                        for task in PLAN[g, jt]:
                            if task in kept(kind) and task[0] == "pj":
                                take_first(task[1], misc_use(kind, b, task), b + 1)
                            if task in kept(kind) and task[0] == "c1":
                                hidden_layer(task[1], misc_use(kind, b, task), b + 1)

            batches(act, body)

        @block.vector
        def _(dve):
            def reduce_block(b, at):
                g, it = at // TT, at % TT
                for h in range(G):
                    n = at * G + h
                    dve.wait_ge(a_ready, b * TILES + n + 1)
                    nc.vector.tensor_reduce(mx[:, g % 2, it, h:h + 1], a_bank[n % RING][:, :], X,
                                            ALU.max).then_inc(a_read, 1)

            def split_maxima(step, g):
                dve.wait_ge(a_read, (step + 1) * TT * G)
                m = mx[:, g % 2, :, :]
                nc.vector.tensor_scalar(mxp[:, g % 2, :, 0, :], m, -1.0, None, ALU.mult).then_inc(max_first, 1)
                dve.wait_ge(max_first, step + 1)
                nc.vector.scalar_tensor_tensor(mxp[:, g % 2, :, 1, :], m, -1.0, mxp[:, g % 2, :, 0, :],
                                               ALU.mult, ALU.subtract).then_inc(mx_split, 1)

            def copy_out(step):
                dve.wait_ge(slots_free, (step + 2) * TT)
                nc.vector.tensor_copy(oT[:, :], pv_bank[:, :]).then_inc(out_copied, 1)

            def read_misc(task, no, b, n, par):
                what, i = task
                dve.wait_ge(misc_ready, no + 1)
                if what == "pj":
                    dve.wait_ge(first_part, 4 * (b + 1) + i + 1)
                    after(dve, parts_done, 4 * (b + 1))
                    nc.vector.scalar_tensor_tensor(rest[:, i, :], misc[:, :],
                                                   w["bq" if i < ET else "bk"][:, i % ET:i % ET + 1],
                                                   parts[:, 0, i, :], ALU.add, ALU.subtract).then_inc(misc_read, 1)
                    dve.wait_ge(misc_read, no + 1)
                    nc.vector.tensor_copy(parts[:, 1, i, :], rest[:, i, :]).then_inc(second_part, 1)
                elif what == "v":
                    nc.vector.tensor_tensor(
                        v[:, 1 - par, 2 * i:2 * i + 2, :, 0:HD], misc[:, :].rearrange("p (t h d) -> p t h d", t=2, h=H),
                        w["bv"][:, :].rearrange("p (h d) -> p h d", h=H)[:, None, :, :]
                        .to_broadcast([P, 2, H, HD]), ALU.add).then_inc(misc_read, 1)
                elif what == "mt":
                    if not (isinstance(b, int) and b * NG + (i or NG) < 2):
                        dve.wait_ge(shift_in, 32 * (b * NG + (i or NG) - 1))
                    nc.vector.tensor_copy(shift[:, i % 2, :], turned_shift).then_inc(misc_read, 1)
                elif what == "coh":
                    nc.vector.tensor_tensor(z[:, :, :], misc[:, 0:TT * H].rearrange("p (t h) -> p t h", t=TT),
                                            w["bc2"][:, None, :].to_broadcast([P, TT, H]), ALU.add).then_inc(link, 1)
                    dve.wait_ge(link, n + 1)
                    nc.vector.tensor_scalar(z[:, :, :], z[:, :, :], -88.0, None, ALU.max).then_inc(z_ready, 1)
                    nc.vector.tensor_copy(facur[:, :], fa[:, :, bass.ds(b, 1)].rearrange("p t b -> p (t b)"))\
                        .then_inc(misc_read, 1)
                    return n + 1
                elif what == "vs":
                    nc.vector.tensor_copy(vsum[:, :], misc[:, 0:E]).then_inc(misc_read, 1)
                elif what == "at":
                    nc.vector.tensor_copy(attT[:, i, :], misc[:, :]).then_inc(misc_read, 1)
                elif what == "op":
                    rows = x1[:, bass.ds((b - 1) * TT + 2 * i, 2), :].rearrange("p t e -> p (t e)")
                    nc.vector.tensor_tensor(rows, misc[:, :], rows, ALU.add).then_inc(misc_read, 1)
                elif what == "ot":
                    dve.wait_ge(misc_read, no)
                    dve.wait_ge(link, n)
                    o = misc[:, :].rearrange("p (t h r) -> p t h r", t=TT, h=G)
                    nc.vector.tensor_tensor(div[:, :, :], o[:, :, :, SUM], coh[:, :, i * G:(i + 1) * G],
                                            ALU.mult).then_inc(link, 1)
                    dve.wait_ge(link, n + 1)
                    nc.vector.reciprocal(rdiv[:, :, :], div[:, :, :]).then_inc(link, 1)
                    dve.wait_ge(link, n + 2)
                    dst = att[:, :, i * G * HD:(i + 1) * G * HD].rearrange("p t (h d) -> p t h d", h=G)
                    scaled = nc.vector.tensor_tensor(dst, o[:, :, :, 0:HD],
                                                     rdiv[:, :, :, None].to_broadcast([P, TT, G, HD]), ALU.mult)
                    if i < NG - 1:
                        scaled.then_inc(misc_read, 1)
                        return n + 2
                    scaled.then_inc(link, 1)
                    dve.wait_ge(link, n + 3)
                    for t in range(TT):
                        last = nc.vector.scalar_tensor_tensor(att[:, t, :], vsum[:, :], facur[:, t:t + 1],
                                                              att[:, t, :], ALU.mult, ALU.add)
                    last.then_inc(misc_read, 1)
                    return n + 3
                return n

            dve.wait_ge(cleared, 5)
            for no, task in enumerate(FIRST):
                if task == ("mt", 0):
                    for at in range(TT):
                        reduce_block(0, at)
                    split_maxima(0, 0)
                if task[0] != "c1":
                    read_misc(task, no, -1, 0, 1)
            for at in range(TT, LEAD):
                reduce_block(0, at)

            def links_before(kind, b):
                return 0 if kind == "first" else LINKS - 3 + (b - 1) * LINKS

            def body(kind, b, par):
                n = links_before(kind, b)
                for g in range(NG):
                    for jt in range(TT):
                        if jt == 0 and not (kind == "last" and g == NG - 1):
                            split_maxima(b * NG + g + 1, (g + 1) % NG)
                        lead = lead_block(kind, b, g, jt)
                        if lead is not None:
                            reduce_block(*lead)
                        if (g, jt) == (1, 0):
                            dve.wait_ge(ez_ready, b + 1)
                            nc.vector.tensor_scalar(coh[:, :, :], ez[:, :, :], 1e-8 / KEEP, (1.0 + 1e-8) / KEEP,
                                                    ALU.mult, ALU.add).then_inc(link, 1)
                            n = n + 1
                        tasks = [t if t in kept(kind) else None for t in PLAN[g, jt]] + [None] * 2
                        for i, task in enumerate(tasks[:2]):
                            if task is not None and task[0] != "c1":
                                n = read_misc(task, misc_use(kind, b, task), b, n, par)
                            if i == 0 and jt == 0 and not (kind == "first" and g == 0):
                                copy_out(b * NG + g - 1)

            batches(dve, body)
            copy_out(B * NG - 1)
            n = links_before("last", B)
            for i, task in enumerate(TAIL):
                n = read_misc(task, TAIL_BASE + i, B, n, 0)


def route(nc, banks, dram, w, x1, gbias, wgr, split, top, slots, expert, xs):
    NT = T // P
    CHUNK = 2048
    chunks = []
    for e in range(0, NX, 2):
        chunks += [("w1", e * ET * M)] + [("w2", (e + i) * M // P * M) for i in range(2)] + [("w3", e * M // P * E)]
    with ExitStack() as own:
        def sb(name, shape, dt=F32):
            return own.enter_context(nc.sbuf_tensor(name, shape, dt))

        def sem(name):
            return own.enter_context(nc.semaphore(name))

        loaded = sem("inputs_in")
        raw = sb("raw", [P, 2, CHUNK])
        x1T = sb("x1T", [P, 2, ET, P])
        junk = sb("junk", [P, E])
        ssq = sb("ssq", [P, NT])
        root = sb("root", [P, NT])
        rstd = sb("rstd", [P, NT])
        tmp = sb("tmp", [P, NT])
        gate = sb("gate", [P, NT, NX])
        g2 = sb("g2", [P, NT, NX])
        hot = [sb(f"hot{i}", [P, NT, NX]) for i in range(2)]
        both = sb("both", [P, NT, NX])
        key = sb("key", [P, NT, NX])
        scan = [sb(f"scan{i}", [P, NT, NX]) for i in range(2)]
        tiles = sb("tiles", [P, NX])
        ends = sb("ends", [P, NX])
        itiles = sb("itiles", [P, NX], I32)
        owner = sb("owner", [P, TILES_MAX + 2, NX])
        ones = sb("ones2", [P, P])
        raw_in = [sem(f"raw_in{i}") for i in range(2)]
        hi_done, lo_done = sem("hi_done"), sem("lo_done")
        turned, copied, gated = sem("turned"), sem("copied"), sem("gated")
        squares = sem("squares")
        act_done, pe_done, link = sem("route_act"), sem("route_pe"), sem("route_link")
        ones_set, sorted_, placed, scattered = sem("ones_set"), sem("sorted"), sem("placed"), sem("scattered")
        logits, below, sums = banks[2], banks[3], banks[4]
        block = own.enter_context(nc.Block())

        def column(t, at):
            return t[:, :, :, :].rearrange("p e k n -> p (e k n)")[:, at:at + CHUNK]

        @block.sync
        def _(sp):
            for name in FOR_EXPERTS:
                sp.dma_start(w[name][tuple(slice(None) for _ in INPUTS[name])], dram[name]).then_inc(loaded, 16)
            for n, (name, at) in enumerate(chunks):
                if n >= 2:
                    sp.wait_ge(lo_done, n - 1)
                sp.dma_start(raw[:, n % 2, :], column(dram[name], at)).then_inc(raw_in[n % 2], 16)

        @block.tensor
        def _(pe):
            def gates(t):
                pe.wait_ge(copied, t + 1)
                for e in range(ET):
                    last = nc.tensor.matmul(logits[:, t * NX:(t + 1) * NX], x1T[:, t % 2, e, :], wgr[:, e, :],
                                            start=(e == 0), stop=(e == ET - 1), skip_group_check=True)
                last.then_inc(gated, 1)

            for t in range(NT):
                if t >= 2:
                    pe.wait_ge(copied, t - 1)
                for e in range(ET):
                    last = nc.tensor.transpose(banks[t % 2][:, e * P:(e + 1) * P], x1[:, t, e * P:(e + 1) * P],
                                               w["ident"][:, :])
                last.then_inc(turned, 1)
                if t >= 1:
                    gates(t - 1)
            gates(NT - 1)
            pe.wait_ge(loaded, 16 * len(FOR_EXPERTS))
            pe.wait_ge(ones_set, 1)
            pe.wait_ge(sorted_, 1)
            marks = both[:, :, :].rearrange("p t e -> p (t e)")
            nc.tensor.matmul(below[:, 0:NT * NX], w["tri"][:, :], marks, start=True, stop=True)
            nc.tensor.matmul(sums[:, 0:NT * NX], ones[:, :], marks, start=True, stop=True).then_inc(pe_done, 1)

        @block.scalar
        def _(act):
            def square(t):
                after(act, squares, t)
                nc.scalar.activation(junk[:, :], x1[:, bass.ds(t, 1), :].rearrange("p a f -> p (a f)"),
                                     ACT.Square, accum_out=ssq[:, bass.ds(t, 1)]).then_inc(squares, 1)

            square(0)
            with act.Fori(1, NT) as t:
                square(t)
            act.wait_ge(link, 1)
            nc.scalar.activation(root[:, :], tmp[:, :], ACT.Sqrt).then_inc(act_done, 1)
            act.wait_ge(link, 10)
            nc.scalar.activation(gate[:, :, :], g2[:, :, :], ACT.Exp).then_inc(act_done, 1)
            for n, (name, at) in enumerate(chunks):
                act.wait_ge(raw_in[n % 2], 16 * (n // 2 + 1))
                nc.scalar.activation(column(split[name][0], at), raw[:, n % 2, :], ACT.Copy, scale=WSCALE).then_inc(hi_done, 1)

        @block.vector
        def _(dve):
            n = [0]

            def chain(ins):
                n[0] += 1
                ins.then_inc(link, 1)
                dve.wait_ge(link, n[0])

            def over_experts(a):
                return a[:, :, None].to_broadcast([P, NT, NX])

            def each_expert(a):
                return a[:, None, 0:NX].to_broadcast([P, NT, NX])

            V = nc.vector
            for t in range(NT):
                dve.wait_ge(turned, t + 1)
                if t >= 2:
                    dve.wait_ge(gated, t - 1)
                V.tensor_copy(x1T[:, t % 2, :, :].rearrange("p e n -> p (e n)"), banks[t % 2][:, 0:E]).then_inc(copied, 1)
            dve.wait_ge(squares, NT)
            chain(V.tensor_scalar(tmp[:, :], ssq[:, :], 1.0 / E, 1e-6, ALU.mult, ALU.add))
            dve.wait_ge(act_done, 1)
            chain(V.reciprocal(rstd[:, :], root[:, :]))
            chain(V.tensor_tensor(root[:, :], rstd[:, :], rstd[:, :], ALU.mult))
            chain(V.tensor_tensor(root[:, :], root[:, :], tmp[:, :], ALU.mult))
            chain(V.tensor_scalar(root[:, :], root[:, :], -0.5, 1.5, ALU.mult, ALU.add))
            chain(V.tensor_tensor(rstd[:, :], rstd[:, :], root[:, :], ALU.mult))
            dve.wait_ge(gated, NT)
            chain(V.tensor_tensor(gate[:, :, :], logits[:, 0:NT * NX].rearrange("p (t e) -> p t e", t=NT),
                                  over_experts(rstd), ALU.mult))
            g4 = gate[:, :, :].rearrange("p (b t) e -> p b t e", b=B)
            chain(V.tensor_tensor(g4, g4, gbias[:, :, None, :].to_broadcast([P, B, TT, NX]), ALU.add))
            chain(V.tensor_reduce(tmp[:, :], gate[:, :, :], X, ALU.max))
            chain(V.tensor_tensor(g2[:, :, :], gate[:, :, :], over_experts(tmp), ALU.subtract))
            dve.wait_ge(act_done, 2)
            chain(V.reduce_sum(tmp[:, :], gate[:, :, :], axis=X))
            chain(V.reciprocal(root[:, :], tmp[:, :]))
            chain(V.tensor_tensor(gate[:, :, :], gate[:, :, :], over_experts(root), ALU.mult))
            dve.wait_ge(loaded, 16 * len(FOR_EXPERTS))
            src = gate
            for i in range(2):
                chain(V.tensor_reduce(top[:, i, :], src[:, :, :], X, ALU.max))
                chain(V.tensor_tensor(key[:, :, :], src[:, :, :], over_experts(top[:, i, :]), ALU.is_lt))
                chain(V.scalar_tensor_tensor(key[:, :, :], key[:, :, :], float(NX), each_expert(w["count"]),
                                             ALU.mult, ALU.add))
                chain(V.tensor_reduce(tmp[:, :], key[:, :, :], X, ALU.min))
                chain(V.tensor_tensor(hot[i][:, :, :], each_expert(w["count"]), over_experts(tmp), ALU.is_equal))
                if i == 0:
                    chain(V.scalar_tensor_tensor(g2[:, :, :], hot[0][:, :, :], -2.0, gate[:, :, :], ALU.mult, ALU.add))
                    src = g2
            V.tensor_tensor(both[:, :, :], hot[0][:, :, :], hot[1][:, :, :], ALU.add).then_inc(sorted_, 1)
            dve.wait_ge(pe_done, 1)
            per_tile = sums[:, 0:NT * NX].rearrange("p (t e) -> p t e", t=NT)
            chain(V.tensor_copy(scan[0][:, :, :], per_tile))
            cur, step = 0, 1
            while step < NT:
                a, b = scan[cur], scan[1 - cur]
                V.tensor_copy(b[:, 0:step, :], a[:, 0:step, :])
                chain(V.tensor_tensor(b[:, step:, :], a[:, step:, :], a[:, 0:NT - step, :], ALU.add))
                cur, step = 1 - cur, 2 * step
            upto = scan[cur]
            chain(V.tensor_scalar(itiles[:, :], upto[:, NT - 1, :], float(TS - 1), None, ALU.add))
            chain(V.tensor_scalar(itiles[:, :], itiles[:, :], TS.bit_length() - 1, None, ALU.arith_shift_right))
            chain(V.tensor_copy(tiles[:, :], itiles[:, :]))
            chain(V.tensor_scalar(tiles[:, :], tiles[:, :], 1.0, None, ALU.max))
            chain(V.tensor_copy(ends[:, :], tiles[:, :]))
            for e in range(1, NX):
                chain(V.tensor_tensor(ends[:, e:e + 1], ends[:, e:e + 1], ends[:, e - 1:e], ALU.add))
            NO = TILES_MAX + 2
            chain(V.tensor_tensor(owner[:, :, :], ends[:, None, :].to_broadcast([P, NO, NX]),
                                  w["count"][:, :, None].to_broadcast([P, NO, NX]), ALU.is_le))
            chain(V.reduce_sum(w["count"][:, :], owner[:, :, :], axis=X))
            chain(V.tensor_scalar(expert[:, :], w["count"][:, :], float(NX - 1), None, ALU.min))
            chain(V.tensor_tensor(tiles[:, :], ends[:, :], tiles[:, :], ALU.subtract))
            chain(V.tensor_scalar(tiles[:, :], tiles[:, :], float(TS), None, ALU.mult))
            row = scan[1 - cur]
            chain(V.tensor_tensor(row[:, :, :], upto[:, :, :], per_tile, ALU.subtract))
            chain(V.tensor_tensor(row[:, :, :], row[:, :, :], below[:, 0:NT * NX].rearrange("p (t e) -> p t e", t=NT),
                                  ALU.add))
            chain(V.tensor_tensor(row[:, :, :], row[:, :, :], each_expert(tiles), ALU.add))
            for i in range(2):
                chain(V.tensor_tensor(key[:, :, :], hot[i][:, :, :], row[:, :, :], ALU.mult))
                chain(V.reduce_sum(tmp[:, :], key[:, :, :], axis=X))
                V.tensor_copy(slots[:, i, :], tmp[:, :]).then_inc(placed, 1)
                dve.wait_ge(placed, i + 1)
            for m, (name, at) in enumerate(chunks):
                dve.wait_ge(hi_done, m + 1)
                V.scalar_tensor_tensor(column(split[name][1], at), raw[:, m % 2, :], WSCALE, column(split[name][0], at),
                                       ALU.mult, ALU.subtract).then_inc(lo_done, 1)

        @block.gpsimd
        def _(pool):
            nc.gpsimd.memset(ones[:, :], 1.0).then_inc(ones_set, 1)
            pool.wait_ge(placed, 2)
            for i in range(2):
                for t in range(NT):
                    pool.indirect_dma_start(out=xs, out_offset=bass.IndirectOffsetOnAxis(ap=slots[:, i, t:t + 1], axis=0),
                                            in_=x1[:, t, :], in_offset=None).then_inc(scattered, 16)
            pool.wait_ge(scattered, 16 * 2 * NT)


def experts(nc, banks, w, split, expert, xs, ys):
    MT = M // P
    SUB = TS // P
    with ExitStack() as own:
        def sb(name, shape, dt=F32):
            return own.enter_context(nc.sbuf_tensor(name, shape, dt))

        def sem(name):
            return own.enter_context(nc.semaphore(name))

        x = sb("x_tile", [P, SUB, E])
        xh, xl = sb("xh", [P, ET, TS], F16), sb("xl", [P, ET, TS], F16)
        hf = [sb(f"hf{i}", [P, MT, TS]) for i in range(2)]
        hh = [sb(f"hh{i}", [P, MT, TS], F16) for i in range(2)]
        hl = [sb(f"hl{i}", [P, MT, TS], F16) for i in range(2)]
        y = sb("y", [P, SUB, E])
        x_in, turned, x_hi, x_lo = sem("xt_in"), sem("xt_turned"), sem("x_hi"), sem("x_lo")
        made = [sem(f"layer{i}") for i in range(3)]
        full = [sem(f"full{i}") for i in range(2)]
        hi = [sem(f"hi{i}") for i in range(2)]
        lo = [sem(f"lo{i}") for i in range(2)]
        y_done, y_out = sem("y_done"), sem("y_out")
        layer = [banks[0:2], banks[2:4]]
        y_bank, t_bank = banks[4], banks[5]
        bias = [w["b1"], w["b2"]]
        block = own.enter_context(nc.Block())

        def turns(engine, body):
            body(0)
            with engine.Fori(1, TILES_MAX) as i:
                body(i)

        @block.sync
        def _(sp):
            def load(i):
                sp.dma_start(x[:, :, :], xs[bass.ds(i * TS, TS), :].rearrange("(s p) e -> p s e", p=P)).then_inc(x_in, 16)

            load(0)
            sp.wait_ge(turned, 1)
            load(1)

            def body(i):
                sp.wait_ge(turned, i + 2)
                load(i + 2)
                sp.wait_ge(y_done, i + 1)
                sp.dma_start(ys[bass.ds(i * TS, TS), :].rearrange("(s p) e -> p s e", p=P), y[:, :, :]).then_inc(y_out, 16)

            turns(sp, body)
            sp.wait_ge(y_out, 16 * TILES_MAX)

        @block.tensor
        def _(pe):
            def turn(i):
                pe.wait_ge(x_in, (i + 1) * 16)
                after(pe, x_lo, i)
                for e in range(ET):
                    for s in range(SUB):
                        last = nc.tensor.transpose(t_bank[:, (e * SUB + s) * P:(e * SUB + s + 1) * P],
                                                   x[:, s, e * P:(e + 1) * P], w["ident"][:, :])
                last.then_inc(turned, 1)

            def weights(name, part, e, k, cols):
                return split[name][part][:, bass.ds(e, 1), k, cols].rearrange("p a n -> p (a n)")

            def hidden(which, i, e):
                name, K = ("w1", ET) if which == 0 else ("w2", MT)
                ah, al = (xh, xl) if which == 0 else (hh[0], hl[0])
                if which == 0:
                    pe.wait_ge(x_lo, i + 1)
                for m in range(MT):
                    if m % 2 == 0 and not (isinstance(i, int) and i == 0):
                        pe.wait_ge(full[which], (i - 1) * MT + m + 2)
                    out = layer[which][m // 2][:, m % 2 * TS:(m % 2 + 1) * TS]
                    c = slice(m * P, (m + 1) * P)
                    for k in range(K):
                        if which == 1 and m == 0:
                            pe.wait_ge(lo[0], i * MT + k + 1)
                        for a, part in ((ah, 0), (ah, 1), (al, 0)):
                            last = nc.tensor.matmul(out, weights(name, part, e, k, c), a[:, k, :],
                                                    start=(k == 0 and a is ah and part == 0),
                                                    stop=(k == K - 1 and a is al), skip_group_check=True)
                    last.then_inc(made[which], 1)

            def final(i, e):
                after(pe, y_done, i)
                for s in range(SUB):
                    r = slice(s * P, (s + 1) * P)
                    for k in range(MT):
                        if s == 0:
                            pe.wait_ge(lo[1], i * MT + k + 1)
                        for a, part in ((hh[1], 0), (hh[1], 1), (hl[1], 0)):
                            last = nc.tensor.matmul(y_bank[:, s * E:(s + 1) * E], a[:, k, r],
                                                    weights("w3", part, e, k, slice(0, E)),
                                                    start=(k == 0 and a is hh[1] and part == 0),
                                                    stop=(k == MT - 1 and a is hl[1]), skip_group_check=True)
                last.then_inc(made[2], 1)

            def expert_of(i):
                return pe.value_load(expert[0:1, bass.ds(i, 1)], min_val=0, max_val=NX - 1)

            turn(0)
            hidden(0, 0, expert_of(0))
            turn(1)

            def body(i):
                e = expert_of(i)
                e_next = expert_of(i + 1)
                hidden(1, i, e)
                hidden(0, i + 1, e_next)
                turn(i + 2)
                final(i, e)

            turns(pe, body)

        @block.scalar
        def _(act):
            def take_turned(i):
                act.wait_ge(turned, i + 1)
                after(act, made[0], i * MT)
                nc.scalar.activation(xh[:, :, :].rearrange("p e n -> p (e n)"), t_bank[:, :], ACT.Copy).then_inc(x_hi, 1)

            def take_hidden(which, i):
                e = act.value_load(expert[0:1, bass.ds(i, 1)], min_val=0, max_val=NX - 1)
                for m in range(MT):
                    act.wait_ge(made[which], i * MT + m // 2 * 2 + 2)
                    after(act, lo[which], i * MT)
                    nc.scalar.activation(hf[which][:, m, :], layer[which][m // 2][:, m % 2 * TS:(m % 2 + 1) * TS],
                                         ACT.Relu, bias=bias[which][:, bass.ds(e, 1), m], scale=1.0 / WSCALE)\
                        .then_inc(full[which], 1)

            take_turned(0)
            take_hidden(0, 0)
            take_turned(1)

            def body(i):
                take_hidden(1, i)
                take_hidden(0, i + 1)
                take_turned(i + 2)

            turns(act, body)

        @block.vector
        def _(dve):
            def take_turned(i):
                dve.wait_ge(x_hi, i + 1)
                nc.vector.tensor_tensor(xl[:, :, :].rearrange("p e n -> p (e n)"), t_bank[:, :],
                                        xh[:, :, :].rearrange("p e n -> p (e n)"), ALU.subtract).then_inc(x_lo, 1)

            def take_hidden(which, i):
                for m in range(MT):
                    dve.wait_ge(full[which], i * MT + m + 1)
                    if m == 0:
                        after(dve, made[which + 1], i * (MT if which == 0 else 1))
                    nc.vector.tensor_copy(hh[which][:, m, :], hf[which][:, m, :]).then_inc(hi[which], 1)

            def take_final(i):
                e = dve.value_load(expert[0:1, bass.ds(i, 1)], min_val=0, max_val=NX - 1)
                dve.wait_ge(made[2], i + 1)
                after(dve, y_out, i * 16)
                for s in range(SUB):
                    last = nc.vector.scalar_tensor_tensor(y[:, s, :], y_bank[:, s * E:(s + 1) * E], 1.0 / WSCALE,
                                                          w["b3"][:, bass.ds(e, 1), :].rearrange("p a n -> p (a n)"),
                                                          ALU.mult, ALU.add)
                last.then_inc(y_done, 1)

            take_turned(0)
            take_hidden(0, 0)
            take_turned(1)

            def body(i):
                take_hidden(1, i)
                take_hidden(0, i + 1)
                take_turned(i + 2)
                take_final(i)

            turns(dve, body)

        @block.gpsimd
        def _(pool):
            def take_hidden(which, i):
                for m in range(MT):
                    pool.wait_ge(hi[which], i * MT + m + 1)
                    nc.gpsimd.tensor_tensor(hl[which][:, m, :], hf[which][:, m, :], hh[which][:, m, :],
                                            ALU.subtract).then_inc(lo[which], 1)

            take_hidden(0, 0)

            def body(i):
                take_hidden(1, i)
                take_hidden(0, i + 1)

            turns(pool, body)


def combine(nc, x1, top, slots, ys, out):
    NT, RINGS = T // P, 4
    with ExitStack() as own:
        def sem(name):
            return own.enter_context(nc.semaphore(name))

        g = own.enter_context(nc.sbuf_tensor("g", [P, 2, RINGS, E], F32))
        part = own.enter_context(nc.sbuf_tensor("part", [P, RINGS, E], F32))
        gathered = [sem(f"gathered{i}") for i in range(RINGS)]
        half, added, stored = sem("half"), sem("added"), sem("stored")
        block = own.enter_context(nc.Block())

        @block.gpsimd
        def _(pool):
            for t in range(NT):
                if t >= RINGS:
                    pool.wait_ge(added, t - RINGS + 1)
                for i in range(2):
                    pool.indirect_dma_start(out=g[:, i, t % RINGS, :], out_offset=None, in_=ys,
                                            in_offset=bass.IndirectOffsetOnAxis(ap=slots[:, i, t:t + 1], axis=0))\
                        .then_inc(gathered[t % RINGS], 16)

        @block.vector
        def _(dve):
            for t in range(NT):
                dve.wait_ge(gathered[t % RINGS], 32 * (t // RINGS + 1))
                nc.vector.scalar_tensor_tensor(part[:, t % RINGS, :], g[:, 0, t % RINGS, :], top[:, 0, t:t + 1],
                                               x1[:, t, :], ALU.mult, ALU.add).then_inc(half, 1)
                dve.wait_ge(half, t + 1)
                nc.vector.scalar_tensor_tensor(x1[:, t, :], g[:, 1, t % RINGS, :], top[:, 1, t:t + 1],
                                               part[:, t % RINGS, :], ALU.mult, ALU.add).then_inc(added, 1)

        @block.sync
        def _(sp):
            for c in range(NT // TT):
                sp.wait_ge(added, (c + 1) * TT)
                sp.dma_start(out[:, c * TT:(c + 1) * TT, :], x1[:, c * TT:(c + 1) * TT, :]).then_inc(stored, 16)
            sp.wait_ge(stored, 16 * (NT // TT))


def kernel(**inputs):
    import concourse.bacc as bacc
    from concourse.bass_utils import run_bass_kernel_spmd

    arrays = {n: np.ascontiguousarray(a) for n, a in layout(inputs).items()}
    nc = bacc.Bacc("TRN2", target_bir_lowering=False, num_devices=1)
    dram = {}
    for n, shape in INPUTS.items():
        assert list(arrays[n].shape) == shape, n
        dram[n] = nc.dram_tensor("in_" + n, shape, F32, kind="ExternalInput").ap()
    out = nc.dram_tensor("out", OUT, F32, kind="ExternalOutput").ap()
    program(nc, dram, out)
    result = run_bass_kernel_spmd(nc, [{"in_" + n: arrays[n] for n in INPUTS}], core_ids=[0])
    return finish(result.results[0]["out"])


def layout(i):
    def cols(a):
        return np.asarray(a).reshape(-1, P).T

    def rows(a):
        a = np.asarray(a)
        return a.reshape(-1, P, a.shape[-1]).transpose(1, 0, 2)

    def rep(a, n=P):
        return np.broadcast_to(np.asarray(a), (n, np.asarray(a).shape[-1]))

    x = np.asarray(i["x"]).reshape(T, E)
    wqkv, bqkv = np.asarray(i["L0_cond_Wqkv"]), np.asarray(i["L0_cond_bqkv"])
    wc1 = np.asarray(i["L0_cond_Wc1"])
    rate = np.float32(10000.0) ** np.repeat(np.arange(0, E, 2, dtype=np.float32) / np.float32(E), 2)
    pe = np.sin(np.arange(S, dtype=np.float32)[:, None] / rate[None, :]).astype(np.float32)
    return {
        "xT": rows(x.T), "x": x.reshape(T // P, P, E).transpose(1, 0, 2),
        "wq": rows(wqkv[0:E].T), "wk": rows(wqkv[E:2 * E].T), "bq": cols(bqkv[0:E]), "bk": cols(bqkv[E:2 * E]),
        "wv": rows(wqkv[2 * E:].T), "bv": rep(bqkv[2 * E:]),
        "wo": rows(np.asarray(i["L0_cond_Wout"]).T), "bo": rep(i["L0_cond_bout"]),
        "wc1x": rows(wc1[:, 0:E].T), "wc1c": wc1[:, E:].T, "bc1": cols(i["L0_cond_bc1"]),
        "wc2": rows(np.asarray(i["L0_cond_Wc2"]).T), "bc2": rep(i["L0_cond_bc2"]),
        "cT": np.asarray(i["cond_256"]).T, "we1": np.asarray(i["L0_cond_We1"]).T, "be1": cols(i["L0_cond_be1"]),
        "we2": rows(np.asarray(i["L0_cond_We2"]).T), "be2": rep(i["L0_cond_be2"], B),
        "ln_g": rep(i["L0_cond_ln_g"], B), "ln_b": rep(i["L0_cond_ln_b"], B),
        "pe": rows(pe.T), "ident": np.eye(P, dtype=np.float32),
        "rms_w": cols(i["L1_cond_rms_w"]), "wg": rows(i["L1_cond_wg_W"]),
        "gate_b": np.stack([rep(i["L1_cond_wg_b"]), rep(i["L1_cond_gg_b"])], 1), "gg": np.asarray(i["L1_cond_gg_W"]),
        "w1": np.asarray(i["L1_cond_W1"]).reshape(NX, ET, P, M).transpose(2, 0, 1, 3),
        "b1": np.asarray(i["L1_cond_b1"]).reshape(NX, M // P, P).transpose(2, 0, 1),
        "w2": np.asarray(i["L1_cond_W2"]).reshape(NX, M // P, P, M).transpose(2, 0, 1, 3),
        "b2": np.asarray(i["L1_cond_b2"]).reshape(NX, M // P, P).transpose(2, 0, 1),
        "w3": np.asarray(i["L1_cond_W3"]).reshape(NX, M // P, P, E).transpose(2, 0, 1, 3),
        "b3": np.broadcast_to(np.asarray(i["L1_cond_b3"])[None], (P, NX, E)),
        "tri": np.triu(np.ones((P, P), np.float32), 1),
        "count": np.broadcast_to(np.arange(TILES_MAX + 2, dtype=np.float32), (P, TILES_MAX + 2)),
    }


OUT = [P, T // P, E]


def finish(out):
    return np.asarray(out).transpose(1, 0, 2).reshape(B, S, E)
```

```python
from contextlib import ExitStack

import numpy as np

import concourse.bass as bass
from concourse import mybir

P = 128
B, S, E = 8, 512, 256
H, HD = 16, 16
CD = 64
NX, M = 8, 512
T = B * S
ET = E // P
TT = S // P
G = 4
NG = H // G
HW = 32
SUM = HD
Q_PARTS = (0, 1, 2, 0, 1, 0)
K_PARTS = (0, 0, 0, 1, 1, 2)
STACK = HD * len(Q_PARTS)
SHIFTS = 2
COUPLING = 0.3 * 0.7
KEEP = 1.0 - COUPLING
SCALE = 1.0 / float(HD) ** 0.5
RING = 3

TS = 256
TILES_MAX = 2 * T // TS + NX - 1
CAP = T + TS
WEIGHTS = (ET + M // P) * M + M // P * E
LAYERS = {"w1": (0, M), "w2": (ET * M, M), "w3": ((ET + M // P) * M, E)}
HALF = WEIGHTS // 2
QUARTER = WEIGHTS // 4
HELD = 6
WSCALE = 16.0

F32 = mybir.dt.float32
F16 = mybir.dt.float16
BF16 = mybir.dt.bfloat16
I32 = mybir.dt.int32
F32R = mybir.dt.float32r
ALU = mybir.AluOpType
ACT = mybir.ActivationFunctionType
X = mybir.AxisListType.X

INPUTS = {
    "xT": [P, ET, T], "x": [P, T // P, E],
    "wq": [P, ET, E], "wk": [P, ET, E], "bq": [P, ET], "bk": [P, ET],
    "wv": [P, ET, E], "bv": [P, E], "wo": [P, ET, E], "bo": [P, E],
    "wc1x": [P, ET, E], "wc1c": [CD, E], "bc1": [P, ET], "wc2": [P, ET, H], "bc2": [P, H],
    "cT": [CD, B], "we1": [CD, E], "be1": [P, ET], "we2": [P, ET, E], "be2": [B, E],
    "ln_g": [B, E], "ln_b": [B, E], "pe": [P, ET, S], "ident": [P, P],
    "rms_w": [P, ET], "wg": [P, ET, NX], "gate_b": [P, 2, NX], "gg": [CD, NX],
    "we": [P, NX, WEIGHTS], "b1": [P, NX, M // P], "b2": [P, NX, M // P], "b3": [P, NX, E],
    "tri": [P, P], "count": [P, TILES_MAX + 2],
    "dest": [P, 2 * T // P + TS // P],
}


FOR_SETUP = ("wc1c", "bc1", "cT", "we1", "be1", "we2", "be2", "ln_g", "ln_b", "pe", "rms_w", "wg", "gate_b", "gg")
FOR_ATTENTION = ("wq", "wk", "bq", "bk", "wv", "bv", "wo", "bo", "wc1x", "wc2", "bc2")
FOR_EXPERTS = ("b1", "b2", "b3")


def program(nc, dram, out):
    with ExitStack() as ctx:
        def sb(name, shape, dt=F32):
            return ctx.enter_context(nc.sbuf_tensor(name, shape, dt))

        banks = [ctx.enter_context(nc.psum_tensor(f"bank{i}", [P, 512], F32)) for i in range(8)]
        w = {n: sb("w_" + n, INPUTS[n]) for n in ("ident", "tri", "count", "dest")}
        gbias = sb("gbias", [P, B, NX])
        wgr = sb("wgr", [P, ET, NX])
        routing = {
            "rows": sb("batch_rows", [P, TT, E]),
            "slot": sb("slot", [P, 2, TT], I32),
            "tag": sb("tag", [P, 2, TT, 2]),
            "dest": sb("dest_rows", [P, 2 * T // P + TS // P], I32),
            "start": sb("start", [P, NX]),
            "region": sb("region", [P, NX]),
        }
        xs = nc.dram_tensor("xs", [NX * CAP + TS, E], F32).ap()
        tags = nc.dram_tensor("tags", [NX * CAP + TS, 2], F32).ap()
        shares = nc.dram_tensor("shares", [2 * T + TS, E], F32).ap()
        parts_dram = nc.dram_tensor("parts_dram", [3, 2 * E, S], BF16).ap()
        x1_dram = nc.dram_tensor("x1_dram", [P, T // P, E], F32).ap()

        with ExitStack() as own:
            def mine(name, shape, dt=F32):
                return own.enter_context(nc.sbuf_tensor(name, shape, dt))

            x1 = mine("x1", [P, T // P, E])
            stacks = {
                "xT": mine("xT", [P, 2, ET, S]),
                "parts": mine("parts", [P, 3, 2 * ET, S], BF16),
                "rest": mine("rest", [P, 2 * ET, S]),
                "q": mine("q", [P, 2, H, S], BF16),
                "k": mine("k", [P, 2, H, S], BF16),
                "dram": parts_dram,
            }
            for n in ("x_in0", "x_in1",
                      "first_part", "second_part", "parts_done",
                      "parts_out",
                      "stack_in"):
                stacks[n] = own.enter_context(nc.semaphore(n))
            for n in FOR_ATTENTION:
                w[n] = own.enter_context(nc.sbuf_tensor("w_" + n, INPUTS[n], F32))
            fa = own.enter_context(nc.sbuf_tensor("fa", [P, TT, B], F32))
            cbias = own.enter_context(nc.sbuf_tensor("cbias", [P, ET, B], F32))
            setup(nc, dram, banks, w, stacks, fa, cbias, gbias, wgr)
            attention(nc, banks, dram, w, x1, stacks, fa, cbias, gbias, wgr, routing, xs, tags, x1_dram)
        x1_again = sb("x1_again", [P, HELD * TT, E])
        with ExitStack() as own:
            def mine(name, shape, dt=F32):
                return own.enter_context(nc.sbuf_tensor(name, shape, dt))

            for n in FOR_EXPERTS:
                w[n] = mine("w_" + n, INPUTS[n])
            split = (mine("w_hi", INPUTS["we"], F16), mine("w_lo", INPUTS["we"], F16))
            raw = mine("raw", [P, 2, HALF])
            expert = mine("expert", [P, TILES_MAX + 2], I32)
            first_row = mine("first_row", [P, TILES_MAX + 2], I32)
            streams = {n: own.enter_context(nc.semaphore(n)) for n in ("raw_half0", "raw_half1", "split_hi", "split_lo")}
            route(nc, dram, w, routing, raw, split, streams, expert, first_row, xs, tags)
            experts(nc, banks, dram, w, raw, split, streams, expert, first_row, xs, tags, shares, x1_dram, x1_again)
        combine(nc, x1_dram, x1_again, shares, out)


FOR_PROJECTIONS = ("wq", "wk", "bq", "bk")


def make_stacks(sp, stacks, b, par):
    sp.wait_ge(stacks["parts_done"], 4 * b + 4)
    for c in range(3):
        sp.dma_start(stacks["dram"][c].rearrange("(i p) n -> p i n", p=P), stacks["parts"][:, c, :, :])\
            .then_inc(stacks["parts_out"], 16)
    sp.wait_ge(stacks["parts_out"], 48 * b + 48)
    for j in range(len(Q_PARTS)):
        rows = slice(j * HD, (j + 1) * HD)
        for stack, c, first in (("q", Q_PARTS[j], 0), ("k", K_PARTS[j], E)):
            sp.dma_start(stacks[stack][rows, par, :, :], stacks["dram"][c][first:first + E, :]
                         .rearrange("(h d) n -> d h n", d=HD)).then_inc(stacks["stack_in"], 16)


def setup(nc, dram, banks, w, stacks, fa, cbias, gbias, wgr):
    with ExitStack() as own:
        def sb(name, shape, dt=F32):
            return own.enter_context(nc.sbuf_tensor(name, shape, dt))

        loaded = own.enter_context(nc.semaphore("loaded"))
        weights_in = own.enter_context(nc.semaphore("weights_in"))
        projected = own.enter_context(nc.semaphore("projected"))
        rest_set = own.enter_context(nc.semaphore("rest_set"))
        xT, parts, rest = (stacks[n] for n in ("xT", "parts", "rest"))
        pe_done = own.enter_context(nc.semaphore("setup_pe"))
        dve_done = own.enter_context(nc.semaphore("setup_dve"))
        act_done = own.enter_context(nc.semaphore("setup_act"))
        w = dict(w, **{n: sb("w_" + n, INPUTS[n]) for n in FOR_SETUP})
        others = [n for n in w if n not in FOR_PROJECTIONS]
        crep = sb("crep", [CD, B, P])
        e1 = sb("e1", [P, ET, B])
        fp = sb("fp", [B, E])
        sq = sb("sq", [B, E])
        fpT = sb("fpT", [P, ET, B])
        lg = sb("lg", [B, S])
        st = sb("st", [B, 8])
        block = own.enter_context(nc.Block())

        @block.sync
        def _(sp):
            sp.dma_start(xT[:, 0, :, :], dram["xT"][:, :, 0:S]).then_inc(stacks["x_in0"], 16)
            for n in FOR_PROJECTIONS:
                sp.dma_start(w[n][tuple(slice(None) for _ in w[n].shape)], dram[n]).then_inc(weights_in, 16)
            for n in others:
                sp.dma_start(w[n][tuple(slice(None) for _ in w[n].shape)], dram[n]).then_inc(loaded, 16)
            sp.dma_start(xT[:, 1, :, :], dram["xT"][:, :, S:2 * S]).then_inc(stacks["x_in1"], 16)
            make_stacks(sp, stacks, 0, 0)

        @block.gpsimd
        def _(pool):
            for i in range(2 * ET):
                pool.wait_ge(stacks["second_part"], i + 1)
                nc.gpsimd.tensor_tensor(parts[:, 2, i, :], rest[:, i, :], parts[:, 1, i, :],
                                        ALU.subtract).then_inc(stacks["parts_done"], 1)

        @block.tensor
        def _(pe):
            pe.wait_ge(weights_in, 16 * len(FOR_PROJECTIONS))
            pe.wait_ge(stacks["x_in0"], 16)
            for i in range(2 * ET):
                wt, f = w["wq" if i < ET else "wk"], i % ET
                for e in range(ET):
                    last = nc.tensor.matmul(banks[4 + i][:, :], wt[:, e, f * P:(f + 1) * P], xT[:, 0, e, :],
                                            start=(e == 0), stop=(e == ET - 1))
                last.then_inc(projected, 1)
            pe.wait_ge(loaded, 16 * len(others))
            for m in range(ET):
                nc.tensor.matmul(banks[0][:, m * B:(m + 1) * B], w["we1"][:, m * P:(m + 1) * P], w["cT"][:, :],
                                 start=(m == 0), stop=True, skip_group_check=True)
                nc.tensor.matmul(banks[2][:, m * B:(m + 1) * B], w["wc1c"][:, m * P:(m + 1) * P], w["cT"][:, :],
                                 start=(m == 0), stop=True, skip_group_check=True).then_inc(pe_done, 1)
            pe.wait_ge(dve_done, 1)
            for b in range(B):
                last = nc.tensor.matmul(banks[3][:, b * NX:(b + 1) * NX], crep[:, b, :], w["gg"][:, :],
                                        start=(b == 0), stop=True, skip_group_check=True)
            last.then_inc(pe_done, 1)
            pe.wait_ge(act_done, 2)
            for k in range(ET):
                last = nc.tensor.matmul(banks[0][0:B, 0:E], e1[:, k, :], w["we2"][:, k, :], start=(k == 0), stop=(k == ET - 1))
            last.then_inc(pe_done, 1)
            pe.wait_ge(dve_done, 18)
            for k in range(ET):
                last = nc.tensor.transpose(banks[1][:, k * B:(k + 1) * B], fp[:, k * P:(k + 1) * P], w["ident"][0:B, 0:B])
            last.then_inc(pe_done, 1)
            pe.wait_ge(dve_done, 19)
            for k in range(ET):
                last = nc.tensor.matmul(banks[2][0:B, :], fpT[:, k, :], w["pe"][:, k, :], start=(k == 0), stop=(k == ET - 1))
            last.then_inc(pe_done, 1)
            pe.wait_ge(dve_done, 22)
            for t in range(TT):
                last = nc.tensor.transpose(banks[3][:, t * B:(t + 1) * B], lg[:, t * P:(t + 1) * P], w["ident"][0:B, 0:B])
            last.then_inc(pe_done, 1)

        @block.scalar
        def _(act):
            for i in range(2 * ET):
                act.wait_ge(projected, i + 1)
                nc.scalar.activation(parts[:, 0, i, :], banks[4 + i][:, :], ACT.Identity,
                                     bias=w["bq" if i < ET else "bk"][:, i % ET:i % ET + 1]).then_inc(stacks["first_part"], 1)
            act.wait_ge(loaded, 16 * len(others))
            act.wait_ge(pe_done, 2)
            for m in range(ET):
                nc.scalar.activation(e1[:, m, :], banks[0][:, m * B:(m + 1) * B], ACT.Relu,
                                     bias=w["be1"][:, m:m + 1]).then_inc(act_done, 1)
            for m in range(ET):
                nc.scalar.activation(cbias[:, m, :], banks[2][:, m * B:(m + 1) * B], ACT.Identity,
                                     bias=w["bc1"][:, m:m + 1])
            act.wait_ge(dve_done, 11)
            nc.scalar.activation(st[:, 7:8], st[:, 3:4], ACT.Sqrt).then_inc(act_done, 1)
            act.wait_ge(dve_done, 20)
            nc.scalar.activation(lg[:, :], banks[2][0:B, :], ACT.Exp, bias=st[:, 5:6],
                                 accum_out=st[:, 6:7]).then_inc(act_done, 1)

        @block.vector
        def _(dve):
            n = [0]

            def chain(ins):
                n[0] += 1
                ins.then_inc(dve_done, 1)
                dve.wait_ge(dve_done, n[0])

            for i in range(2 * ET):
                dve.wait_ge(stacks["first_part"], i + 1)
                nc.vector.scalar_tensor_tensor(rest[:, i, :], banks[4 + i][:, :],
                                               w["bq" if i < ET else "bk"][:, i % ET:i % ET + 1],
                                               parts[:, 0, i, :], ALU.add, ALU.subtract).then_inc(rest_set, 1)
                dve.wait_ge(rest_set, i + 1)
                nc.vector.tensor_copy(parts[:, 1, i, :], rest[:, i, :]).then_inc(stacks["second_part"], 1)
            dve.wait_ge(loaded, 16 * len(others))
            chain(nc.vector.tensor_copy(crep[:, :, :], w["cT"][:, :, None].to_broadcast([CD, B, P])))
            for k in range(ET):
                last = nc.vector.tensor_scalar(wgr[:, k, :], w["wg"][:, k, :], w["rms_w"][:, k:k + 1], None, ALU.mult)
            chain(last)
            dve.wait_ge(pe_done, 3)
            gb = gbias[:, :, :]
            chain(nc.vector.tensor_tensor(gb, banks[3][:, 0:B * NX].rearrange("p (b e) -> p b e", b=B),
                                          w["gate_b"][:, 0:1, :].to_broadcast([P, B, NX]), ALU.add))
            chain(nc.vector.tensor_tensor(gb, gb, w["gate_b"][:, 1:2, :].to_broadcast([P, B, NX]), ALU.add))
            dve.wait_ge(pe_done, 4)
            chain(nc.vector.tensor_tensor(fp[:, :], banks[0][0:B, 0:E], w["be2"][:, :], ALU.add))
            chain(nc.vector.reduce_sum(st[:, 0:1], fp[:, :], axis=X))
            chain(nc.vector.tensor_scalar(st[:, 1:2], st[:, 0:1], 1.0 / E, None, ALU.mult))
            chain(nc.vector.tensor_scalar(fp[:, :], fp[:, :], st[:, 1:2], None, ALU.subtract))
            chain(nc.vector.tensor_tensor(sq[:, :], fp[:, :], fp[:, :], ALU.mult))
            chain(nc.vector.reduce_sum(st[:, 2:3], sq[:, :], axis=X))
            chain(nc.vector.tensor_scalar(st[:, 3:4], st[:, 2:3], 1.0 / E, 1e-5, ALU.mult, ALU.add))
            dve.wait_ge(act_done, 3)
            chain(nc.vector.reciprocal(st[:, 4:5], st[:, 7:8]))
            chain(nc.vector.tensor_tensor(st[:, 6:7], st[:, 4:5], st[:, 4:5], ALU.mult))
            chain(nc.vector.tensor_tensor(st[:, 6:7], st[:, 6:7], st[:, 3:4], ALU.mult))
            chain(nc.vector.tensor_scalar(st[:, 6:7], st[:, 6:7], -0.5, 1.5, ALU.mult, ALU.add))
            chain(nc.vector.tensor_tensor(st[:, 4:5], st[:, 4:5], st[:, 6:7], ALU.mult))
            chain(nc.vector.scalar_tensor_tensor(fp[:, :], fp[:, :], st[:, 4:5], w["ln_g"][:, :],
                                                 ALU.mult, ALU.mult))
            chain(nc.vector.tensor_tensor(fp[:, :], fp[:, :], w["ln_b"][:, :], ALU.add))
            dve.wait_ge(pe_done, 5)
            chain(nc.vector.tensor_copy(fpT[:, :, :], banks[1][:, 0:ET * B].rearrange("p (k b) -> p k b", k=ET)))
            dve.wait_ge(pe_done, 6)
            chain(nc.vector.tensor_reduce(st[:, 5:6], banks[2][0:B, :], X, ALU.max, negate=True))
            dve.wait_ge(act_done, 4)
            chain(nc.vector.reciprocal(st[:, 7:8], st[:, 6:7]))
            chain(nc.vector.tensor_scalar(lg[:, :], lg[:, :], st[:, 7:8], COUPLING, ALU.mult, ALU.mult))
            dve.wait_ge(pe_done, 7)
            chain(nc.vector.tensor_copy(fa[:, :, :], banks[3][:, 0:TT * B].rearrange("p (t b) -> p t b", t=TT)))


PLAN = {
    (0, 0): [("pj", 0), ("pj", 1)],
    (0, 1): [("mt", 1), ("pj", 2)],
    (0, 2): [("ot", 3), ("pj", 3)],
    (0, 3): [("at", 0), ("at", 1)],
    (1, 0): [("coh", 0), ("op", 0)],
    (1, 1): [("mt", 2), ("op", 1)],
    (1, 2): [("ot", 0), ("xt", 0)],
    (1, 3): [("xt", 1), ("c1", 0)],
    (2, 0): [("v", 0), ("gate", 0)],
    (2, 1): [("mt", 3), ("vs", 0)],
    (2, 2): [("v", 1), ("ot", 1)],
    (2, 3): [("c1", 1)],
    (3, 0): [],
    (3, 1): [("mt", 0)],
    (3, 2): [("ot", 2), ("count", 0)],
    (3, 3): [],
}
ROUTE_PLAN = {(1, 3): 0, (2, 0): 1, (2, 1): 2, (2, 2): 3, (2, 3): 4, (3, 0): 5, (3, 1): 6, (3, 3): 7}
LAST_WORK = [("ot", 3), ("at", 0), ("at", 1), ("op", 0), ("op", 1), ("xt", 0), ("xt", 1), ("gate", 0),
             ("count", 0)]
NEXT_WORK = [("pj", i) for i in range(4)] + [("c1", 0), ("c1", 1)] + [("v", 0), ("v", 1)] + [("mt", 0)]
DVE_READS = ("pj", "mt", "ot", "coh", "vs", "v", "op", "gate", "count")
FIRST, TAIL = [task for task in NEXT_WORK if task[0] != "pj"], LAST_WORK
ORDER = [task for step in range(NG) for slot in range(TT) for task in PLAN[step, slot]]
LEAD = 2 * TT
TILES = NG * TT * G
SLOTS = NG * TT
LINKS = 2 * NG + 3
ROUTE_COUNTS = [6, 6, 3, 3, 6, 4, 1, 2]
ROUTE_STARTS = [sum(ROUTE_COUNTS[:i]) for i in range(8)]
ROUTE_LINKS = sum(ROUTE_COUNTS)
RSTD_AT, EXP_AT = ROUTE_STARTS[2], ROUTE_STARTS[3]
READS = 16 * 2 * len(Q_PARTS)


def kept(kind):
    left_out = {"first": LAST_WORK, "mid": [], "last": NEXT_WORK}[kind]
    return [task for task in ORDER if task not in left_out]


def misc_base(kind, b):
    return len(FIRST) if kind == "first" else len(FIRST) + len(kept("first")) + (b - 1) * len(ORDER)


def misc_use(kind, b, task):
    return misc_base(kind, b) + kept(kind).index(task)


def slot_tasks(kind, g, jt):
    return ([task if task in kept(kind) else None for task in PLAN[g, jt]] + [None, None])[:2]


def earlier_task(kind, g, jt):
    return slot_tasks(kind, g if jt else g - 1, (jt - 1) % TT)[1] if (g, jt) != (0, 0) else None


def uses_before(kind, g, jt):
    return sum(task in kept(kind) for at in PLAN if at < (g, jt) for task in PLAN[at])


TAIL_BASE = misc_base("last", B - 1) + len(kept("last"))


def lead_block(kind, b, g, jt):
    at = g * TT + jt + LEAD
    if at < SLOTS:
        return b, at
    return None if kind == "last" else (b + 1, at - SLOTS)


def after(engine, semaphore, count):
    if not (isinstance(count, int) and count == 0):
        engine.wait_ge(semaphore, count)


def batches(engine, body):
    body("first", 0, 0)
    with engine.Fori(0, (B - 2) // 2) as pair:
        body("mid", 2 * pair + 1, 1)
        body("mid", 2 * pair + 2, 0)
    body("last", B - 1, 1)


def attention(nc, banks, dram, w, x1, stacks, fa, cbias, gbias, wgr, routing, xs, tags, x1_dram):
    with ExitStack() as own:
        def sb(name, shape, dt=F32):
            return own.enter_context(nc.sbuf_tensor(name, shape, dt))

        def sem(name):
            return own.enter_context(nc.semaphore(name))

        xT, parts, rest, q, k = (stacks[n] for n in ("xT", "parts", "rest", "q", "k"))
        v = sb("v", [P, 2, TT, H, SUM + 1])
        mx = sb("mx", [P, 2, TT, G])
        mxp = sb("mxp", [P, 2, TT, SHIFTS, G], BF16)
        shift = sb("shift", [SHIFTS * G, 2, S], BF16)
        ident = sb("ident16", [P, P], BF16)
        pr = sb("pr", [P, TT, G, S])
        oT = sb("oT", [P, S])
        hT = sb("hT", [P, ET, S])
        z = sb("z", [P, TT, H])
        ez = sb("ez", [P, TT, H])
        coh = sb("coh", [P, TT, H])
        div = sb("div", [P, TT, G])
        rdiv = sb("rdiv", [P, TT, G])
        att = sb("att", [P, TT, E])
        attT = sb("attT", [P, ET, S])
        vsum = sb("vsum", [P, E])
        facur = sb("facur", [P, TT])
        ones = sb("ones", [P, P])
        rows, slot, tag, dest = (routing[n] for n in ("rows", "slot", "tag", "dest"))
        start, region = routing["start"], routing["region"]
        top = sb("top", [P, 2, TT])
        hot = sb("hot", [P, 2, TT, NX])
        squared = sb("squared", [P, TT, E], BF16)
        ssq = sb("ssq", [P, TT])
        ms = sb("ms", [P, TT])
        rstd = sb("rstd", [P, TT])
        t4 = sb("t4", [P, TT])
        logit = sb("logit", [P, TT, NX])
        gate = sb("gate", [P, TT, NX])
        left = sb("left", [P, TT, NX])
        key = sb("key", [P, TT, NX])
        both = sb("both", [P, TT, NX])
        row = sb("row", [P, TT, NX])
        picked = sb("batch_picked", [P, 2, TT, NX])
        batch_place = sb("batch_place", [P, 2, TT])
        none = sb("none", [P, 2, TT], I32)

        cleared = sem("cleared")
        rows_kept = sem("rows_kept")
        squares = sem("squares")
        gate_exp = sem("gate_exp")
        routed = sem("routed")
        marked = sem("marked")
        start_set, bank_cleared = sem("start_set"), sem("bank_cleared")
        row_set = sem("row_set")
        passed = sem("passed")
        placed = sem("placed")
        scattered = sem("scattered")
        x_in = [stacks["x_in0"], stacks["x_in1"]]
        first_part, second_part, parts_done, parts_out, stack_in = (
            stacks[n] for n in ("first_part", "second_part", "parts_done", "parts_out", "stack_in"))
        x_loaded, bias_added = sem("x_loaded"), sem("bias_added")
        a_ready, a_read = sem("a_ready"), sem("a_read")
        b_ready, b_read = sem("b_ready"), sem("b_read")
        max_first, mx_split = sem("max_first"), sem("mx_split")
        shift_in = sem("shift_in")
        slots_free = sem("slots_free")
        out_copied = sem("out_copied")
        misc_ready, misc_read = sem("misc_ready"), sem("misc_read")
        z_ready, ez_ready = sem("z_ready"), sem("ez_ready")
        link = sem("link")
        a_bank, b_bank, pv_bank, misc = banks[0:RING], banks[RING:2 * RING], banks[6], banks[7]
        turned_shift = misc[0:SHIFTS * G, 0:S // 2].bitcast(BF16)
        block = own.enter_context(nc.Block())

        @block.sync
        def _(sp):
            sp.dma_start(x1[:, :, :], dram["x"]).then_inc(x_loaded, 16)

            def body(kind, b, par):
                sp.wait_ge(stack_in, READS * (b + 1))
                make_stacks(sp, stacks, b + 1, 1 - par)

            def keep_rows(kind, b):
                at = (b - 1) * TT if isinstance(b, int) else sp.snap((b - 1) * TT)
                use = TAIL_BASE + TAIL.index(("op", 1)) if b is B else misc_use(kind, b, ("op", 1))
                sp.wait_ge(misc_read, use + 1)
                sp.dma_start(x1_dram[:, bass.ds(at, TT), :], rows[:, :, :]).then_inc(rows_kept, 16)

            def load_after(kind, b, par):
                first = (b + 2) * S if isinstance(b, int) else sp.snap((b + 2) * S)
                sp.wait_ge(misc_ready, misc_base(kind, b))
                sp.dma_start(xT[:, par, :, :], dram["xT"][:, :, bass.ds(first, S)]).then_inc(x_in[par], 16)

            def turn(kind, b, par, more=True):
                if more:
                    load_after(kind, b, par)
                body(kind, b, par)
                if kind != "first":
                    keep_rows(kind, b)

            turn("first", 0, 0)
            with sp.Fori(0, (B - 4) // 2) as pair:
                turn("mid", 2 * pair + 1, 1)
                turn("mid", 2 * pair + 2, 0)
            turn("mid", B - 3, 1)
            turn("mid", B - 2, 0, more=False)
            keep_rows("last", B - 1)
            keep_rows("last", B)
            sp.wait_ge(stack_in, READS * B)
            sp.wait_ge(rows_kept, 16 + 16 * B)

        @block.gpsimd
        def _(pool):
            nc.gpsimd.tensor_scalar(region[:, :], w["count"][:, 0:NX], float(CAP), None, ALU.mult).then_inc(cleared, 1)
            nc.gpsimd.memset(ones[:, :], 1.0).then_inc(cleared, 1)
            nc.gpsimd.memset(v[:, :, :, :, SUM:SUM + 1], 1.0).then_inc(cleared, 1)
            nc.gpsimd.tensor_copy(ident[:, :], w["ident"][:, :]).then_inc(cleared, 1)
            nc.gpsimd.memset(z[:, :, :], 0.0).then_inc(slots_free, TT)
            nc.gpsimd.memset(ssq[:, :], 0.0).then_inc(rows_kept, 16)
            nc.gpsimd.memset(none[:, :, :], 0).then_inc(cleared, 1)

            def split(b):
                for i in range(4):
                    pool.wait_ge(second_part, 4 * b + i + 1)
                    nc.gpsimd.tensor_tensor(parts[:, 2, i, :], rest[:, i, :], parts[:, 1, i, :],
                                            ALU.subtract).then_inc(parts_done, 1)

            pool.wait_ge(cleared, 5)
            nc.gpsimd.memset(k[STACK:STACK + SHIFTS, :, :, :], 1.0).then_inc(cleared, 1)
            pool.wait_ge(cleared, 6)

            def scatter(b):
                pool.wait_ge(placed, b + 1)
                nc.gpsimd.tensor_tensor(none[:, 1, :], none[:, 0, :], none[:, 0, :], ALU.add).then_inc(passed, 1)
                for i in range(2):
                    for t in range(TT):
                        pool.indirect_dma_start(out=xs, out_offset=bass.IndirectOffsetOnAxis(ap=slot[:, i, t:t + 1], axis=0),
                                                in_=rows[:, t, :], in_offset=None).then_inc(scattered, 16)
                        pool.indirect_dma_start(out=tags, out_offset=bass.IndirectOffsetOnAxis(ap=slot[:, i, t:t + 1], axis=0),
                                                in_=tag[:, i, t, :], in_offset=None).then_inc(scattered, 16)
                pool.wait_ge(passed, b + 1)
                pool.wait_ge(scattered, 16 * 4 * TT * (b + 1))

            def body(kind, b, par):
                if kind != "last":
                    split(b + 1)
                if kind != "first":
                    scatter(b - 1)

            pool.wait_ge(x_loaded, 16)
            nc.gpsimd.tensor_tensor(x1[:, :, :], x1[:, :, :],
                                    w["bo"][:, None, :].to_broadcast([P, T // P, E]), ALU.add).then_inc(bias_added, 1)
            batches(pool, body)

        @block.tensor
        def _(pe):
            def bank_free(read, b, n):
                if n >= RING:
                    pe.wait_ge(read, b * TILES + n - RING + 1)
                elif not (isinstance(b, int) and b == 0):
                    pe.wait_ge(read, b * TILES)

            def a_tile(b, at, h, par):
                g, it = at // TT, at % TT
                n = at * G + h
                bank_free(a_read, b, n)
                nc.tensor.matmul(a_bank[n % RING][:, :], q[0:STACK, par, g * G + h, it * P:(it + 1) * P],
                                 k[0:STACK, par, g * G + h, :], start=True, stop=True).then_inc(a_ready, 1)

            def b_tile(b, g, jt, h, par):
                n = (g * TT + jt) * G + h
                bank_free(b_read, b, n)
                r = slice(0, STACK + SHIFTS)
                nc.tensor.matmul(b_bank[n % RING][:, :], k[r, par, g * G + h, jt * P:(jt + 1) * P],
                                 q[r, par, g * G + h, :], start=True, stop=True).then_inc(b_ready, 1)

            def pv(b, g, jt, par):
                pe.wait_ge(b_read, b * TILES + (g * TT + jt + 1) * G)
                if jt == 0 and not (isinstance(b, int) and b == 0 and g == 0):
                    pe.wait_ge(out_copied, b * NG + g)
                for h in range(G):
                    last = nc.tensor.matmul(pv_bank[HW * h:HW * h + SUM + 1, :], v[:, par, jt, g * G + h, :], pr[:, jt, h, :],
                                            start=(jt == 0), stop=(jt == TT - 1), tile_position=(0, HW * h))
                last.then_inc(slots_free, 1)

            def turned(src):
                for t in range(TT):
                    last = nc.tensor.transpose(misc[:, t * P:(t + 1) * P], src(t), w["ident"][:, :])
                return last

            def product(task, no, par):
                what, i = task
                after(pe, misc_read, no)
                if what in ("pj", "c1"):
                    wt = w["wc1x"] if what == "c1" else w["wq"] if i < ET else w["wk"]
                    f = i % ET
                    for e in range(ET):
                        last = nc.tensor.matmul(misc[:, :], wt[:, e, f * P:(f + 1) * P], xT[:, par, e, :],
                                                start=(e == 0), stop=(e == ET - 1))
                elif what == "v":
                    for t in range(2):
                        for e in range(ET):
                            last = nc.tensor.matmul(misc[:, t * E:(t + 1) * E],
                                                    xT[:, par, e, (2 * i + t) * P:(2 * i + t + 1) * P], w["wv"][:, e, :],
                                                    start=(t == 0 and e == 0), stop=(e == ET - 1), skip_group_check=True)
                elif what == "coh":
                    for t in range(TT):
                        for e in range(ET):
                            last = nc.tensor.matmul(misc[:, t * H:(t + 1) * H], hT[:, e, t * P:(t + 1) * P],
                                                    w["wc2"][:, e, :], start=(t == 0 and e == 0),
                                                    stop=(e == ET - 1), skip_group_check=True)
                elif what == "vs":
                    for t in range(TT):
                        last = nc.tensor.matmul(misc[:, 0:E].rearrange("p (h d) -> p h d", h=H), ones[:, :],
                                                v[:, par, t, :, 0:HD], start=(t == 0), stop=(t == TT - 1))
                elif what == "ot":
                    last = turned(lambda t: oT[:, t * P:(t + 1) * P])
                elif what == "mt":
                    for t in range(TT):
                        last = nc.tensor.transpose(turned_shift[:, t * P:(t + 1) * P],
                                                   mxp[:, i % 2, t, :, :].rearrange("p c h -> p (c h)"), ident[:, :])
                elif what == "at":
                    last = turned(lambda t: att[:, t, i * P:(i + 1) * P])
                elif what == "xt":
                    last = turned(lambda t: rows[:, t, i * P:(i + 1) * P])
                elif what == "gate":
                    for t in range(TT):
                        for e in range(ET):
                            last = nc.tensor.matmul(misc[:, t * NX:(t + 1) * NX], attT[:, e, t * P:(t + 1) * P],
                                                    wgr[:, e, :], start=(t == 0 and e == 0), stop=(e == ET - 1),
                                                    skip_group_check=True)
                elif what == "count":
                    marks = both[:, :, :].rearrange("p t e -> p (t e)")
                    nc.tensor.matmul(misc[:, 0:TT * NX], w["tri"][:, :], marks, start=True, stop=True,
                                     skip_group_check=True)
                    for t in range(1, TT + 1):
                        last = nc.tensor.matmul(misc[:, t * NX:(TT + 1) * NX], ones[:, :], marks[:, 0:(TT + 1 - t) * NX],
                                                start=False, stop=(t == TT), skip_group_check=True)
                elif what == "op":
                    for t in range(2):
                        for e in range(ET):
                            r = slice((2 * i + t) * P, (2 * i + t + 1) * P)
                            last = nc.tensor.matmul(misc[:, t * E:(t + 1) * E], attT[:, e, r], w["wo"][:, e, :],
                                                    start=(t == 0 and e == 0), stop=(e == ET - 1),
                                                    skip_group_check=True)
                last.then_inc(misc_ready, 1)

            def inputs_ready(task, b, par):
                what, i = task
                if what == "mt":
                    pe.wait_ge(mx_split, b * NG + (i if i > 0 else NG) + 1)
                if what == "count":
                    pe.wait_ge(marked, b)
                if what == "ot":
                    pe.wait_ge(out_copied, b * NG + (i + 1 if i < NG - 1 else 0))

            pe.wait_ge(cleared, 5)
            pe.wait_ge(stack_in, READS)
            for no, task in enumerate(FIRST):
                if task == ("mt", 0):
                    pe.wait_ge(mx_split, 1)
                else:
                    for h in range(G):
                        a_tile(0, no, h, 0)
                product(task, no, 0)
            for at in range(TT, LEAD):
                for h in range(G):
                    a_tile(0, at, h, 0)

            def body(kind, b, par):
                for g in range(NG):
                    for jt in range(TT):
                        if jt == 0:
                            pe.wait_ge(shift_in, 32 * (b * NG + g + 1))
                        if kind == "first" and g == 0 and jt == 0:
                            pe.wait_ge(cleared, 6)
                            pe.wait_ge(bank_cleared, 1)
                        lead = lead_block(kind, b, g, jt)
                        if lead is not None and lead[1] == 0:
                            pe.wait_ge(stack_in, READS * (b + 2))
                        for h in range(G):
                            b_tile(b, g, jt, h, par)
                            if lead is not None:
                                a_tile(*lead, h, par if g * TT + jt + LEAD < SLOTS else 1 - par)
                        for i, task in enumerate(slot_tasks(kind, g, jt)):
                            if task is not None:
                                if task == ("pj", 0):
                                    x_loaded(kind, b, par)
                                else:
                                    inputs_ready(task, b, par)
                                product(task, misc_use(kind, b, task), 1 - par if task in NEXT_WORK else par)
                            if i == 0 and (g, jt) == (0, 0):
                                if kind != "first":
                                    pv(b - 1, NG - 1, TT - 1, 1 - par)
                            elif i == 0:
                                pv(b, g if jt else g - 1, (jt - 1) % TT, par)

            def x_loaded(kind, b, par):
                pe.wait_ge(x_in[1 - par], (b + 1 + 2 - (1 - par)) * 8)

            batches(pe, body)
            pv(B - 1, NG - 1, TT - 1, 1)
            for n, task in enumerate(TAIL):
                inputs_ready(task, B, 0)
                product(task, TAIL_BASE + n, 0)

        @block.scalar
        def _(act):
            def hidden_layer(i, no, b):
                act.wait_ge(misc_ready, no + 1)
                nc.scalar.activation(hT[:, i, :], misc[:, :], ACT.Tanh,
                                     bias=cbias[:, i, bass.ds(b, 1)]).then_inc(misc_read, 1)

            def take_first(i, no, b):
                act.wait_ge(misc_ready, no + 1)
                after(act, parts_out, 48 * b)
                nc.scalar.activation(parts[:, 0, i, :], misc[:, :], ACT.Identity,
                                     bias=w["bq" if i < ET else "bk"][:, i % ET:i % ET + 1]).then_inc(first_part, 1)

            def store_shift(no, g, par):
                act.wait_ge(misc_read, no + 1)
                for c in range(SHIFTS):
                    act.dma_start(q[STACK + c:STACK + c + 1, par, g * G:(g + 1) * G, :],
                                  shift[c * G:(c + 1) * G, g % 2, :]).then_inc(shift_in, 16)

            def square(b, no):
                act.wait_ge(misc_read, no + 1)
                for t in range(TT):
                    nc.scalar.activation(squared[:, t, :], rows[:, t, :], ACT.Square,
                                         accum_out=ssq[:, t:t + 1]).then_inc(squares, 1)

            def copy_out(step, uses):
                act.wait_ge(slots_free, (step + 2) * TT)
                act.wait_ge(misc_ready, uses)
                nc.scalar.activation(oT[:, :], pv_bank[:, :], ACT.Copy).then_inc(out_copied, 1)

            def by_features(i, no):
                act.wait_ge(misc_ready, no + 1)
                nc.scalar.activation(attT[:, i, :], misc[:, :], ACT.Copy).then_inc(misc_read, 1)

            def gate_exponentials(b):
                act.wait_ge(routed, ROUTE_LINKS * b + EXP_AT)
                nc.scalar.activation(gate[:, :, :], logit[:, :, :], ACT.Exp).then_inc(gate_exp, 1)

            for no, task in enumerate(FIRST):
                if task[0] == "c1":
                    hidden_layer(task[1], no, 0)
            store_shift(FIRST.index(("mt", 0)), 0, 0)

            def take(kind, b, task):
                no = misc_use(kind, b, task)
                if task[0] in ("at", "xt"):
                    by_features(task[1], no)
                elif task[0] == "pj":
                    take_first(task[1], no, b + 1)
                elif task[0] == "c1":
                    hidden_layer(task[1], no, b + 1)

            def body(kind, b, par):
                for g in range(NG):
                    for jt in range(TT):
                        if jt == 2 and not (kind == "last" and g == NG - 1):
                            store_shift(misc_use(kind, b, ("mt", (g + 1) % NG)), (g + 1) % NG,
                                        par if g < NG - 1 else 1 - par)
                        act.wait_ge(slots_free, b * SLOTS + g * TT + jt + 1)
                        for h in range(G):
                            if h == 1 and earlier_task(kind, g, jt) is not None:
                                take(kind, b, earlier_task(kind, g, jt))
                            if h == G - 1 and slot_tasks(kind, g, jt)[0] is not None:
                                take(kind, b, slot_tasks(kind, g, jt)[0])
                            n = (g * TT + jt) * G + h
                            act.wait_ge(b_ready, b * TILES + n + 1)
                            nc.scalar.activation(pr[:, jt, h, :], b_bank[n % RING][:, :], ACT.Exp,
                                                 scale=SCALE).then_inc(b_read, 1)
                        if (g, jt) == (1, 0):
                            act.wait_ge(z_ready, b + 1)
                            nc.scalar.activation(ez[:, :, :], z[:, :, :], ACT.Exp, scale=-1.0).then_inc(ez_ready, 1)
                        if jt == 0 and not (kind == "first" and g == 0):
                            copy_out(b * NG + g - 1, misc_base(kind, b) + uses_before(kind, g, jt))
                        if kind != "first" and (g, jt) == (1, 2):
                            square(b - 1, misc_use(kind, b, ("op", 1)))
                        if kind != "first" and (g, jt) == (2, 1):
                            gate_exponentials(b - 1)

            batches(act, body)
            copy_out(B * NG - 1, TAIL_BASE)
            for no, task in enumerate(TAIL):
                if task[0] == "at":
                    by_features(task[1], TAIL_BASE + no)
            square(B - 1, TAIL_BASE + TAIL.index(("op", 1)))
            for no, task in enumerate(TAIL):
                if task[0] == "xt":
                    by_features(task[1], TAIL_BASE + no)
            gate_exponentials(B - 1)

        @block.vector
        def _(dve):
            def reduce_head(b, at, h):
                g, it = at // TT, at % TT
                n = at * G + h
                dve.wait_ge(a_ready, b * TILES + n + 1)
                nc.vector.tensor_reduce(mx[:, g % 2, it, h:h + 1], a_bank[n % RING][:, :], X, ALU.max).then_inc(a_read, 1)

            def split_maxima(step, g):
                dve.wait_ge(a_read, (step + 1) * TT * G)
                m = mx[:, g % 2, :, :]
                nc.vector.tensor_scalar(mxp[:, g % 2, :, 0, :], m, -1.0, None, ALU.mult).then_inc(max_first, 1)
                dve.wait_ge(max_first, step + 1)
                nc.vector.scalar_tensor_tensor(mxp[:, g % 2, :, 1, :], m, -1.0, mxp[:, g % 2, :, 0, :],
                                               ALU.mult, ALU.subtract).then_inc(mx_split, 1)

            def read_misc(task, no, b, n, par):
                what, i = task
                dve.wait_ge(misc_ready, no + 1)
                if what == "pj":
                    dve.wait_ge(first_part, 4 * (b + 1) + i + 1)
                    after(dve, parts_done, 4 * (b + 1))
                    nc.vector.scalar_tensor_tensor(rest[:, i, :], misc[:, :],
                                                   w["bq" if i < ET else "bk"][:, i % ET:i % ET + 1],
                                                   parts[:, 0, i, :], ALU.add, ALU.subtract).then_inc(misc_read, 1)
                    dve.wait_ge(misc_read, no + 1)
                    nc.vector.tensor_copy(parts[:, 1, i, :], rest[:, i, :]).then_inc(second_part, 1)
                elif what == "v":
                    nc.vector.tensor_tensor(
                        v[:, 1 - par, 2 * i:2 * i + 2, :, 0:HD], misc[:, :].rearrange("p (t h d) -> p t h d", t=2, h=H),
                        w["bv"][:, :].rearrange("p (h d) -> p h d", h=H)[:, None, :, :]
                        .to_broadcast([P, 2, H, HD]), ALU.add).then_inc(misc_read, 1)
                elif what == "mt":
                    if not (isinstance(b, int) and b * NG + (i or NG) < 2):
                        dve.wait_ge(shift_in, 32 * (b * NG + (i or NG) - 1))
                    nc.vector.tensor_copy(shift[:, i % 2, :], turned_shift).then_inc(misc_read, 1)
                elif what == "coh":
                    nc.vector.tensor_tensor(z[:, :, :], misc[:, 0:TT * H].rearrange("p (t h) -> p t h", t=TT),
                                            w["bc2"][:, None, :].to_broadcast([P, TT, H]), ALU.add).then_inc(link, 1)
                    dve.wait_ge(link, n + 1)
                    nc.vector.tensor_scalar(z[:, :, :], z[:, :, :], -88.0, None, ALU.max).then_inc(z_ready, 1)
                    nc.vector.tensor_copy(facur[:, :], fa[:, :, bass.ds(b, 1)].rearrange("p t b -> p (t b)"))\
                        .then_inc(misc_read, 1)
                    return n + 1
                elif what == "vs":
                    nc.vector.tensor_copy(vsum[:, :], misc[:, 0:E]).then_inc(misc_read, 1)
                elif what == "op":
                    dve.wait_ge(rows_kept, 16 * b)
                    if not isinstance(b, int):
                        dve.wait_ge(parts_done, 4 * (b + 2))
                    elif b > 1:
                        dve.wait_ge(scattered, 16 * 4 * TT * (b - 1))
                    nc.vector.tensor_tensor(rows[:, 2 * i:2 * i + 2, :].rearrange("p t e -> p (t e)"), misc[:, :],
                                            x1[:, bass.ds((b - 1) * TT + 2 * i, 2), :].rearrange("p t e -> p (t e)"),
                                            ALU.add).then_inc(misc_read, 1)
                elif what == "gate":
                    dve.wait_ge(routed, ROUTE_LINKS * (b - 1) + RSTD_AT)
                    nc.vector.tensor_tensor(logit[:, :, :], misc[:, 0:TT * NX].rearrange("p (t e) -> p t e", t=TT),
                                            rstd[:, :, None].to_broadcast([P, TT, NX]), ALU.mult).then_inc(misc_read, 1)
                    dve.wait_ge(misc_read, no + 1)
                elif what == "count":
                    nc.vector.tensor_tensor(row[:, :, :], start[:, None, :].to_broadcast([P, TT, NX]),
                                            misc[:, 0:TT * NX].rearrange("p (t e) -> p t e", t=TT),
                                            ALU.add).then_inc(row_set, 1)
                    dve.wait_ge(row_set, b)
                    nc.vector.tensor_tensor(start[:, :], start[:, :], misc[:, TT * NX:(TT + 1) * NX],
                                            ALU.add).then_inc(misc_read, 1)
                elif what == "ot":
                    dve.wait_ge(misc_read, no)
                    dve.wait_ge(link, n)
                    o = misc[:, :].rearrange("p (t h r) -> p t h r", t=TT, h=G)
                    nc.vector.tensor_tensor(div[:, :, :], o[:, :, :, SUM], coh[:, :, i * G:(i + 1) * G],
                                            ALU.mult).then_inc(link, 1)
                    dve.wait_ge(link, n + 1)
                    nc.vector.reciprocal(rdiv[:, :, :], div[:, :, :]).then_inc(link, 1)
                    dve.wait_ge(link, n + 2)
                    dst = att[:, :, i * G * HD:(i + 1) * G * HD].rearrange("p t (h d) -> p t h d", h=G)
                    scaled = nc.vector.tensor_tensor(dst, o[:, :, :, 0:HD],
                                                     rdiv[:, :, :, None].to_broadcast([P, TT, G, HD]), ALU.mult)
                    if i < NG - 1:
                        scaled.then_inc(misc_read, 1)
                        return n + 2
                    scaled.then_inc(link, 1)
                    dve.wait_ge(link, n + 3)
                    for t in range(TT):
                        last = nc.vector.scalar_tensor_tensor(att[:, t, :], vsum[:, :], facur[:, t:t + 1],
                                                              att[:, t, :], ALU.mult, ALU.add)
                    last.then_inc(misc_read, 1)
                    return n + 3
                return n

            def route_batch(step, b, no=None):
                V = nc.vector
                at = ROUTE_LINKS * b + ROUTE_STARTS[step]
                here = bass.ds(b * TT, TT)
                count = [0]

                def chain(ins):
                    count[0] += 1
                    ins.then_inc(routed, 1)
                    dve.wait_ge(routed, at + count[0])

                def over_experts(a):
                    return a[:, :, None].to_broadcast([P, TT, NX])

                def numbers():
                    return w["count"][:, None, 0:NX].to_broadcast([P, TT, NX])

                def newton():
                    chain(V.tensor_tensor(t4[:, :], rstd[:, :], rstd[:, :], ALU.mult))
                    chain(V.scalar_tensor_tensor(t4[:, :], t4[:, :], -0.5, ms[:, :], ALU.mult, ALU.mult))
                    chain(V.scalar_tensor_tensor(rstd[:, :], t4[:, :], 1.5, rstd[:, :], ALU.add, ALU.mult))

                def best(i, src):
                    chain(V.tensor_reduce(top[:, i, :], src[:, :, :], X, ALU.max))
                    chain(V.tensor_tensor(key[:, :, :], src[:, :, :], over_experts(top[:, i, :]), ALU.is_lt))
                    chain(V.scalar_tensor_tensor(key[:, :, :], key[:, :, :], float(NX), numbers(), ALU.mult, ALU.add))
                    chain(V.tensor_reduce(t4[:, :], key[:, :, :], X, ALU.min))

                if step == 0:
                    dve.wait_ge(squares, TT * (b + 1))
                    chain(V.tensor_scalar(ms[:, :], ssq[:, :], 1.0 / E, 1e-6, ALU.mult, ALU.add))
                    chain(V.tensor_scalar(t4[:, :].bitcast(I32), ms[:, :].bitcast(I32), 1, None, ALU.arith_shift_right))
                    chain(V.tensor_scalar(rstd[:, :].bitcast(I32), t4[:, :].bitcast(I32), -1.0, float(0x5f3759df),
                                          ALU.mult, ALU.add))
                    newton()
                elif step == 1:
                    newton()
                    newton()
                elif step == 2:
                    chain(V.tensor_tensor(logit[:, :, :], logit[:, :, :],
                                          gbias[:, bass.ds(b, 1), :].to_broadcast([P, TT, NX]), ALU.add))
                    chain(V.tensor_reduce(t4[:, :], logit[:, :, :], X, ALU.max))
                    chain(V.tensor_tensor(logit[:, :, :], logit[:, :, :], over_experts(t4), ALU.subtract))
                elif step == 3:
                    dve.wait_ge(gate_exp, b + 1)
                    chain(V.reduce_sum(t4[:, :], gate[:, :, :], axis=X))
                    chain(V.reciprocal(t4[:, :], t4[:, :]))
                    chain(V.tensor_tensor(gate[:, :, :], gate[:, :, :], over_experts(t4), ALU.mult))
                elif step == 4:
                    best(0, gate)
                    chain(V.tensor_tensor(hot[:, 0, :, :], numbers(), over_experts(t4), ALU.is_equal))
                    chain(V.scalar_tensor_tensor(left[:, :, :], hot[:, 0, :, :], -2.0, gate[:, :, :], ALU.mult, ALU.add))
                elif step == 5:
                    best(1, left)
                elif step == 6:
                    chain(V.tensor_tensor(hot[:, 1, :, :], numbers(), over_experts(t4), ALU.is_equal))
                    V.tensor_tensor(both[:, :, :], hot[:, 0, :, :], hot[:, 1, :, :], ALU.add).then_inc(marked, 1)
                elif step == 7:
                    dve.wait_ge(misc_read, no + 1)
                    chain(V.tensor_tensor(picked[:, :, :, :], hot[:, :, :, :],
                                          row[:, None, :, :].to_broadcast([P, 2, TT, NX]), ALU.mult))
                    chain(V.reduce_sum(batch_place[:, :, :], picked[:, :, :, :], axis=X))
                    V.tensor_copy(slot[:, :, :], batch_place[:, :, :])
                    V.tensor_copy(tag[:, :, :, 0], top[:, :, :])
                    V.tensor_copy(tag[:, :, :, 1].bitcast(I32), dest[:, 0:2 * T // P].rearrange("p (i t) -> p i t", i=2)[:, :, here])\
                        .then_inc(placed, 1)
                assert count[0] == ROUTE_COUNTS[step]

            dve.wait_ge(cleared, 5)
            nc.vector.memset(pv_bank[:, :], 0.0).then_inc(bank_cleared, 1)
            nc.vector.tensor_copy(dest[:, :], w["dest"][:, :]).then_inc(start_set, 1)
            nc.vector.tensor_copy(start[:, :], region[:, :]).then_inc(start_set, 1)
            dve.wait_ge(start_set, 2)
            for no, task in enumerate(FIRST):
                if task == ("mt", 0):
                    split_maxima(0, 0)
                else:
                    for h in range(G):
                        reduce_head(0, no, h)
                if task[0] in DVE_READS:
                    read_misc(task, no, -1, 0, 1)
            for n in range(TT * G, LEAD * G):
                reduce_head(0, n // G, n % G)

            def links_before(kind, b):
                return 0 if kind == "first" else LINKS - 3 + (b - 1) * LINKS

            def body(kind, b, par):
                n = links_before(kind, b)
                for g in range(NG):
                    for jt in range(TT):
                        if jt == 0 and not (kind == "last" and g == NG - 1):
                            split_maxima(b * NG + g + 1, (g + 1) % NG)
                        lead = lead_block(kind, b, g, jt)
                        if kind == "first" and (g, jt) == (3, 3):
                            dve.wait_ge(bias_added, 1)
                        first, earlier = slot_tasks(kind, g, jt)[0], earlier_task(kind, g, jt)
                        for h in range(G):
                            if lead is not None:
                                reduce_head(*lead, h)
                            if h == 0 and earlier is not None and earlier[0] in DVE_READS:
                                n = read_misc(earlier, misc_use(kind, b, earlier), b, n, par)
                            if h == G - 2 and first is not None and first[0] in DVE_READS:
                                n = read_misc(first, misc_use(kind, b, first), b, n, par)
                        if (g, jt) == (1, 1):
                            dve.wait_ge(ez_ready, b + 1)
                            nc.vector.tensor_scalar(coh[:, :, :], ez[:, :, :], 1e-8 / KEEP, (1.0 + 1e-8) / KEEP,
                                                    ALU.mult, ALU.add).then_inc(link, 1)
                            n = n + 1
                        if kind != "first" and (g, jt) in ROUTE_PLAN:
                            route_batch(ROUTE_PLAN[g, jt], b - 1,
                                        misc_use(kind, b, ("count", 0)) if (g, jt) == (3, 3) else None)

            batches(dve, body)
            n = links_before("last", B)
            for i, task in enumerate(TAIL):
                if task[0] in DVE_READS:
                    n = read_misc(task, TAIL_BASE + i, B, n, 0)
                for step in {"xt": [0, 1] if task[1] == 0 else [], "gate": [2, 3, 4, 5, 6], "count": [7]}.get(task[0], []):
                    route_batch(step, B - 1, TAIL_BASE + i)


def route(nc, dram, w, routing, raw, split, streams, expert, first_row, xs, tags):
    NO = TILES_MAX + 2
    with ExitStack() as own:
        def sb(name, shape, dt=F32):
            return own.enter_context(nc.sbuf_tensor(name, shape, dt))

        def sem(name):
            return own.enter_context(nc.semaphore(name))

        rows, slot, tag, dest = (routing[n] for n in ("rows", "slot", "tag", "dest"))
        start, region = routing["start"], routing["region"]
        loaded = sem("inputs_in")
        zeros = sb("zeros", [P, TS // P * E])
        pad = sb("pad", [P, TS // P, 2])
        count = sb("row_count", [P, NX])
        icount = sb("irow_count", [P, NX], I32)
        iend = sb("iend", [P, NX], I32)
        tiles = sb("tiles", [P, NX])
        ends = sb("ends", [P, NX])
        shift = sb("region_shift", [P, NX])
        used = sb("used", [P, NO])
        owned = sb("owned", [P, NO, NX])
        number = sb("number", [P, NO])
        raw_in, hi_done, lo_done = (streams["raw_half0"], streams["raw_half1"]), streams["split_hi"], streams["split_lo"]
        scattered = sem("last_scattered")
        pad_cleared = sem("pad_cleared")
        cleared, ends_set, filled, link = sem("zeros_set"), sem("ends_set"), sem("filled"), sem("route_link")
        block = own.enter_context(nc.Block())

        def quarter_of(a, c):
            return a[:, 0, c * QUARTER:(c + 1) * QUARTER]

        def raw_quarter(c):
            return raw[:, c // 2, c % 2 * QUARTER:(c % 2 + 1) * QUARTER]

        @block.sync
        def _(sp):
            for half in range(2):
                sp.dma_start(raw[:, half, :], dram["we"][:, 0, half * HALF:(half + 1) * HALF]).then_inc(raw_in[half], 16)
            for name in ("b1", "b2"):
                sp.dma_start(w[name][:, :, :], dram[name]).then_inc(loaded, 16)
            sp.wait_ge(cleared, 2)
            sp.wait_ge(ends_set, 1)
            for e in range(NX + 1):
                end = NX * CAP if e == NX else sp.value_load(iend[0:1, e:e + 1], min_val=0, max_val=NX * CAP - TS)
                sp.dma_start(tags[bass.ds(end, TS), :].rearrange("(s p) n -> p s n", p=P), pad[:, :, :]).then_inc(filled, 16)
            sp.wait_ge(loaded, 16 * 2)

        @block.scalar
        def _(act):
            act.wait_ge(cleared, 1)
            act.wait_ge(ends_set, 1)
            for e in range(NX + 1):
                end = NX * CAP if e == NX else act.value_load(iend[0:1, e:e + 1], min_val=0, max_val=NX * CAP - TS)
                act.dma_start(xs[bass.ds(end, TS), :].rearrange("(p r) e -> p (r e)", r=TS // P), zeros[:, :]).then_inc(filled, 16)
            for c in range(4):
                act.wait_ge(raw_in[c // 2], 16)
                nc.scalar.activation(quarter_of(split[0], c), raw_quarter(c), ACT.Copy, scale=WSCALE).then_inc(hi_done, 1)
            act.wait_ge(filled, 16 * 2 * (NX + 1))

        @block.vector
        def _(dve):
            n = [0]

            def chain(ins):
                n[0] += 1
                ins.then_inc(link, 1)
                dve.wait_ge(link, n[0])

            V = nc.vector
            V.memset(zeros[:, :], 0.0).then_inc(cleared, 1)
            V.memset(pad[:, :, :], 0.0).then_inc(pad_cleared, 1)
            dve.wait_ge(pad_cleared, 1)
            V.tensor_copy(pad[:, :, 1].bitcast(I32), dest[:, 2 * T // P:]).then_inc(cleared, 1)
            end = start[:, :]
            V.tensor_copy(iend[:, :], end).then_inc(ends_set, 1)
            chain(V.tensor_tensor(count[:, :], end, region[:, :], ALU.subtract))
            chain(V.tensor_scalar(icount[:, :], count[:, :], float(TS - 1), None, ALU.add))
            chain(V.tensor_scalar(icount[:, :], icount[:, :], TS.bit_length() - 1, None, ALU.arith_shift_right))
            chain(V.tensor_copy(tiles[:, :], icount[:, :]))
            chain(V.tensor_scalar(tiles[:, :], tiles[:, :], 1.0, None, ALU.max))
            chain(V.tensor_copy(ends[:, :], tiles[:, :]))
            for e in range(1, NX):
                chain(V.tensor_tensor(ends[:, e:e + 1], ends[:, e:e + 1], ends[:, e - 1:e], ALU.add))
            chain(V.tensor_tensor(shift[:, :], ends[:, :], tiles[:, :], ALU.subtract))
            chain(V.scalar_tensor_tensor(shift[:, :], shift[:, :], float(TS), region[:, :], ALU.mult, ALU.subtract))
            chain(V.tensor_tensor(owned[:, :, :], ends[:, None, :].to_broadcast([P, NO, NX]),
                                  w["count"][:, :, None].to_broadcast([P, NO, NX]), ALU.is_le))
            chain(V.reduce_sum(number[:, :], owned[:, :, :], axis=X))
            chain(V.tensor_scalar(number[:, :], number[:, :], float(NX - 1), None, ALU.min))
            chain(V.tensor_copy(expert[:, :], number[:, :]))
            chain(V.tensor_tensor(owned[:, :, :], w["count"][:, None, 0:NX].to_broadcast([P, NO, NX]),
                                  number[:, :, None].to_broadcast([P, NO, NX]), ALU.is_equal))
            chain(V.tensor_tensor(owned[:, :, :], owned[:, :, :], shift[:, None, :].to_broadcast([P, NO, NX]), ALU.mult))
            chain(V.reduce_sum(number[:, :], owned[:, :, :], axis=X))
            chain(V.tensor_scalar(used[:, :], w["count"][:, :], ends[:, NX - 1:NX], None, ALU.is_lt))
            chain(V.scalar_tensor_tensor(number[:, :], w["count"][:, :], float(TS), number[:, :], ALU.mult, ALU.subtract))
            chain(V.scalar_tensor_tensor(number[:, :], number[:, :], float(-NX * CAP), used[:, :], ALU.add, ALU.mult))
            chain(V.tensor_scalar(first_row[:, :], number[:, :], float(NX * CAP), None, ALU.add))
            for c in range(4):
                dve.wait_ge(hi_done, c + 1)
                V.scalar_tensor_tensor(quarter_of(split[1], c), raw_quarter(c), WSCALE, quarter_of(split[0], c),
                                       ALU.mult, ALU.subtract).then_inc(lo_done, 1)

        @block.gpsimd
        def _(pool):
            for i in range(2):
                for t in range(TT):
                    pool.indirect_dma_start(out=xs, out_offset=bass.IndirectOffsetOnAxis(ap=slot[:, i, t:t + 1], axis=0),
                                            in_=rows[:, t, :], in_offset=None).then_inc(scattered, 16)
                    pool.indirect_dma_start(out=tags, out_offset=bass.IndirectOffsetOnAxis(ap=slot[:, i, t:t + 1], axis=0),
                                            in_=tag[:, i, t, :], in_offset=None).then_inc(scattered, 16)
            pool.wait_ge(scattered, 16 * 4 * TT)


def experts(nc, banks, dram, w, raw, split, streams, expert, first_row, xs, tags, shares, x1_dram, x1_again):
    MT = M // P
    SUB = TS // P
    with ExitStack() as own:
        def sb(name, shape, dt=F32):
            return own.enter_context(nc.sbuf_tensor(name, shape, dt))

        def sem(name):
            return own.enter_context(nc.semaphore(name))

        x = sb("x_tile", [P, SUB, E])
        xh, xl = sb("xh", [P, ET, TS], F16), sb("xl", [P, ET, TS], F16)
        hf = [sb(f"hf{i}", [P, MT, TS]) for i in range(2)]
        hh = [sb(f"hh{i}", [P, MT, TS], F16) for i in range(2)]
        hl = [sb(f"hl{i}", [P, MT, TS], F16) for i in range(2)]
        y = sb("y", [P, SUB, E])
        x_in, turned, x_hi, x_lo = sem("xt_in"), sem("xt_turned"), sem("x_hi"), sem("x_lo")
        made = [sem(f"layer{i}") for i in range(3)]
        full = [sem(f"full{i}") for i in range(2)]
        hi = [sem(f"hi{i}") for i in range(2)]
        lo = [sem(f"lo{i}") for i in range(2)]
        tag = sb("tile_tag", [P, SUB, 2])
        y_dest = sb("y_dest", [P, SUB], I32)
        y_made, y_done, y_out = sem("y_made"), sem("y_done"), sem("y_out")
        tag_in, x1_in = sem("tag_in"), sem("x1_in")
        b3_in = sem("b3_in")
        raw_in, split_hi, split_lo = (streams["raw_half0"], streams["raw_half1"]), streams["split_hi"], streams["split_lo"]
        layer = [banks[0:2], banks[2:4]]
        y_bank, t_bank = banks[4], banks[5]
        bias = [w["b1"], w["b2"]]
        block = own.enter_context(nc.Block())

        def turns(engine, body):
            body(0, "first")
            with engine.Fori(1, NX - 3) as i:
                body(i, "splits")
            body(NX - 3, "last")
            body(NX - 2, "after")
            with engine.Fori(NX - 1, TILES_MAX) as i:
                body(i, None)

        def quarter_of(a, e, c):
            return a[:, bass.ds(e, 1), c * QUARTER:(c + 1) * QUARTER].rearrange("p a n -> p (a n)")

        def half_of(a, e, half):
            return a[:, bass.ds(e, 1), half * HALF:(half + 1) * HALF].rearrange("p a n -> p (a n)")

        def raw_quarter(c):
            return raw[:, c // 2, c % 2 * QUARTER:(c % 2 + 1) * QUARTER]

        @block.sync
        def _(sp):
            def load(i):
                row = sp.value_load(first_row[0:1, bass.ds(i, 1)], min_val=0, max_val=NX * CAP)
                sp.dma_start(x[:, :, :], xs[bass.ds(row, TS), :].rearrange("(s p) e -> p s e", p=P)).then_inc(x_in, 16)

            def load_tag(i):
                row = sp.value_load(first_row[0:1, bass.ds(i, 1)], min_val=0, max_val=NX * CAP)
                sp.dma_start(tag[:, :, :], tags[bass.ds(row, TS), :].rearrange("(s p) n -> p s n", p=P)).then_inc(tag_in, 16)

            load(0)
            load_tag(0)
            for half in range(2):
                sp.wait_ge(split_lo, 2 * half + 2)
                sp.dma_start(raw[:, half, :], half_of(dram["we"], 1, half)).then_inc(raw_in[half], 16)
            sp.wait_ge(turned, 1)
            load(1)
            sp.dma_start(w["b3"][:, :, :], dram["b3"]).then_inc(b3_in, 16)

            def body(i, splits):
                sp.wait_ge(turned, i + 2)
                load(i + 2)
                if splits in ("last", "after"):
                    n = HELD * TT // 2
                    held = slice(0, n) if splits == "last" else slice(n, 2 * n)
                    sp.dma_start(x1_again[:, held, :], x1_dram[:, held, :]).then_inc(x1_in, 16)
                sp.wait_ge(y_done, i + 1)
                load_tag(i + 1)

            turns(sp, body)
            sp.wait_ge(x1_in, 32)
            sp.wait_ge(tag_in, 16 * (TILES_MAX + 1))

        @block.tensor
        def _(pe):
            def turn(i):
                pe.wait_ge(x_in, (i + 1) * 16)
                after(pe, x_lo, i)
                for e in range(ET):
                    for s in range(SUB):
                        last = nc.tensor.transpose(t_bank[:, (e * SUB + s) * P:(e * SUB + s + 1) * P],
                                                   x[:, s, e * P:(e + 1) * P], w["ident"][:, :])
                last.then_inc(turned, 1)

            def weights(name, part, e, k, cols):
                first, width = LAYERS[name]
                at = first + k * width + cols.start
                return split[part][:, bass.ds(e, 1), at:at + cols.stop - cols.start].rearrange("p a n -> p (a n)")

            def hidden(which, i, e):
                name, K = ("w1", ET) if which == 0 else ("w2", MT)
                ah, al = (xh, xl) if which == 0 else (hh[0], hl[0])
                if which == 0:
                    pe.wait_ge(x_lo, i + 1)
                for m in range(MT):
                    if m % 2 == 0 and not (isinstance(i, int) and i == 0):
                        pe.wait_ge(full[which], (i - 1) * MT + m + 2)
                    out = layer[which][m // 2][:, m % 2 * TS:(m % 2 + 1) * TS]
                    c = slice(m * P, (m + 1) * P)
                    for k in range(K):
                        if which == 1 and m == 0:
                            pe.wait_ge(lo[0], i * MT + k + 1)
                        for a, part in ((ah, 0), (ah, 1), (al, 0)):
                            last = nc.tensor.matmul(out, weights(name, part, e, k, c), a[:, k, :],
                                                    start=(k == 0 and a is ah and part == 0),
                                                    stop=(k == K - 1 and a is al), skip_group_check=True)
                    last.then_inc(made[which], 1)

            def final(i, e):
                after(pe, y_done, i)
                for s in range(SUB):
                    r = slice(s * P, (s + 1) * P)
                    for k in range(MT):
                        if s == 0:
                            pe.wait_ge(lo[1], i * MT + k + 1)
                        for a, part in ((hh[1], 0), (hh[1], 1), (hl[1], 0)):
                            last = nc.tensor.matmul(y_bank[:, s * E:(s + 1) * E], a[:, k, r],
                                                    weights("w3", part, e, k, slice(0, E)),
                                                    start=(k == 0 and a is hh[1] and part == 0),
                                                    stop=(k == MT - 1 and a is hl[1]), skip_group_check=True)
                last.then_inc(made[2], 1)

            def expert_of(i):
                return pe.value_load(expert[0:1, bass.ds(i, 1)], min_val=0, max_val=NX - 1)

            turn(0)
            hidden(0, 0, expert_of(0))
            turn(1)

            def body(i, splits):
                e = expert_of(i)
                e_next = expert_of(i + 1)
                hidden(1, i, e)
                if splits is not None:
                    pe.wait_ge(split_lo, 4 * (i + 2))
                hidden(0, i + 1, e_next)
                turn(i + 2)
                final(i, e)

            turns(pe, body)

        @block.scalar
        def _(act):
            def take_turned(i):
                act.wait_ge(turned, i + 1)
                after(act, made[0], i * MT)
                nc.scalar.activation(xh[:, :, :].rearrange("p e n -> p (e n)"), t_bank[:, :], ACT.Copy).then_inc(x_hi, 1)

            def take_hidden(which, i, splits=None):
                e = act.value_load(expert[0:1, bass.ds(i, 1)], min_val=0, max_val=NX - 1)
                for m in range(MT):
                    act.wait_ge(made[which], i * MT + m // 2 * 2 + 2)
                    after(act, lo[which], i * MT)
                    nc.scalar.activation(hf[which][:, m, :], layer[which][m // 2][:, m % 2 * TS:(m % 2 + 1) * TS],
                                         ACT.Relu, bias=bias[which][:, bass.ds(e, 1), m], scale=1.0 / WSCALE)\
                        .then_inc(full[which], 1)
                    if splits is not None and m % 2 == 1:
                        split_quarter(splits, m // 2 + (0 if which == 1 else 2))

            def load_half(e, half):
                here = half_of(dram["we"], e if isinstance(e, int) else act.snap(e), half)
                act.wait_ge(split_lo, 4 * (e - 1) + 2 * half + 2)
                act.dma_start(raw[:, half, :], here).then_inc(raw_in[half], 16)

            def split_quarter(e, c):
                act.wait_ge(raw_in[c // 2], 16 * (e + 1))
                nc.scalar.activation(quarter_of(split[0], e, c), raw_quarter(c), ACT.Copy, scale=WSCALE).then_inc(split_hi, 1)

            take_turned(0)
            take_hidden(0, 0)
            take_turned(1)
            for c in range(4):
                split_quarter(1, c)
            load_half(2, 0)

            def body(i, splits):
                e = i + 2 if splits in ("first", "splits", "last") else None
                if e is not None:
                    load_half(e, 1)
                take_hidden(1, i, e)
                take_hidden(0, i + 1, e)
                if splits in ("first", "splits"):
                    load_half(i + 3, 0)
                take_turned(i + 2)

            turns(act, body)

        @block.vector
        def _(dve):
            def take_turned(i):
                dve.wait_ge(x_hi, i + 1)
                nc.vector.tensor_tensor(xl[:, :, :].rearrange("p e n -> p (e n)"), t_bank[:, :],
                                        xh[:, :, :].rearrange("p e n -> p (e n)"), ALU.subtract).then_inc(x_lo, 1)

            def take_hidden(which, i, splits=None):
                for m in range(MT):
                    dve.wait_ge(full[which], i * MT + m + 1)
                    if m == 0:
                        after(dve, made[which + 1], i * (MT if which == 0 else 1))
                    nc.vector.tensor_copy(hh[which][:, m, :], hf[which][:, m, :]).then_inc(hi[which], 1)
                    if splits is not None and m % 2 == 1:
                        split_quarter(splits, m // 2 + (0 if which == 1 else 2))

            def take_final(i):
                e = dve.value_load(expert[0:1, bass.ds(i, 1)], min_val=0, max_val=NX - 1)
                dve.wait_ge(made[2], i + 1)
                after(dve, y_out, i * 16 * SUB)
                for s in range(SUB):
                    last = nc.vector.scalar_tensor_tensor(y[:, s, :], y_bank[:, s * E:(s + 1) * E], 1.0 / WSCALE,
                                                          w["b3"][:, bass.ds(e, 1), :].rearrange("p a n -> p (a n)"),
                                                          ALU.mult, ALU.add)
                last.then_inc(y_made, 1)
                dve.wait_ge(tag_in, 16 * (i + 1))
                dve.wait_ge(y_made, i + 1)
                for s in range(SUB):
                    nc.vector.tensor_scalar(y[:, s, :], y[:, s, :], tag[:, s, 0:1], None, ALU.mult)
                nc.vector.tensor_copy(y_dest[:, :], tag[:, :, 1].bitcast(I32)).then_inc(y_done, 1)

            def split_quarter(e, c):
                dve.wait_ge(split_hi, 4 * e + c + 1)
                nc.vector.scalar_tensor_tensor(quarter_of(split[1], e, c), raw_quarter(c), WSCALE,
                                               quarter_of(split[0], e, c), ALU.mult, ALU.subtract).then_inc(split_lo, 1)

            take_turned(0)
            take_hidden(0, 0)
            take_turned(1)
            for c in range(4):
                split_quarter(1, c)

            dve.wait_ge(b3_in, 16)

            def body(i, splits):
                e = i + 2 if splits in ("first", "splits", "last") else None
                take_hidden(1, i, e)
                take_hidden(0, i + 1, e)
                take_turned(i + 2)
                take_final(i)

            turns(dve, body)

        @block.gpsimd
        def _(pool):
            def take_hidden(which, i, scatters=False):
                for m in range(MT):
                    if m == MT - 1 and scatters:
                        pool.wait_ge(y_done, i)
                    pool.wait_ge(hi[which], i * MT + m + 1)
                    nc.gpsimd.tensor_tensor(hl[which][:, m, :], hf[which][:, m, :], hh[which][:, m, :],
                                            ALU.subtract).then_inc(lo[which], 1)

            def scatter():
                for s in range(SUB):
                    pool.indirect_dma_start(out=shares, out_offset=bass.IndirectOffsetOnAxis(ap=y_dest[:, s:s + 1], axis=0),
                                            in_=y[:, s, :], in_offset=None).then_inc(y_out, 16)

            take_hidden(0, 0)

            def body(i, splits):
                take_hidden(1, i, scatters=splits != "first")
                if splits != "first":
                    scatter()
                take_hidden(0, i + 1)

            turns(pool, body)
            pool.wait_ge(y_done, TILES_MAX)
            scatter()
            pool.wait_ge(y_out, 16 * SUB * TILES_MAX)


def combine(nc, x1_dram, x1_again, shares, out):
    RINGS = 4
    with ExitStack() as own:
        def sem(name):
            return own.enter_context(nc.semaphore(name))

        share = own.enter_context(nc.sbuf_tensor("share", [P, RINGS, 2, TT, E], F32))
        x1_rest = own.enter_context(nc.sbuf_tensor("x1_rest", [P, (B - HELD) * TT, E], F32))
        x1_in = sem("x1_rest_in")
        share_in = [sem(f"share_in{i}") for i in range(RINGS)]
        added, stored = sem("added"), sem("stored")
        block = own.enter_context(nc.Block())

        def rows_of(b):
            held, at = (x1_again, b) if b < HELD else (x1_rest, b - HELD)
            return held[:, at * TT:(at + 1) * TT, :]

        @block.sync
        def _(sp):
            for b in range(B):
                if b == HELD - 1:
                    sp.dma_start(x1_rest[:, :, :], x1_dram[:, HELD * TT:, :]).then_inc(x1_in, 16)
                if b >= RINGS:
                    sp.wait_ge(added, 2 * (b - RINGS + 1))
                for i in range(2):
                    sp.dma_start(share[:, b % RINGS, i, :, :], shares[i * T + b * S:i * T + (b + 1) * S, :]
                                 .rearrange("(t p) e -> p t e", p=P)).then_inc(share_in[b % RINGS], 16)

        @block.vector
        def _(dve):
            for b in range(B):
                rows = rows_of(b)
                if b == HELD:
                    dve.wait_ge(x1_in, 16)
                dve.wait_ge(share_in[b % RINGS], 32 * (b // RINGS + 1))
                for i in range(2):
                    nc.vector.tensor_tensor(rows, rows, share[:, b % RINGS, i, :, :], ALU.add).then_inc(added, 1)
                    dve.wait_ge(added, 2 * b + i + 1)

        @block.scalar
        def _(act):
            for b in range(B):
                act.wait_ge(added, 2 * (b + 1))
                act.dma_start(out[:, b * TT:(b + 1) * TT, :], rows_of(b)).then_inc(stored, 16)
            act.wait_ge(stored, 16 * B)


def kernel(**inputs):
    import concourse.bacc as bacc
    from concourse.bass_utils import run_bass_kernel_spmd

    arrays = {n: np.ascontiguousarray(a) for n, a in layout(inputs).items()}
    nc = bacc.Bacc("TRN2", target_bir_lowering=False, num_devices=1)
    dram = {}
    for n, shape in INPUTS.items():
        assert list(arrays[n].shape) == shape, n
        dram[n] = nc.dram_tensor("in_" + n, shape, F32, kind="ExternalInput").ap()
    out = nc.dram_tensor("out", OUT, F32, kind="ExternalOutput").ap()
    program(nc, dram, out)
    result = run_bass_kernel_spmd(nc, [{"in_" + n: arrays[n] for n in INPUTS}], core_ids=[0])
    return finish(result.results[0]["out"])


def layout(i):
    def cols(a):
        return np.asarray(a).reshape(-1, P).T

    def rows(a):
        a = np.asarray(a)
        return a.reshape(-1, P, a.shape[-1]).transpose(1, 0, 2)

    def rep(a, n=P):
        return np.broadcast_to(np.asarray(a), (n, np.asarray(a).shape[-1]))

    def by_rows(a):
        a = np.asarray(a)
        return a.reshape(NX, -1, P, a.shape[-1]).transpose(2, 0, 1, 3).reshape(P, NX, -1)

    x = np.asarray(i["x"]).reshape(T, E)
    dest = np.arange((2 * T + TS) // P * P, dtype=np.float32).reshape(-1, P).T
    wqkv, bqkv = np.asarray(i["L0_cond_Wqkv"]), np.asarray(i["L0_cond_bqkv"])
    wc1 = np.asarray(i["L0_cond_Wc1"])
    rate = np.float32(10000.0) ** np.repeat(np.arange(0, E, 2, dtype=np.float32) / np.float32(E), 2)
    pe = np.sin(np.arange(S, dtype=np.float32)[:, None] / rate[None, :]).astype(np.float32)
    return {
        "xT": rows(x.T), "x": x.reshape(T // P, P, E).transpose(1, 0, 2),
        "wq": rows(wqkv[0:E].T), "wk": rows(wqkv[E:2 * E].T), "bq": cols(bqkv[0:E]), "bk": cols(bqkv[E:2 * E]),
        "wv": rows(wqkv[2 * E:].T), "bv": rep(bqkv[2 * E:]),
        "wo": rows(np.asarray(i["L0_cond_Wout"]).T), "bo": rep(i["L0_cond_bout"]),
        "wc1x": rows(wc1[:, 0:E].T), "wc1c": wc1[:, E:].T, "bc1": cols(i["L0_cond_bc1"]),
        "wc2": rows(np.asarray(i["L0_cond_Wc2"]).T), "bc2": rep(i["L0_cond_bc2"]),
        "cT": np.asarray(i["cond_256"]).T, "we1": np.asarray(i["L0_cond_We1"]).T, "be1": cols(i["L0_cond_be1"]),
        "we2": rows(np.asarray(i["L0_cond_We2"]).T), "be2": rep(i["L0_cond_be2"], B),
        "ln_g": rep(i["L0_cond_ln_g"], B), "ln_b": rep(i["L0_cond_ln_b"], B),
        "pe": rows(pe.T), "ident": np.eye(P, dtype=np.float32),
        "rms_w": cols(i["L1_cond_rms_w"]), "wg": rows(i["L1_cond_wg_W"]),
        "gate_b": np.stack([rep(i["L1_cond_wg_b"]), rep(i["L1_cond_gg_b"])], 1), "gg": np.asarray(i["L1_cond_gg_W"]),
        "we": np.concatenate([by_rows(i["L1_cond_W1"]), by_rows(i["L1_cond_W2"]), by_rows(i["L1_cond_W3"])], 2),
        "b1": np.asarray(i["L1_cond_b1"]).reshape(NX, M // P, P).transpose(2, 0, 1),
        "b2": np.asarray(i["L1_cond_b2"]).reshape(NX, M // P, P).transpose(2, 0, 1),
        "b3": np.broadcast_to(np.asarray(i["L1_cond_b3"])[None], (P, NX, E)),
        "tri": np.triu(np.ones((P, P), np.float32), 1),
        "dest": dest,
        "count": np.broadcast_to(np.arange(TILES_MAX + 2, dtype=np.float32), (P, TILES_MAX + 2)),
    }


OUT = [P, T // P, E]


def finish(out):
    return np.asarray(out).transpose(1, 0, 2).reshape(B, S, E)
```
